# Optimizing a Trainium2 kernel written in Bass

```python
import numpy as np
import jax
import jax.numpy as jnp

def _softmax(x, axis=-1):
    return jax.nn.softmax(x, axis=axis)

def _gelu(x):
    return jax.nn.gelu(x, approximate=True)

def _silu(x):
    return jax.nn.silu(x)

def _sigmoid(x):
    return jax.nn.sigmoid(x)

def _layernorm(x, axis=-1, eps=1e-05):
    m = jnp.mean(x, axis=axis, keepdims=True)
    v = jnp.var(x, axis=axis, keepdims=True)
    return (x - m) / jnp.sqrt(v + eps)

def _scatter_add(tgt, idx, src, axis=0):
    return tgt.at[idx].add(src)

def _segment_sum(src, seg, n):
    return jax.ops.segment_sum(src, seg, n)
kernel_name = 'mk_prb_d2_jaxref_r8_999e2d'

def setup_inputs(seed: int=0):
    np.random.seed(seed)
    _w = jnp.asarray

    def _L0_attn_setup():
        import jax, jax.numpy as jnp
        import numpy as np
        B, N, D = (4, 256, 128)
        H = 16
        HD = D // H
        SCALE = 1.0 / HD
        NEG = -10000.0
        THETA = 10000.0

        def _rope(t):
            d, n = (t.shape[-1], t.shape[-2])
            inv_freq = 1.0 / THETA ** (jnp.arange(0, d, 2, dtype=jnp.float32) / d)
            ang = jnp.arange(n, dtype=jnp.float32)[:, None] * inv_freq[None, :]
            cos = jnp.repeat(jnp.cos(ang), 2, axis=-1)
            sin = jnp.repeat(jnp.sin(ang), 2, axis=-1)
            x1, x2 = (t[..., ::2], t[..., 1::2])
            rot = jnp.stack([-x2, x1], axis=-1).reshape(t.shape)
            return t * cos + rot * sin
        key = jax.random.key(seed)
        ks = jax.random.split(key, 6)
        s = (1.0 / D) ** 0.5
        return {'x': jax.random.normal(ks[0], (B, N, D), jnp.float32), 'Wq': jax.random.normal(ks[1], (D, D), jnp.float32) * s, 'Wk': jax.random.normal(ks[2], (D, D), jnp.float32) * s, 'Wv': jax.random.normal(ks[3], (D, D), jnp.float32) * s, 'Wo': jax.random.normal(ks[4], (D, D), jnp.float32) * s, 'bo': jnp.zeros((D,), jnp.float32)}
    _L0_attn_in = _L0_attn_setup()

    def _L0_ffn_setup():
        import jax, jax.numpy as jnp
        import numpy as np
        DIM = 128
        HIDDEN = 384
        SCALE = 1.0 / 127.0

        def _dequant(w_int, dtype):
            return w_int.astype(dtype) * jnp.asarray(SCALE, dtype)
        key = jax.random.key(seed)
        k_x, k_g, k_u, k_d = jax.random.split(key, 4)
        x = jax.random.normal(k_x, (4, 256, DIM), dtype=jnp.float32)
        w_gate = jax.random.randint(k_g, (HIDDEN, DIM), -127, 128, dtype=jnp.int32)
        w_up = jax.random.randint(k_u, (HIDDEN, DIM), -127, 128, dtype=jnp.int32)
        w_down = jax.random.randint(k_d, (DIM, HIDDEN), -127, 128, dtype=jnp.int32)
        return {'x': x, 'w_gate': w_gate, 'w_up': w_up, 'w_down': w_down}
    _L0_ffn_in = _L0_ffn_setup()

    def _L1_attn_setup():
        import jax, jax.numpy as jnp
        import numpy as np
        from math import log2, ceil
        HEADS, DIM_HEAD, BLOCK, EPS = (16, 64, 16, 1e-08)
        key = jax.random.key(seed)
        k1, k2, k3, k4 = jax.random.split(key, 4)
        b, n, dim = (4, 512, 128)
        inner = HEADS * DIM_HEAD
        return {'x': jax.random.normal(k1, (b, n, dim), jnp.float32), 'w_qkv': jax.random.normal(k2, (inner * 3, dim), jnp.float32) * 0.02, 'w_out': jax.random.normal(k3, (dim, inner), jnp.float32) * 0.02, 'b_out': jax.random.normal(k4, (dim,), jnp.float32) * 0.02}
    _L1_attn_in = _L1_attn_setup()

    def _L1_ffn_setup():
        import jax, jax.numpy as jnp
        import numpy as np
        B, S, D = (2, 128, 128)
        L, H = (64, 16)
        HD = L // H
        F, E, K = (256, 8, 2)
        THETA = 10000.0
        EPS = 1e-05

        def _rmsnorm(x, g):
            return x * g * jax.lax.rsqrt(jnp.mean(x * x, axis=-1, keepdims=True) + EPS)

        def _rope(t, pos):
            inv_freq = 1.0 / THETA ** (jnp.arange(0, HD, 2, dtype=jnp.float32) / HD)
            ang = pos[:, None].astype(jnp.float32) * inv_freq[None, :]
            cos, sin = (jnp.cos(ang), jnp.sin(ang))
            t1, t2 = (t[..., 0::2], t[..., 1::2])
            r1 = t1 * cos - t2 * sin
            r2 = t1 * sin + t2 * cos
            return jnp.stack([r1, r2], axis=-1).reshape(t.shape)

        def _forward(x, g1, g2, w_down, wq, wk, wv, w_up, router_w, w1, w2, w3):
            b, s, _ = x.shape
            pos = jnp.arange(s)
            h = _rmsnorm(x, g1)
            c = h @ w_down
            split = lambda t: t.reshape(b, s, H, HD).transpose(0, 2, 1, 3)
            q = _rope(split(c @ wq), pos)
            k = _rope(split(c @ wk), pos)
            v = split(c @ wv)
            scores = jnp.einsum('bhqd,bhkd->bhqk', q, k) / jnp.sqrt(jnp.float32(HD))
            causal = jnp.tril(jnp.ones((s, s), bool))
            scores = jnp.where(causal, scores, -jnp.inf)
            attn = jax.nn.softmax(scores, axis=-1)
            o = jnp.einsum('bhqk,bhkd->bhqd', attn, v).transpose(0, 2, 1, 3).reshape(b, s, L)
            x = x + o @ w_up
            res = x
            t = _rmsnorm(x, g2).reshape(-1, D)
            probs = jax.nn.softmax(t @ router_w, axis=-1)
            vals, idx = jax.lax.top_k(probs, K)
            w = vals / jnp.sum(vals, axis=-1, keepdims=True)
            gate = jnp.sum(jax.nn.one_hot(idx, E, dtype=t.dtype) * w[..., None], axis=1)
            hid = jax.nn.silu(jnp.einsum('td,edf->tef', t, w1)) * jnp.einsum('td,edf->tef', t, w3)
            y_e = jnp.einsum('tef,efd->ted', hid, w2)
            y = jnp.einsum('ted,te->td', y_e, gate)
            return res + y.reshape(b, s, D)
        key = jax.random.key(seed)
        ks = jax.random.split(key, 12)
        g = lambda k, shape, scale: jax.random.normal(k, shape, dtype=jnp.float32) * scale
        return {'x': g(ks[0], (B, S, D), 1.0), 'g1': jnp.ones((D,), jnp.float32), 'g2': jnp.ones((D,), jnp.float32), 'w_down': g(ks[1], (D, L), 0.02), 'wq': g(ks[2], (L, L), 0.02), 'wk': g(ks[3], (L, L), 0.02), 'wv': g(ks[4], (L, L), 0.02), 'w_up': g(ks[5], (L, D), 0.02), 'router_w': g(ks[6], (D, E), 0.02), 'w1': g(ks[7], (E, D, F), 0.02), 'w3': g(ks[8], (E, D, F), 0.02), 'w2': g(ks[9], (E, F, D), 0.02)}
    _L1_ffn_in = _L1_ffn_setup()
    _d = {'L0_attn_x': _L0_attn_in['x'], 'L0_attn_Wq': _L0_attn_in['Wq'], 'L0_attn_Wk': _L0_attn_in['Wk'], 'L0_attn_Wv': _L0_attn_in['Wv'], 'L0_attn_Wo': _L0_attn_in['Wo'], 'L0_attn_bo': _L0_attn_in['bo'], 'L0_ffn_w_gate': _L0_ffn_in['w_gate'], 'L0_ffn_w_up': _L0_ffn_in['w_up'], 'L0_ffn_w_down': _L0_ffn_in['w_down'], 'L1_attn_w_qkv': _L1_attn_in['w_qkv'], 'L1_attn_w_out': _L1_attn_in['w_out'], 'L1_attn_b_out': _L1_attn_in['b_out'], 'L1_ffn_g1': _L1_ffn_in['g1'], 'L1_ffn_g2': _L1_ffn_in['g2'], 'L1_ffn_w_down': _L1_ffn_in['w_down'], 'L1_ffn_wq': _L1_ffn_in['wq'], 'L1_ffn_wk': _L1_ffn_in['wk'], 'L1_ffn_wv': _L1_ffn_in['wv'], 'L1_ffn_w_up': _L1_ffn_in['w_up'], 'L1_ffn_router_w': _L1_ffn_in['router_w'], 'L1_ffn_w1': _L1_ffn_in['w1'], 'L1_ffn_w2': _L1_ffn_in['w2'], 'L1_ffn_w3': _L1_ffn_in['w3']}
    _x0 = _d['L0_attn_x']
    _d['L0_attn_x'] = jax.random.normal(jax.random.fold_in(jax.random.key(seed), 1), (4, 512, 128), dtype=_x0.dtype)
    del _x0
    return _d

def reference(L0_attn_x, L0_attn_Wq, L0_attn_Wk, L0_attn_Wv, L0_attn_Wo, L0_attn_bo, L0_ffn_w_gate, L0_ffn_w_up, L0_ffn_w_down, L1_attn_w_qkv, L1_attn_w_out, L1_attn_b_out, L1_ffn_g1, L1_ffn_g2, L1_ffn_w_down, L1_ffn_wq, L1_ffn_wk, L1_ffn_wv, L1_ffn_w_up, L1_ffn_router_w, L1_ffn_w1, L1_ffn_w2, L1_ffn_w3):

    def _L0_attn_ref(x, Wq, Wk, Wv, Wo, bo):
        import jax, jax.numpy as jnp
        import numpy as np
        B, N, D = (4, 256, 128)
        H = 16
        HD = D // H
        SCALE = 1.0 / HD
        NEG = -10000.0
        THETA = 10000.0

        def _rope(t):
            d, n = (t.shape[-1], t.shape[-2])
            inv_freq = 1.0 / THETA ** (jnp.arange(0, d, 2, dtype=jnp.float32) / d)
            ang = jnp.arange(n, dtype=jnp.float32)[:, None] * inv_freq[None, :]
            cos = jnp.repeat(jnp.cos(ang), 2, axis=-1)
            sin = jnp.repeat(jnp.sin(ang), 2, axis=-1)
            x1, x2 = (t[..., ::2], t[..., 1::2])
            rot = jnp.stack([-x2, x1], axis=-1).reshape(t.shape)
            return t * cos + rot * sin
        b, n, _ = x.shape
        q = (x @ Wq.T).reshape(b, n, H, HD).transpose(0, 2, 1, 3)
        k = (x @ Wk.T).reshape(b, n, H, HD).transpose(0, 2, 1, 3)
        v = (x @ Wv.T).reshape(b, n, H, HD).transpose(0, 2, 1, 3)
        q = _rope(q)
        k = _rope(k)
        i = jnp.arange(n)
        add_mask = jnp.where(i[:, None] >= i[None, :], 0.0, NEG).astype(x.dtype)
        scores = jnp.einsum('bhqd,bhkd->bhqk', q, k) * SCALE + add_mask
        attn = jax.nn.softmax(scores, axis=-1)
        out = jnp.einsum('bhqk,bhkd->bhqd', attn, v)
        out = out.transpose(0, 2, 1, 3).reshape(b, n, H * HD)
        return out @ Wo.T + bo

    def _L0_ffn_ref(x, w_gate, w_up, w_down):
        import jax, jax.numpy as jnp
        import numpy as np
        DIM = 128
        HIDDEN = 384
        SCALE = 1.0 / 127.0

        def _dequant(w_int, dtype):
            return w_int.astype(dtype) * jnp.asarray(SCALE, dtype)
        wg = _dequant(w_gate, x.dtype)
        wu = _dequant(w_up, x.dtype)
        wd = _dequant(w_down, x.dtype)
        gate = jnp.einsum('bsd,hd->bsh', x, wg)
        up = jnp.einsum('bsd,hd->bsh', x, wu)
        h = jax.nn.silu(gate) * up
        return jnp.einsum('bsh,dh->bsd', h, wd)

    def _L1_attn_ref(x, w_qkv, w_out, b_out):
        import jax, jax.numpy as jnp
        import numpy as np
        from math import log2, ceil
        HEADS, DIM_HEAD, BLOCK, EPS = (16, 64, 16, 1e-08)
        b, n, dim = x.shape
        pad_to_len = 2 ** ceil(log2(n))
        if pad_to_len != n:
            x = jnp.pad(x, ((0, 0), (0, pad_to_len - n), (0, 0)))
        qkv = x @ w_qkv.T
        q, k, v = jnp.split(qkv, 3, axis=-1)

        def split_heads(t):
            return t.reshape(b, pad_to_len, HEADS, DIM_HEAD).transpose(0, 2, 1, 3).reshape(b * HEADS, pad_to_len, DIM_HEAD)
        q = split_heads(q) * DIM_HEAD ** (-0.5)
        k = split_heads(k)
        v = split_heads(v)
        num_levels = int(log2(pad_to_len // BLOCK)) - 1
        qkvs = [(q, k, v)]
        for _ in range(num_levels):
            q = q.reshape(q.shape[0], -1, 2, DIM_HEAD).mean(2)
            k = k.reshape(k.shape[0], -1, 2, DIM_HEAD).mean(2)
            v = v.reshape(v.shape[0], -1, 2, DIM_HEAD).sum(2)
            qkvs.append((q, k, v))
        neg_max = -jnp.finfo(x.dtype).max
        idx = jnp.arange(pad_to_len)
        Ysum = jnp.zeros((b * HEADS, pad_to_len, DIM_HEAD), x.dtype)
        Asum = jnp.zeros((b * HEADS, pad_to_len), x.dtype)
        for lvl, (ql, kl, vl) in enumerate(qkvs):
            B = ql.shape[0]
            nb = ql.shape[1] // BLOCK
            ql = ql.reshape(B, nb, BLOCK, DIM_HEAD)
            kl = kl.reshape(B, nb, BLOCK, DIM_HEAD)
            vl = vl.reshape(B, nb, BLOCK, DIM_HEAD)
            if lvl == 0:
                S = jnp.einsum('bnid,bnjd->bnij', ql, kl)
                S = jnp.where(jnp.triu(jnp.ones((BLOCK, BLOCK), bool), 1), neg_max, S)
                S = S - S.max(-1, keepdims=True)
                A = jnp.exp(S)
                y = jnp.einsum('bnij,bnjd->bnid', A, vl).reshape(B, pad_to_len, DIM_HEAD)
                Av = A.sum(-1).reshape(B, pad_to_len)
            else:
                q2 = ql.reshape(B, nb // 2, 2, BLOCK, DIM_HEAD)[:, :, 1]
                k1b = kl.reshape(B, nb // 2, 2, BLOCK, DIM_HEAD)[:, :, 0]
                v1b = vl.reshape(B, nb // 2, 2, BLOCK, DIM_HEAD)[:, :, 0]
                S = jnp.einsum('bnid,bnjd->bnij', q2, k1b)
                S = S - S.max(-1, keepdims=True)
                A = jnp.exp(S)
                y = jnp.einsum('bnij,bnjd->bnid', A, v1b)
                Av = A.sum(-1)
                y = jnp.pad(y[:, :, None], ((0, 0), (0, 0), (1, 0), (0, 0), (0, 0))).reshape(B, -1, DIM_HEAD)
                Av = jnp.pad(Av[:, :, None], ((0, 0), (0, 0), (1, 0), (0, 0))).reshape(B, -1)
                y = jnp.repeat(y, 2 ** lvl, axis=1)
                Av = jnp.repeat(Av, 2 ** lvl, axis=1)
            seq_key = (idx >> lvl << lvl) + (2 ** lvl - 1)
            keep = seq_key <= idx
            Ysum = Ysum + jnp.where(keep[None, :, None], y, 0.0)
            Asum = Asum + jnp.where(keep[None, :], Av, 0.0)
        out = Ysum / (Asum + EPS)[..., None]
        out = out.reshape(b, HEADS, pad_to_len, DIM_HEAD).transpose(0, 2, 1, 3).reshape(b, pad_to_len, HEADS * DIM_HEAD)
        out = out @ w_out.T + b_out
        return out[:, :n]

    def _L1_ffn_ref(x, g1, g2, w_down, wq, wk, wv, w_up, router_w, w1, w2, w3):
        import jax, jax.numpy as jnp
        import numpy as np
        B, S, D = (2, 128, 128)
        L, H = (64, 16)
        HD = L // H
        F, E, K = (256, 8, 2)
        THETA = 10000.0
        EPS = 1e-05

        def _rmsnorm(x, g):
            return x * g * jax.lax.rsqrt(jnp.mean(x * x, axis=-1, keepdims=True) + EPS)

        def _rope(t, pos):
            inv_freq = 1.0 / THETA ** (jnp.arange(0, HD, 2, dtype=jnp.float32) / HD)
            ang = pos[:, None].astype(jnp.float32) * inv_freq[None, :]
            cos, sin = (jnp.cos(ang), jnp.sin(ang))
            t1, t2 = (t[..., 0::2], t[..., 1::2])
            r1 = t1 * cos - t2 * sin
            r2 = t1 * sin + t2 * cos
            return jnp.stack([r1, r2], axis=-1).reshape(t.shape)

        def _forward(x, g1, g2, w_down, wq, wk, wv, w_up, router_w, w1, w2, w3):
            b, s, _ = x.shape
            pos = jnp.arange(s)
            h = _rmsnorm(x, g1)
            c = h @ w_down
            split = lambda t: t.reshape(b, s, H, HD).transpose(0, 2, 1, 3)
            q = _rope(split(c @ wq), pos)
            k = _rope(split(c @ wk), pos)
            v = split(c @ wv)
            scores = jnp.einsum('bhqd,bhkd->bhqk', q, k) / jnp.sqrt(jnp.float32(HD))
            causal = jnp.tril(jnp.ones((s, s), bool))
            scores = jnp.where(causal, scores, -jnp.inf)
            attn = jax.nn.softmax(scores, axis=-1)
            o = jnp.einsum('bhqk,bhkd->bhqd', attn, v).transpose(0, 2, 1, 3).reshape(b, s, L)
            x = x + o @ w_up
            res = x
            t = _rmsnorm(x, g2).reshape(-1, D)
            probs = jax.nn.softmax(t @ router_w, axis=-1)
            vals, idx = jax.lax.top_k(probs, K)
            w = vals / jnp.sum(vals, axis=-1, keepdims=True)
            gate = jnp.sum(jax.nn.one_hot(idx, E, dtype=t.dtype) * w[..., None], axis=1)
            hid = jax.nn.silu(jnp.einsum('td,edf->tef', t, w1)) * jnp.einsum('td,edf->tef', t, w3)
            y_e = jnp.einsum('tef,efd->ted', hid, w2)
            y = jnp.einsum('ted,te->td', y_e, gate)
            return res + y.reshape(b, s, D)
        return _forward(x, g1, g2, w_down, wq, wk, wv, w_up, router_w, w1, w2, w3)
    x = L0_attn_x
    xn = _layernorm(x, axis=-1)
    x = x + _L0_attn_ref(xn, L0_attn_Wq, L0_attn_Wk, L0_attn_Wv, L0_attn_Wo, L0_attn_bo) + _L0_ffn_ref(xn, L0_ffn_w_gate, L0_ffn_w_up, L0_ffn_w_down)
    xn = _layernorm(x, axis=-1)
    x = x + _L1_attn_ref(xn, L1_attn_w_qkv, L1_attn_w_out, L1_attn_b_out) + _L1_ffn_ref(xn, L1_ffn_g1, L1_ffn_g2, L1_ffn_w_down, L1_ffn_wq, L1_ffn_wk, L1_ffn_wv, L1_ffn_w_up, L1_ffn_router_w, L1_ffn_w1, L1_ffn_w2, L1_ffn_w3)
    return x

_drawn_inputs = setup_inputs


def setup_inputs(seed=0):
    import zlib

    import numpy as np

    out = dict(_drawn_inputs(seed))
    spreads = {'L0_attn_bo': (0.0, 2.0), 'L1_ffn_g1': (1.0, 0.6), 'L1_ffn_g2': (1.0, 0.6)}
    factors = {'L0_attn_Wq': 8.0,
     'L0_attn_Wk': 8.0,
     'L0_attn_Wv': 8.0,
     'L0_attn_Wo': 8.0,
     'L1_attn_w_qkv': 22.639,
     'L1_attn_w_out': 23.07,
     'L1_attn_b_out': 64.0,
     'L1_ffn_w_down': 8.0,
     'L1_ffn_wq': 8.0,
     'L1_ffn_wk': 8.0,
     'L1_ffn_wv': 8.0,
     'L1_ffn_w_up': 8.0,
     'L1_ffn_router_w': 8.0,
     'L1_ffn_w1': 22.284,
     'L1_ffn_w2': 8.0,
     'L1_ffn_w3': 8.0}
    for name, (base, spread) in spreads.items():
        noise = np.random.default_rng([zlib.crc32(name.encode()), seed]).standard_normal(out[name].shape)
        drawn = base * np.exp(spread * noise) if base else spread * noise
        out[name] = jnp.asarray(drawn.astype(out[name].dtype))
    for name, factor in factors.items():
        out[name] = (out[name] * factor).astype(out[name].dtype)
    return out
```

```python
from contextlib import ExitStack

import concourse.bass as bass
from concourse import mybir
import numpy as np

F32 = mybir.dt.float32
BF16 = mybir.dt.bfloat16
I32 = mybir.dt.int32
U32 = mybir.dt.uint32
ALU = mybir.AluOpType
ACT = mybir.ActivationFunctionType
AX = mybir.AxisListType

P = 128
BATCH, N, D = 4, 512, 128
T = N // P
H = 16
HD0, HD1, HDH = 8, 4, 64
HIDDEN = 384
FC0 = HIDDEN // P
EXPERTS, F = 8, 256
FC1 = F // P
BLOCK = 16
LEVELS = 4
LN_EPS, RMS_EPS, H_EPS = 1e-5, 1e-5, 1e-8
W_SCALE = 1.0 / 127.0
NEG = -1e30

R, C = 2, H // 2
G, GH = 4, 4
SLOT = 64
MROW = 48
Q_PARTS = (0, 1, 2, 0, 1, 0)
K_PARTS = (0, 0, 0, 1, 1, 2)
XT = T + 2
UNITS = G * XT // 2
SOFT = GH * T
P_RING = 4


def product_plan():
    plan, uses, signals = {}, [0] * 4, [0] * 4

    def use(pair, *key, signalled=True):
        uses[pair] += 1
        signals[pair] += signalled
        plan[key] = (pair, uses[pair], signals[pair])

    def attention(a):
        def maxima(g, i):
            use(0, "smax", a, g, i)
        for g in range(2):
            for i in range(SOFT):
                maxima(g, i)
            use(3, "mT", a, g)
        for g in range(G):
            for i in range(SOFT):
                use(1, "st", a, g, i)
                if i == 0:
                    use(2, "oT", a, g, signalled=False)
                if g + 2 < G:
                    maxima(g + 2, i)
                if g and i == OT_AT:
                    use(3, "o", a, g - 1)
            if g + 2 < G:
                use(3, "mT", a, g + 2)
        use(3, "o", a, G - 1)
        use(3, "aoT", a)

    use(3, "xnT")
    use(0, "rope", 0)
    use(1, "rope", 1)
    use(3, "v0")
    for f in range(FC0):
        use(2 + f % 2, "ffn", f)
    attention(0)
    use(2, "out0")
    use(3, "xn1T")
    use(3, "hT")
    use(0, "c")
    use(1, "rope", 2)
    use(0, "v1")

    def project(g):
        for cc in range(2):
            for side in range(2):
                use(3, "hqk", g, cc, side, 0)
                use(3, "hqk", g, cc, side, 1)
        for tp in range(XT // 2):
            use(3, "hv", g, tp)
    project(0)
    for u in range(UNITS + 2):
        if u < UNITS:
            use(u % 2, "hs", u)
            if u % 3 == 2 and u // 3 + 1 < G:
                project(u // 3 + 1)
        if u >= 2 and (u - 2) % 3 == 0:
            use(2, "hy", (u - 2) // 3, signalled=False)
    use(3, "asum")
    for t in range(T):
        for half in range(2):
            use(3, "spread", t, half)
    use(2, "hout")
    attention(1)
    use(2, "up1")
    use(3, "tT")
    use(3, "logit")
    for e in range(EXPERTS + 1):
        if e < EXPERTS:
            for fc in range(FC1):
                use(fc % 2, "ehid", e, fc)
        if e:
            use(2, "ey", e - 1)
    return plan, uses, signals


OT_AT = 5
PLAN, USES, SIGNALS = product_plan()
RINGS = {"smax", "st", "oT", "o", "mT", "hqk", "hv", "spread", "ey"}


def build(nc, dram, out):
    ctx = ExitStack()
    with ctx:
        def sb(name, shape, dt=F32):
            return ctx.enter_context(nc.sbuf_tensor(name, shape, dt))

        psum = ctx.enter_context(nc.psum_tensor("psum", [P, 8, N], F32))
        primed = []

        def sem(name, per_batch=0, prime=False):
            s = ctx.enter_context(nc.semaphore(name))
            if prime:
                primed.append(s)
            return s, per_batch, int(prime)

        w = {name: sb("w_" + name, shape) for name, shape in RESIDENT.items()}
        w_f = {name: sb("f_" + name, [P, HIDDEN]) for name in ("gate", "up", "down")}
        zeros = sb("zeros", [P, N], BF16)
        scratch = sb("scratch", [P, 24])
        ident_b = sb("ident_b", [P, P], BF16)
        hidden = sb("hidden", [P, 2, P], BF16)

        x_sb = sb("x_sb", [P, T, D])
        xn = sb("xn", [P, T, D])
        xnT = sb("xnT", [P, N])
        x1 = sb("x1", [P, T, D])
        xn1 = sb("xn1", [P, T, D])
        xn1T = sb("xn1T", [P, N])
        hT = sb("hT", [P, N])
        x2 = sb("x2", [P, T, D])
        stats = sb("stats", [P, T, 6])
        mv = sb("mv", [P, T, 2])
        rms = sb("rms", [P, T])
        var_eps = sb("var_eps", [P, T])
        rstd = sb("rstd", [P, T])

        rot = sb("rot", [P, 4, N])
        parts = sb("parts", [P, 2, 3, N], BF16)
        qs = sb("qs", [P, H, N], BF16)
        ks = sb("ks", [P, C, N], BF16)
        maxima = sb("maxima", [P, 2, SOFT])
        m_hi = sb("m_hi", [SOFT, 2, P], BF16)
        m_lo = sb("m_lo", [SOFT, 2, P], BF16)
        probs = sb("probs", [P, P_RING, N])
        v_aug = sb("v_aug", [P, T, H, 32])
        o_sb = sb("o_sb", [P, N])
        o_rc = sb("o_rc", [P, 2, T, GH])
        ao = sb("ao", [P, T, D])
        aoT = sb("aoT", [P, N])
        cT = sb("cT", [64, N])

        coarse = sb("coarse", [P, 3, 2 * P])
        qT = sb("qT", [P, 2, XT * P])
        kT = sb("kT", [P, 2, XT * P])
        v_h = sb("v_h", [P, 2, XT, GH * HDH])
        s32 = sb("s32", [P, 2, 2 * GH, 32])
        a32 = sb("a32", [P, 2, 2 * GH, 32])
        hmx = sb("hmx", [P, 2, 2 * GH])
        a_bd = sb("a_bd", [P, 2, 2 * GH, P])
        a_sum = sb("a_sum", [P, XT, H])
        a_rc = sb("a_rc", [P, 2, T, H])
        wide = sb("wide", [P, 8, N])
        w_int = {name: wide[:, i, 0:HIDDEN].bitcast(I32) for i, name in enumerate(("gate", "up", "down"))}
        sums = probs[:, 0, 0:480]
        rc_wide = rot[:, :, :].rearrange("p (two h) (k d) -> p two (h k) d", two=2, d=HDH)

        logit = sb("logit", [P, T, EXPERTS])
        top = sb("top", [P, T, EXPERTS])
        top_at = sb("top_at", [P, T, EXPERTS], U32)
        top_f = sb("top_f", [P, T, 2])
        route = sb("route", [P, 6, T, EXPERTS])
        route_s = sb("route_s", [P, 4, T])

        filled = [sem(f"filled_{i}", SIGNALS[i], prime=True) for i in range(4)]
        drained = [sem(f"drained_{i}", USES[i], prime=True) for i in range(4)]
        setup_pool = sem("setup_pool")
        setup_dve = sem("setup_dve")
        in_first = sem("in_first")
        in_rest = sem("in_rest")
        x_in = sem("x_in", 16)
        out_done = sem("out_done", 16, prime=True)
        xb_done = sem("xb_done", 1)
        stats_done = sem("stats_done", 4 * T, prime=True)
        rstd_done = sem("rstd_done", 8)
        xn_done = sem("xn_done", T)
        xn1_done = sem("xn1_done", T)
        ss_done = sem("ss_done", 2 * T)
        h_done = sem("h_done", 2 * T)
        rot_a = sem("rot_a", 3)
        rot_done = sem("rot_done", 3)
        hi_done = sem("hi_done", 3)
        rem_done = sem("rem_done", 3)
        mid_done = sem("mid_done", 3)
        lo_done = sem("lo_done", 3)
        stack_in = [sem("stack_in0", 16 * STACK_DMAS[0]), sem("stack_in1", 16 * STACK_DMAS[1], prime=True)]
        m_hi_done = sem("m_hi_done", 2 * G)
        m_in = [sem(f"m_in{g}", 2 * M_DMAS * 16) for g in range(G)]
        pv_done = sem("pv_done", 2 * G * SOFT, prime=True)
        orc_done = sem("orc_done", 2 * G, prime=True)
        silu_done = sem("silu_done", FC0 + EXPERTS * FC1)
        base_done = sem("base_done", 1)
        coarse_done = sem("coarse_done", COARSE_STEPS)
        hmax_done = sem("hmax_done", UNITS)
        hsub_done = sem("hsub_done", UNITS)
        hexp_done = sem("hexp_done", UNITS)
        hsum_done = sem("hsum_done", UNITS)
        habd_done = sem("habd_done", UNITS)
        hpv_done = sem("hpv_done", UNITS, prime=True)
        arc_done = sem("arc_done", 1)
        wide_rc = sem("wide_rc", T)
        acc_done = sem("acc_done", 1)
        route_done = sem("route_done", ROUTE_STEPS)
        route_exp = sem("route_exp", 1)

        def nth(s, b, k):
            assert k + s[2] > 0
            return s[0], b * s[1] + (k + s[2])

        def fill(b, *key):
            pair, _, signal = PLAN[key]
            return nth(filled[pair], b, signal)

        def drain(b, *key):
            pair, use, _ = PLAN[key]
            return nth(drained[pair], b, use)

        def room(b, *key):
            pair, use, _ = PLAN[key]
            held = 2 if key[0] in RINGS and use > 1 and LAST_KIND[key] else 1
            return nth(drained[pair], b, use - held)

        def ends(*key):
            return filled[PLAN[key][0]][0], 1

        def frees(*key):
            return drained[PLAN[key][0]][0], 1

        def bank(*key):
            pair, use, _ = PLAN[key]
            return 2 * pair + (use % 2 if key[0] in RINGS else 0)

        def apart(dve, at):
            dve.memset(scratch[:, at:at + 1], 0.0)

        block = ctx.enter_context(nc.Block())

        @block.sync
        def _(sp):
            x_v = dram["x"].rearrange("b (t p) d -> b p t d", p=P)
            out_v = out.rearrange("b (t p) d -> b p t d", p=P)

            def stack(b, a):
                hd = (HD0, HD1)[a]
                rows = hd * C
                for r in range(R):
                    to = qs[SLOT * r + MROW:SLOT * r + MROW + 2, C * r:C * (r + 1), :]
                    sp.dma_start(to, zeros[0:2 * C, :]).then_inc(stack_in[a][0], 16)
                    if a == 1:
                        used = 6 * HD1
                        for p0 in range(used, MROW, 16):
                            n = min(16, MROW - p0)
                            sp.dma_start(ks[SLOT * r + p0:SLOT * r + p0 + n, :, :], zeros[0:n * C, :])\
                                .then_inc(stack_in[a][0], 16)
                for side, (dst, order) in enumerate(((qs, Q_PARTS), (ks, K_PARTS))):
                    sp.wait_ge(*nth(lo_done, b, side + 1 if a == 0 else 3))
                    for s, part in enumerate(order):
                        for r in range(R):
                            p0 = SLOT * r + hd * s
                            if side == 0:
                                to = qs[p0:p0 + hd, C * r:C * (r + 1), :]
                            else:
                                to = ks[p0:p0 + hd, :, :]
                            src = parts[rows * r:rows * (r + 1), side, part, :] if a == 0 else \
                                parts[64 * side + rows * r:64 * side + rows * (r + 1), 0, part, :]
                            sp.dma_start(to, src).then_inc(stack_in[a][0], 16)

            def maxima_rows(b, a, g):
                sp.wait_ge(*drain(b, "mT", a, g))
                c0 = g * GH // R
                for src, row in ((m_hi, MROW), (m_lo, MROW + 1)):
                    for r in range(R):
                        k = SOFT // R
                        to = qs[SLOT * r + row:SLOT * r + row + 1, C * r + c0:C * r + c0 + GH // R, :]
                        sp.dma_start(to, src[k * r:k * (r + 1), g % 2, :]).then_inc(m_in[g][0], 16)

            with sp.Fori(0, BATCH) as b:
                sp.wait_ge(*nth(stats_done, b, 0))
                sp.dma_start(x_sb[:, :, :], x_v[bass.ds(b, 1), :, :, :].rearrange("a p t d -> (a p) t d"))\
                    .then_inc(x_in[0], 16)
                for a in range(2):
                    if a == 0:
                        sp.wait_ge(setup_dve[0], SETUP_DVE)
                        sp.wait_ge(setup_pool[0], SETUP_POOL)
                    sp.wait_ge(*nth(pv_done, b, a * G * SOFT))
                    stack(b, a)
                    for g in range(G):
                        maxima_rows(b, a, g)
                sp.wait_ge(*drain(b, "ey", EXPERTS - 1))
                sp.dma_start(out_v[bass.ds(b, 1), :, :, :].rearrange("a p t d -> (a p) t d"), x1[:, :, :])\
                    .then_inc(out_done[0], 16)
            sp.wait_ge(*nth(out_done, 0, 16 * BATCH))

        @block.gpsimd
        def _(pool):
            pool.memset(qs[:, :, :].rearrange("p h n -> p (h n)").bitcast(F32), 0.0).then_inc(setup_pool[0], 1)
            pool.memset(v_aug[:, :, :, :], 1.0).then_inc(setup_pool[0], 1)
            pool.memset(a_bd[:, :, :, :], 0.0).then_inc(setup_pool[0], 1)
            pool.memset(coarse[:, :, 2 * P - BLOCK:2 * P], 0.0).then_inc(setup_pool[0], 1)
            pool.memset(hidden[:, :, :], 0.0).then_inc(setup_pool[0], 1)
            pool.wait_ge(setup_pool[0], 5)
            for k, sign in enumerate((-1, 1)):
                pool.affine_select(out=hidden[:, k, :], in_=hidden[:, k, :], compare_op=ALU.is_ge, fill=NEG,
                                   base=0, pattern=[[sign, P]], channel_multiplier=-sign)\
                    .then_inc(setup_pool[0], 1)
            pool.wait_ge(in_first[0], 16 * len(FIRST))
            pool.wait_ge(in_rest[0], 16 * len(REST))

            def inverse_root(b, k, src, eps):
                pool.tensor_tensor(var_eps[:, :], src, w["eps"][:, eps, :], ALU.add).then_inc(rstd_done[0], 1)
                pool.wait_ge(*nth(rstd_done, b, 2 * k + 1))
                pool.tensor_tensor(rstd[:, :], var_eps[:, :], w["neg_half"][:, :], ALU.pow)\
                    .then_inc(rstd_done[0], 1)

            with pool.Fori(0, BATCH) as b:
                pool.wait_ge(*nth(stats_done, b, 2 * T))
                inverse_root(b, 0, mv[:, :, 1], 0)
                pool.wait_ge(*nth(xn_done, b, T))
                pool.tensor_tensor(x_sb[:, :, :], x_sb[:, :, :],
                                   w["bo"][:, :].unsqueeze(1).to_broadcast([P, T, D]), ALU.add)\
                    .then_inc(xb_done[0], 1)
                pool.wait_ge(*nth(stats_done, b, 4 * T))
                inverse_root(b, 1, mv[:, :, 1], 0)
                pool.wait_ge(*nth(ss_done, b, T))
                inverse_root(b, 2, rms[:, :], 1)
                pool.wait_ge(*nth(xn1_done, b, T))
                pool.tensor_tensor(x1[:, :, :], x1[:, :, :],
                                   w["b_out"][:, :].unsqueeze(1).to_broadcast([P, T, D]), ALU.add)\
                    .then_inc(base_done[0], 1)
                pool.wait_ge(*drain(b, "xn1T"))
                pool.wait_ge(*nth(hpv_done, b, 0))
                src, at, width = xn1T[:, :], 0, N // 2
                for level in range(1, LEVELS + 1):
                    pair = src.rearrange("p (n two) -> p n two", two=2)
                    if level > 1:
                        pool.wait_ge(*nth(coarse_done, b, level - 1))
                    pool.tensor_tensor(sums[:, at:at + width], pair[:, :, 0], pair[:, :, 1], ALU.add)\
                        .then_inc(coarse_done[0], 1)
                    src, at, width = sums[:, at:at + width], at + width, width // 2
                pool.wait_ge(*nth(coarse_done, b, LEVELS))
                at, to = 0, 0
                for level in range(1, LEVELS + 1):
                    width = N >> level
                    halves = sums[:, at:at + width].rearrange("p (k two i) -> p k two i", two=2, i=BLOCK)
                    half = width // 2
                    for kind, (odd, power) in enumerate(((1, level), (0, level), (0, 0))):
                        scale = w["halves"][:, power:power + 1].unsqueeze(2)\
                            .to_broadcast([P, half // BLOCK, BLOCK])
                        pool.tensor_tensor(
                            coarse[:, kind, to:to + half].rearrange("p (k i) -> p k i", i=BLOCK),
                            halves[:, :, odd, :], scale, ALU.mult).then_inc(coarse_done[0], 1)
                    at, to = at + width, to + half
                for u in range(UNITS):
                    pool.wait_ge(*nth(hmax_done, b, u + 1))
                    pool.tensor_tensor(s32[:, u % 2, :, :], s32[:, u % 2, :, :],
                                       hmx[:, u % 2, :].unsqueeze(2).to_broadcast([P, 2 * GH, 32]),
                                       ALU.subtract).then_inc(hsub_done[0], 1)
                pool.wait_ge(*nth(ss_done, b, 2 * T))
                inverse_root(b, 3, rms[:, :], 1)
                pool.wait_ge(*drain(b, "up1"))
                pool.wait_ge(*drain(b, "hout"))
                pool.tensor_tensor(x1[:, :, :], x1[:, :, :], x2[:, :, :], ALU.add).then_inc(acc_done[0], 1)

        def take_y(act, b, g):
            act.wait_ge(*nth(hpv_done, b, 3 * (g + 1)))
            for cc in range(2):
                ins = act.activation(wide[:, 2 * g + cc, :], psum[:, bank("hy", g) + cc, :], ACT.Copy)
            ins.then_inc(*frees("hy", g))

        @block.scalar
        def _(act):
            for name in FIRST:
                target = w_int[name] if name in w_int else w[name][:]
                act.dma_start(target, dram[name]).then_inc(in_first[0], 16)
            for name in REST:
                act.dma_start(w[name][:], dram[name]).then_inc(in_rest[0], 16)
            act.wait_ge(in_first[0], 16 * len(FIRST))
            act.wait_ge(setup_pool[0], SETUP_POOL)

            def split(b, k, src, side):
                act.wait_ge(*nth(rot_done, b, k + 1))
                if k < 2:
                    act.wait_ge(*nth(stack_in[1], b, 0))
                else:
                    act.wait_ge(*nth(stack_in[0], b, 16 * STACK_DMAS[0]))
                act.activation(parts[:, side, 0, :], src, ACT.Copy).then_inc(hi_done[0], 1)
                act.wait_ge(*nth(rem_done, b, k + 1))
                act.activation(parts[:, side, 1, :], src, ACT.Copy).then_inc(mid_done[0], 1)

            def attention(b, a):
                for g in range(G):
                    for i in range(SOFT):
                        n = (a * G + g) * SOFT + i
                        width = N - (i % T) * P
                        act.wait_ge(*fill(b, "st", a, g, i))
                        act.wait_ge(*nth(pv_done, b, max(n - P_RING + 1, 0)))
                        act.activation(probs[:, n % P_RING, 0:width], psum[:, bank("st", a, g, i), 0:width],
                                       ACT.Exp, scale=(1.0 / HD0, 1.0 / HD1 ** 0.5)[a])\
                            .then_inc(*frees("st", a, g, i))
                        if i == OT_AT - 3 and g:
                            output(b, a, g - 1)
                output(b, a, G - 1)
                act.wait_ge(*fill(b, "aoT", a))
                act.activation(aoT[:, :], psum[:, bank("aoT", a), :], ACT.Copy).then_inc(*frees("aoT", a))

            def output(b, a, g):
                act.wait_ge(*nth(pv_done, b, (a * G + g + 1) * SOFT))
                if g:
                    act.wait_ge(*fill(b, "o", a, g - 1))
                elif a:
                    act.wait_ge(*fill(b, "o", 0, G - 1))
                else:
                    act.wait_ge(*nth(orc_done, b, 0))
                act.activation(o_sb[:, :], psum[:, bank("oT", a, g), :], ACT.Copy).then_inc(*frees("oT", a, g))

            with act.Fori(0, BATCH) as b:
                act.wait_ge(*fill(b, "xnT"))
                act.activation(xnT[:, :], psum[:, bank("xnT"), :], ACT.Copy).then_inc(*frees("xnT"))
                split(b, 0, rot[:, 0, :], 0)
                act.wait_ge(*fill(b, "v0"))
                act.activation(v_aug[:, :, :, 0:HD0],
                               psum[:, bank("v0"), :].rearrange("p (t h d) -> p t h d", t=T, h=H), ACT.Copy)\
                    .then_inc(*frees("v0"))
                split(b, 1, rot[:, 2, :], 1)
                for f in range(FC0):
                    act.wait_ge(*fill(b, "ffn", f))
                    if f == 0:
                        act.wait_ge(*nth(filled[2], b, 0))
                    act.activation(wide[:, 3 + f, :], psum[:, bank("ffn", f), :], ACT.Silu, scale=W_SCALE)\
                        .then_inc(silu_done[0], 1)
                attention(b, 0)
                act.wait_ge(*fill(b, "xn1T"))
                act.activation(xn1T[:, :], psum[:, bank("xn1T"), :], ACT.Copy).then_inc(*frees("xn1T"))
                act.wait_ge(in_rest[0], 16 * len(REST))
                act.wait_ge(*fill(b, "hT"))
                act.activation(hT[:, :], psum[:, bank("hT"), :], ACT.Copy, scale=w["g1"][:, 0:1])\
                    .then_inc(*frees("hT"))
                act.wait_ge(*fill(b, "c"))
                act.activation(cT[:, :], psum[0:64, bank("c"), :], ACT.Copy).then_inc(*frees("c"))
                split(b, 2, rot[:, 0, :], 0)
                act.wait_ge(*fill(b, "v1"))
                act.activation(v_aug[:, :, :, 0:HD1],
                               psum[:, bank("v1"), 0:T * 64].rearrange("p (t h d) -> p t h d", t=T, h=H),
                               ACT.Copy).then_inc(*frees("v1"))

                def take_projection(g):
                    for cc in range(2):
                        for side, dst in enumerate((qT, kT)):
                            for ext in range(2):
                                act.wait_ge(*fill(b, "hqk", g, cc, side, ext))
                                if g and cc == 0 and side == 0 and ext == 0:
                                    act.wait_ge(*fill(b, "hs", 3 * g - 1))
                                n0, n = (0, N) if ext == 0 else (N, 2 * P)
                                act.activation(dst[:, cc, n0:n0 + n],
                                               psum[:, bank("hqk", g, cc, side, ext), 0:n], ACT.Copy)\
                                    .then_inc(*frees("hqk", g, cc, side, ext))
                    for tp in range(XT // 2):
                        act.wait_ge(*fill(b, "hv", g, tp))
                        if tp == 0 and g >= 2:
                            act.wait_ge(*nth(hpv_done, b, 3 * (g - 1)))
                        act.activation(v_h[:, g % 2, 2 * tp:2 * tp + 2, :],
                                       psum[:, bank("hv", g, tp), :].rearrange("p (t n) -> p t n", t=2),
                                       ACT.Copy).then_inc(*frees("hv", g, tp))

                take_projection(0)
                for u in range(UNITS + 2):
                    if u < UNITS:
                        act.wait_ge(*nth(hsub_done, b, u + 1))
                        if u >= 2:
                            act.wait_ge(*nth(habd_done, b, u - 1))
                        act.activation(a32[:, u % 2, :, :], s32[:, u % 2, :, :], ACT.Exp, scale=HDH ** -0.5)\
                            .then_inc(hexp_done[0], 1)
                        if u % 3 == 2 and u // 3 + 1 < G:
                            take_projection(u // 3 + 1)
                    if u >= 4 and (u - 4) % 3 == 0:
                        take_y(act, b, (u - 4) // 3)
                attention(b, 1)
                act.wait_ge(*fill(b, "tT"))
                act.activation(hT[:, :], psum[:, bank("tT"), :], ACT.Copy, scale=w["g2"][:, 0:1])\
                    .then_inc(*frees("tT"))
                act.wait_ge(*nth(route_done, b, ROUTE_SUB))
                act.activation(route[:, 1, :, :], route[:, 0, :, :], ACT.Exp).then_inc(route_exp[0], 1)
                for e in range(EXPERTS):
                    for fc in range(FC1):
                        act.wait_ge(*fill(b, "ehid", e, fc))
                        if e >= 2 and fc == 0:
                            act.wait_ge(*fill(b, "ey", e - 2))
                        act.activation(wide[:, 4 + 2 * (e % 2) + fc, :], psum[:, bank("ehid", e, fc), :], ACT.Silu)\
                            .then_inc(silu_done[0], 1)

        def spread(dve, b, t):
            if t == 0:
                dve.wait_ge(*drain(b, "hy", G - 1))
            for half in range(2):
                y = wide[:, 4 * half:4 * half + 4, t * P:(t + 1) * P]
                dve.wait_ge(*fill(b, "spread", t, half))
                dve.tensor_tensor(y, psum[:, bank("spread", t, half), :].rearrange("p (c n) -> p c n", c=4),
                                  y, ALU.mult).then_inc(*frees("spread", t, half))

        def router(dve, b):
            steps = [0]

            def link(ins, wait=True):
                steps[0] += 1
                ins.then_inc(route_done[0], 1)
                if wait:
                    dve.wait_ge(*nth(route_done, b, steps[0]))

            def wide_of(s):
                return s.unsqueeze(2).to_broadcast([P, T, EXPERTS])

            dve.wait_ge(*fill(b, "logit"))
            dve.tensor_copy(logit[:, :, :], psum[:, bank("logit"), 0:T * EXPERTS].rearrange(
                "p (t e) -> p t e", t=T)).then_inc(*frees("logit"))
            dve.wait_ge(*drain(b, "logit"))
            apart(dve, 4)
            for t in range(T):
                link(dve.max(top[:, t, :], logit[:, t, :]), wait=t == T - 1)
            link(dve.tensor_tensor(route[:, 0, :, :], logit[:, :, :], wide_of(top[:, :, 0]), ALU.subtract))
            assert steps[0] == ROUTE_SUB
            apart(dve, 5)
            for t in range(T):
                link(dve.max_index(top_at[:, t, :], top[:, t, :], logit[:, t, :]), wait=t == T - 1)
            link(dve.tensor_copy(top_f[:, :, :], top_at[:, :, 0:2]))
            numbers = w["numbers"][:, :].unsqueeze(1).to_broadcast([P, T, EXPERTS])
            for k in range(2):
                link(dve.tensor_tensor(route[:, 2 + k, :, :], numbers, wide_of(top_f[:, :, k]), ALU.is_equal))
            link(dve.tensor_tensor(route[:, 2, :, :], route[:, 2, :, :], route[:, 3, :, :], ALU.add))
            dve.wait_ge(*nth(route_exp, b, 1))
            link(dve.tensor_reduce(route_s[:, 0, :], route[:, 1, :, :], AX.X, ALU.add))
            link(dve.reciprocal(route_s[:, 1, :], route_s[:, 0, :]))
            link(dve.tensor_tensor(route[:, 4, :, :], route[:, 1, :, :], wide_of(route_s[:, 1, :]), ALU.mult))
            link(dve.tensor_tensor(route[:, 4, :, :], route[:, 4, :, :], route[:, 2, :, :], ALU.mult))
            link(dve.tensor_reduce(route_s[:, 2, :], route[:, 4, :, :], AX.X, ALU.add))
            link(dve.reciprocal(route_s[:, 3, :], route_s[:, 2, :]))
            link(dve.tensor_tensor(route[:, 5, :, :], route[:, 4, :, :], wide_of(route_s[:, 3, :]), ALU.mult))
            assert steps[0] == ROUTE_STEPS, steps[0]

        def add_expert(dve, b, e):
            dve.wait_ge(*fill(b, "ey", e))
            if e == 0:
                dve.wait_ge(*nth(acc_done, b, 1))
            else:
                dve.wait_ge(*drain(b, "ey", e - 1))
            for t in range(T):
                ins = dve.scalar_tensor_tensor(out=x1[:, t, :], in0=psum[:, bank("ey", e), t * P:(t + 1) * P],
                                               scalar=route[:, 5, t, e:e + 1], in1=x1[:, t, :],
                                               op0=ALU.mult, op1=ALU.add)
            ins.then_inc(*frees("ey", e))

        @block.vector
        def _(dve):
            dve.memset(zeros[:, :], 0.0).then_inc(setup_dve[0], 1)
            dve.memset(ks[:, :, :], 0.0).then_inc(setup_dve[0], 1)
            for k, s in enumerate(primed):
                dve.memset(scratch[:, 8 + k:9 + k], 0.0).then_inc(s, 1)
            dve.wait_ge(setup_dve[0], 2)
            for r in range(R):
                dve.memset(ks[SLOT * r + 32:SLOT * (r + 1), :, :], 1.0).then_inc(setup_dve[0], 1)
            dve.wait_ge(in_first[0], 16 * len(FIRST))
            dve.tensor_copy(ident_b[:, :], w["ident"][:, :]).then_inc(setup_dve[0], 1)
            for name in ("gate", "up", "down"):
                dve.tensor_copy(w_f[name][:, :], w_int[name]).then_inc(setup_dve[0], 1)
            dve.wait_ge(setup_pool[0], SETUP_POOL)

            def norm_stats(b, k, src):
                for t in range(T):
                    dve.bn_stats(stats[:, t, :], src[:, t, :]).then_inc(stats_done[0], 1)
                dve.wait_ge(*nth(stats_done, b, 2 * T * k + T))
                apart(dve, k)
                for t in range(T):
                    dve.bn_aggr(mv[:, t, :], stats[:, t, :]).then_inc(stats_done[0], 1)

            def square_sums(b, k, src):
                apart(dve, 2 + k)
                for t in range(T):
                    dve.tensor_tensor_reduce(xn[:, t, :], src[:, t, :], src[:, t, :], 1.0 / D, 0.0,
                                             ALU.mult, ALU.add, rms[:, t:t + 1]).then_inc(ss_done[0], 1)

            def rotate(b, k, i, table, side):
                key = ("rope", k)
                dve.wait_ge(*fill(b, *key))
                dve.tensor_tensor(rot[:, i, :], psum[:, bank(*key), :], w[table][:, 0, :], ALU.mult)\
                    .then_inc(rot_a[0], 1)
                dve.tensor_tensor(rot[:, i + 1, :], psum[:, bank(*key) + 1, :], w[table][:, 1, :], ALU.mult)\
                    .then_inc(*frees(*key))
                dve.wait_ge(*drain(b, *key))
                dve.tensor_tensor(rot[:, i, :], rot[:, i, :], rot[:, i + 1, :], ALU.add).then_inc(rot_done[0], 1)

            def split(b, k, i, side):
                dve.wait_ge(*nth(hi_done, b, k + 1))
                dve.tensor_tensor(rot[:, i, :], rot[:, i, :], parts[:, side, 0, :], ALU.subtract)\
                    .then_inc(rem_done[0], 1)
                dve.wait_ge(*nth(mid_done, b, k + 1))
                dve.tensor_tensor(parts[:, side, 2, :], rot[:, i, :], parts[:, side, 1, :], ALU.subtract)\
                    .then_inc(lo_done[0], 1)

            def row_maxima(b, a, g, i):
                t = i % T
                width = (t + 1) * P
                s = psum[:, bank("smax", a, g, i), 0:width]
                dve.wait_ge(*fill(b, "smax", a, g, i))
                if i == 0:
                    before = a * G + g - 2
                    if before >= 0:
                        dve.wait_ge(*fill(b, "mT", before // G, before % G))
                dve.tensor_reduce(maxima[:, g % 2, i:i + 1], s, AX.X, ALU.max)\
                    .then_inc(*frees("smax", a, g, i))

            def negate_maxima(b, a, g):
                src = psum[0:SOFT, bank("mT", a, g), 0:P]
                dve.wait_ge(*fill(b, "mT", a, g))
                before = a * G + g - 2
                if before >= 0:
                    dve.wait_ge(*nth(m_in[before % G], b, M_DMAS * 16 * (before // G + 1)))
                dve.tensor_scalar(m_hi[:, g % 2, :], src, -1.0, None, ALU.mult).then_inc(m_hi_done[0], 1)
                dve.wait_ge(*nth(m_hi_done, b, a * G + g + 1))
                dve.scalar_tensor_tensor(out=m_lo[:, g % 2, :], in0=src, scalar=-1.0, in1=m_hi[:, g % 2, :],
                                         op0=ALU.mult, op1=ALU.subtract).then_inc(*frees("mT", a, g))

            def normalise(b, a, g):
                hd = (HD0, HD1)[a]
                o = psum[:, bank("o", a, g), :].rearrange("p (t j d) -> p t j d", t=T, j=GH)
                dve.wait_ge(*fill(b, "o", a, g))
                dve.reciprocal(o_rc[:, g % 2, :, :], o[:, :, :, HD0]).then_inc(orc_done[0], 1)
                dve.wait_ge(*nth(orc_done, b, a * G + g + 1))
                dve.tensor_tensor(
                    ao[:, :, 0:H * hd].rearrange("p t (h d) -> p t h d", d=hd)[:, :, g * GH:(g + 1) * GH, :],
                    o[:, :, :, 0:hd], o_rc[:, g % 2, :, :].unsqueeze(3).to_broadcast([P, T, GH, hd]), ALU.mult)\
                    .then_inc(*frees("o", a, g))

            def attention(b, a):
                for g in range(2):
                    for i in range(SOFT):
                        row_maxima(b, a, g, i)
                    negate_maxima(b, a, g)
                for g in range(G):
                    for i in range(SOFT):
                        if g + 2 < G:
                            row_maxima(b, a, g + 2, i)
                        if g and i == OT_AT:
                            normalise(b, a, g - 1)
                    if g + 2 < G:
                        negate_maxima(b, a, g + 2)
                normalise(b, a, G - 1)

            with dve.Fori(0, BATCH) as b:
                dve.wait_ge(*nth(x_in, b, 16))
                norm_stats(b, 0, x_sb)
                dve.wait_ge(*nth(rstd_done, b, 2))
                dve.wait_ge(*nth(filled[3], b, 0))
                for t in range(T):
                    dve.tensor_scalar(xn[:, t, :], x_sb[:, t, :], mv[:, t, 0:1], rstd[:, t:t + 1],
                                      ALU.subtract, ALU.mult).then_inc(xn_done[0], 1)
                rotate(b, 0, 0, "rope0", 0)
                rotate(b, 1, 2, "rope0", 1)
                split(b, 0, 0, 0)
                split(b, 1, 2, 1)
                for f in range(FC0):
                    dve.wait_ge(*nth(silu_done, b, f + 1))
                    dve.scalar_tensor_tensor(out=wide[:, f, :], in0=psum[:, bank("ffn", f) + 1, :],
                                             scalar=W_SCALE * W_SCALE, in1=wide[:, 3 + f, :],
                                             op0=ALU.mult, op1=ALU.mult).then_inc(*frees("ffn", f))
                attention(b, 0)
                dve.wait_ge(*nth(xb_done, b, 1))
                dve.wait_ge(*nth(out_done, b, 0))
                dve.wait_ge(*fill(b, "out0"))
                dve.tensor_tensor(x1[:, :, :], psum[:, bank("out0"), :].rearrange("p (t d) -> p t d", t=T),
                                  x_sb[:, :, :], ALU.add).then_inc(*frees("out0"))
                dve.wait_ge(*drain(b, "out0"))
                norm_stats(b, 1, x1)
                dve.wait_ge(*nth(rstd_done, b, 4))
                for t in range(T):
                    dve.tensor_scalar(xn1[:, t, :], x1[:, t, :], mv[:, t, 0:1], rstd[:, t:t + 1],
                                      ALU.subtract, ALU.mult).then_inc(xn1_done[0], 1)
                dve.wait_ge(*nth(xn1_done, b, T))
                dve.wait_ge(*fill(b, "xnT"))
                square_sums(b, 0, xn1)
                dve.wait_ge(*nth(rstd_done, b, 6))
                for t in range(T):
                    dve.tensor_scalar(xn[:, t, :], xn1[:, t, :], rstd[:, t:t + 1], None, ALU.mult)\
                        .then_inc(h_done[0], 1)
                rotate(b, 2, 0, "rope1", 0)
                split(b, 2, 0, 0)

                def extract(u):
                    kind = 0 if u % 3 < 2 else 1
                    pair = psum[:, bank("hs", u):bank("hs", u) + 2, :].rearrange("p k (h n) -> p (k h) n", n=P)
                    dve.wait_ge(*fill(b, "hs", u))
                    if u >= 2:
                        dve.wait_ge(*nth(hexp_done, b, u - 1))
                    for q in range(4):
                        rows = slice(32 * q, 32 * q + 32)
                        ins = dve.tensor_tensor(
                            s32[rows, u % 2, :, :], pair[rows, :, rows],
                            w["band"][rows, kind, :].unsqueeze(1).to_broadcast([32, 2 * GH, 32]), ALU.add)
                    ins.then_inc(*frees("hs", u))
                    dve.wait_ge(*drain(b, "hs", u))
                    dve.tensor_reduce(hmx[:, u % 2, :], s32[:, u % 2, :, :], AX.X, ALU.max)\
                        .then_inc(hmax_done[0], 1)

                def turn(u):
                    g, tp = u // 3, u % 3
                    dve.wait_ge(*nth(hexp_done, b, u + 1))
                    dve.tensor_reduce(
                        a_sum[:, 2 * tp:2 * tp + 2, GH * g:GH * (g + 1)].rearrange("p t (c r) -> p r t c", r=R),
                        a32[:, u % 2, :, :].rearrange("p (r t c) n -> p r t c n", r=R, t=2), AX.X, ALU.add)\
                        .then_inc(hsum_done[0], 1)
                    if u >= 2:
                        dve.wait_ge(*nth(hpv_done, b, u - 1))
                    for q in range(4):
                        rows = slice(32 * q, 32 * q + 32)
                        ins = dve.transpose(a_bd[rows, u % 2, :, rows], a32[rows, u % 2, :, :])
                    ins.then_inc(habd_done[0], 1)

                for u in range(UNITS + 1):
                    if u < UNITS:
                        extract(u)
                    if u:
                        turn(u - 1)
                dve.wait_ge(*fill(b, "asum"))
                dve.tensor_scalar(a_rc[:, 0, :, :], psum[:, bank("asum"), 0:T * H].rearrange(
                    "p (t h) -> p t h", t=T), H_EPS, None, ALU.add).then_inc(*frees("asum"))
                dve.wait_ge(*drain(b, "asum"))
                dve.reciprocal(a_rc[:, 1, :, :], a_rc[:, 0, :, :]).then_inc(arc_done[0], 1)
                dve.wait_ge(*nth(arc_done, b, 1))
                for t in range(T):
                    if t >= 2:
                        dve.wait_ge(*fill(b, "spread", t - 2, 1))
                    dve.tensor_copy(rc_wide[:, t % 2, :, :],
                                    a_rc[:, 1, t, :].unsqueeze(2).to_broadcast([P, H, HDH]))\
                        .then_inc(wide_rc[0], 1)
                    if t:
                        spread(dve, b, t - 1)
                spread(dve, b, T - 1)
                dve.wait_ge(*nth(base_done, b, 1))
                dve.wait_ge(*fill(b, "hout"))
                dve.tensor_tensor(x1[:, :, :], psum[:, bank("hout"), :].rearrange("p (t d) -> p t d", t=T),
                                  x1[:, :, :], ALU.add).then_inc(*frees("hout"))
                attention(b, 1)
                dve.wait_ge(*fill(b, "up1"))
                dve.tensor_tensor(x2[:, :, :], psum[:, bank("up1"), :].rearrange("p (t d) -> p t d", t=T),
                                  xn1[:, :, :], ALU.add).then_inc(*frees("up1"))
                dve.wait_ge(*drain(b, "up1"))
                dve.wait_ge(*fill(b, "hT"))
                square_sums(b, 1, x2)
                dve.wait_ge(*nth(rstd_done, b, 8))
                for t in range(T):
                    dve.tensor_scalar(xn[:, t, :], x2[:, t, :], rstd[:, t:t + 1], None, ALU.mult)\
                        .then_inc(h_done[0], 1)
                router(dve, b)
                for e in range(EXPERTS):
                    for fc in range(FC1):
                        n = FC0 + e * FC1 + fc
                        dve.wait_ge(*nth(silu_done, b, n + 1))
                        dve.tensor_tensor(wide[:, 2 * (e % 2) + fc, :], psum[:, bank("ehid", e, fc) + 1, :],
                                          wide[:, 4 + 2 * (e % 2) + fc, :], ALU.mult)\
                            .then_inc(*frees("ehid", e, fc))
                    if e:
                        add_expert(dve, b, e - 1)
                add_expert(dve, b, EXPERTS - 1)

        @block.tensor
        def _(pe):
            ident = w["ident"][:, :]
            used = []

            def product(b, *key):
                used.append(key)
                pe.wait_ge(*room(b, *key))
                return bank(*key)

            def turn4(b, key, src, ready, n0, parts_of=P):
                k = product(b, *key)
                for t in range(T):
                    if ready is not None:
                        pe.wait_ge(*nth(ready, b, n0 + t + 1))
                    ins = pe.transpose(psum[0:parts_of, k, t * P:(t + 1) * P], src[:, t, 0:parts_of], ident)
                ins.then_inc(*ends(*key))

            def scores_q(b, a, g, i):
                r, cc, t = i // (SOFT // R), i // T % (GH // R), i % T
                c = g * GH // R + cc
                k = product(b, "smax", a, g, i)
                pe.matmul(psum[:, k, 0:(t + 1) * P], qs[:, C * r + c, t * P:(t + 1) * P],
                          ks[:, c, 0:(t + 1) * P], start=True, stop=True)
                pe.matmul(psum[:, k, t * P:(t + 1) * P], ident_b[:, :], hidden[:, 0, :], start=False, stop=True,
                          skip_group_check=True).then_inc(*ends("smax", a, g, i))

            def turn_maxima(b, a, g):
                k = product(b, "mT", a, g)
                pe.wait_ge(*drain(b, "smax", a, g, SOFT - 1))
                pe.transpose(psum[0:SOFT, k, 0:P], maxima[:, g % 2, :], ident).then_inc(*ends("mT", a, g))

            def scores_k(b, a, g, i):
                j, kb = i // T, i % T
                h = g * GH + j
                k = product(b, "st", a, g, i)
                if i == 0:
                    pe.wait_ge(*nth(m_in[g], b, 16 * M_DMAS * (a + 1)))
                pe.matmul(psum[:, k, 0:N - kb * P], ks[:, h // R, kb * P:(kb + 1) * P],
                          qs[:, C * (h % R) + h // R, kb * P:N], start=True, stop=True)
                pe.matmul(psum[:, k, 0:P], ident_b[:, :], hidden[:, 1, :], start=False, stop=True,
                          skip_group_check=True).then_inc(*ends("st", a, g, i))

            def weigh(b, a, g, i):
                j, kb = i // T, i % T
                n = (a * G + g) * SOFT + i
                k = bank("oT", a, g)
                pe.wait_ge(*drain(b, "st", a, g, i))
                pe.matmul(psum[32 * j:32 * j + 32, k, kb * P:N], v_aug[:, kb, g * GH + j, :],
                          probs[:, n % P_RING, 0:N - kb * P], start=(kb == 0), stop=(kb == T - 1),
                          skip_group_check=True).then_inc(pv_done[0], 1)

            def turn_output(b, a, g):
                k = product(b, "o", a, g)
                pe.wait_ge(*drain(b, "oT", a, g))
                for t in range(T):
                    ins = pe.transpose(psum[:, k, t * P:(t + 1) * P], o_sb[:, t * P:(t + 1) * P], ident)
                ins.then_inc(*ends("o", a, g))

            def attention(b, a):
                pe.wait_ge(*nth(stack_in[a], b, 16 * STACK_DMAS[a]))
                for g in range(2):
                    for i in range(SOFT):
                        scores_q(b, a, g, i)
                    turn_maxima(b, a, g)
                for g in range(G):
                    for i in range(SOFT):
                        scores_k(b, a, g, i)
                        if i == 0:
                            product(b, "oT", a, g)
                        if i >= 2:
                            weigh(b, a, g, i - 2)
                        if g + 2 < G:
                            scores_q(b, a, g + 2, i)
                        if g and i == OT_AT:
                            turn_output(b, a, g - 1)
                    weigh(b, a, g, SOFT - 2)
                    weigh(b, a, g, SOFT - 1)
                    if g + 2 < G:
                        turn_maxima(b, a, g + 2)
                turn_output(b, a, G - 1)
                k = product(b, "aoT", a)
                pe.wait_ge(*drain(b, "o", a, G - 1))
                for t in range(T):
                    ins = pe.transpose(psum[:, k, t * P:(t + 1) * P], ao[:, t, :], ident)
                ins.then_inc(*ends("aoT", a))

            pe.wait_ge(in_first[0], 16 * len(FIRST))
            pe.wait_ge(setup_pool[0], SETUP_POOL)
            pe.wait_ge(setup_dve[0], SETUP_DVE)
            with pe.Fori(0, BATCH) as b:
                turn4(b, ("xnT",), xn, xn_done, 0)
                pe.wait_ge(*drain(b, "xnT"))
                for k in range(2):
                    bk = product(b, "rope", k)
                    for swap in range(2):
                        ins = pe.matmul(psum[:, bk + swap, :], w["qk0"][:, 2 * k + swap, :], xnT[:, :],
                                        start=True, stop=True)
                    ins.then_inc(*ends("rope", k))
                bk = product(b, "v0")
                for t in range(T):
                    ins = pe.matmul(psum[:, bk, t * P:(t + 1) * P], xnT[:, t * P:(t + 1) * P], w["v0"][:, :],
                                    start=True, stop=True)
                ins.then_inc(*ends("v0"))
                for f in range(FC0):
                    bk = product(b, "ffn", f)
                    for k, name in enumerate(("gate", "up")):
                        ins = pe.matmul(psum[:, bk + k, :], w_f[name][:, f * P:(f + 1) * P], xnT[:, :],
                                        start=True, stop=True)
                    ins.then_inc(*ends("ffn", f))
                attention(b, 0)
                bk = product(b, "out0")
                pe.wait_ge(*drain(b, "aoT", 0))
                pe.wait_ge(*drain(b, "ffn", FC0 - 1))
                for t in range(T):
                    pe.matmul(psum[:, bk, t * P:(t + 1) * P], aoT[:, t * P:(t + 1) * P], w["o0"][:, :],
                              start=(t == 0), stop=False, skip_group_check=True)
                    for f in range(FC0):
                        ins = pe.matmul(psum[:, bk, t * P:(t + 1) * P], wide[:, f, t * P:(t + 1) * P],
                                        w_f["down"][:, f * P:(f + 1) * P], start=False, stop=(f == FC0 - 1),
                                        skip_group_check=True)
                ins.then_inc(*ends("out0"))
                pe.wait_ge(in_rest[0], 16 * len(REST))
                turn4(b, ("xn1T",), xn1, xn1_done, 0)
                turn4(b, ("hT",), xn, h_done, 0)
                bk = product(b, "c")
                pe.wait_ge(*drain(b, "hT"))
                pe.matmul(psum[0:64, bk, :], w["down1"][:, :], hT[:, :], start=True, stop=True)\
                    .then_inc(*ends("c"))
                bk = product(b, "rope", 2)
                pe.wait_ge(*drain(b, "c"))
                for swap in range(2):
                    ins = pe.matmul(psum[:, bk + swap, :], w["qk1"][:, swap, :], cT[:, :], start=True, stop=True)
                ins.then_inc(*ends("rope", 2))
                bk = product(b, "v1")
                for t in range(T):
                    ins = pe.matmul(psum[:, bk, t * 64:(t + 1) * 64], cT[:, t * P:(t + 1) * P], w["v1"][:, :],
                                    start=True, stop=True)
                ins.then_inc(*ends("v1"))

                def project(g):
                    for cc in range(2):
                        for side in range(2):
                            lhs = w["qkv"][:, side * H * HDH + (2 * g + cc) * P:][:, 0:P]
                            for ext in range(2):
                                k = product(b, "hqk", g, cc, side, ext)
                                if g == 0 and ext == 1:
                                    pe.wait_ge(*nth(coarse_done, b, COARSE_STEPS))
                                rhs, n = (xn1T[:, :], N) if ext == 0 else (coarse[:, side, :], 2 * P)
                                pe.matmul(psum[:, k, 0:n], lhs, rhs, start=True, stop=True)\
                                    .then_inc(*ends("hqk", g, cc, side, ext))
                    for tp in range(XT // 2):
                        k = product(b, "hv", g, tp)
                        for i in range(2):
                            t = 2 * tp + i
                            lhs = xn1T[:, t * P:(t + 1) * P] if t < T else \
                                coarse[:, 2, (t - T) * P:(t - T + 1) * P]
                            ins = pe.matmul(psum[:, k, i * GH * HDH:(i + 1) * GH * HDH], lhs,
                                            w["qkv"][:, 2 * H * HDH + g * GH * HDH:][:, 0:GH * HDH],
                                            start=True, stop=True)
                        ins.then_inc(*ends("hv", g, tp))

                def hscores(u):
                    g, tp = u // 3, u % 3
                    k = product(b, "hs", u)
                    if tp == 0:
                        pe.wait_ge(*drain(b, "hqk", g, 1, 1, 1))
                    for i in range(2):
                        t = 2 * tp + i
                        for j in range(GH):
                            rows = slice(64 * (j % 2), 64 * (j % 2) + 64)
                            m = 2 * i + j // 2
                            ins = pe.matmul(psum[:, k + j % 2, m * P:(m + 1) * P],
                                            qT[rows, j // 2, t * P:(t + 1) * P],
                                            kT[rows, j // 2, t * P:(t + 1) * P], start=True, stop=True)
                    ins.then_inc(*ends("hs", u))

                def hweigh(u):
                    g, tp = u // 3, u % 3
                    k = bank("hy", g)
                    if tp == 0:
                        product(b, "hy", g)
                        pe.wait_ge(*drain(b, "hv", g, XT // 2 - 1))
                    pe.wait_ge(*nth(habd_done, b, u + 1))
                    for i in range(2):
                        t = 2 * tp + i
                        for j in range(GH):
                            rows = slice(64 * (j % 2), 64 * (j % 2) + 64)
                            y = psum[rows, k + j // 2, :]
                            v = v_h[:, g % 2, t, j * HDH:(j + 1) * HDH]
                            at = 0
                            for level in (range(0, 1) if t < T else range(1, 2) if t == T
                                          else range(2, LEVELS + 1)):
                                if level == 0:
                                    to, n = y[:, t * P:(t + 1) * P], P
                                    rhs = a_bd[:, u % 2, (j % 2) * GH + 2 * i + j // 2, :]
                                else:
                                    span = 2 * BLOCK << level
                                    n = N // span * BLOCK
                                    to = y.rearrange("p (k s) -> p k s", s=span)[
                                        :, :, span // 2 + (1 << level) - 1:span:1 << level]
                                    rhs = a_bd[:, u % 2, (j % 2) * GH + 2 * i + j // 2, at:at + n]\
                                        .rearrange("p (k i) -> p k i", i=BLOCK)
                                    at += n
                                ins = pe.matmul(to, v, rhs, start=(t == 0), stop=(level == LEVELS),
                                                skip_group_check=True)
                    ins.then_inc(hpv_done[0], 1)

                project(0)
                for u in range(UNITS + 2):
                    if u < UNITS:
                        hscores(u)
                        if u % 3 == 2 and u // 3 + 1 < G:
                            project(u // 3 + 1)
                    if u >= 2:
                        hweigh(u - 2)
                k = product(b, "asum")
                pe.wait_ge(*nth(hsum_done, b, UNITS))
                for t in range(T):
                    to = psum[:, k, t * H:(t + 1) * H]
                    pe.matmul(to, ident, a_sum[:, t, :], start=(t == 0), stop=False, skip_group_check=True)
                    for i in range(2):
                        ins = pe.matmul(to, w["scatter"][:, i, t * P:(t + 1) * P], a_sum[:, T + i, :],
                                        start=False, stop=(i == 1), skip_group_check=True)
                ins.then_inc(*ends("asum"))
                for t in range(T):
                    for half in range(2):
                        k = product(b, "spread", t, half)
                        pe.wait_ge(*nth(wide_rc, b, t + 1))
                        for c in range(4):
                            h = 2 * (4 * half + c)
                            ins = pe.transpose(
                                psum[:, k, c * P:(c + 1) * P],
                                rc_wide[:, t % 2, h:h + 2, :].rearrange("p h d -> p (h d)"), ident)
                        ins.then_inc(*ends("spread", t, half))
                k = product(b, "hout")
                for t in range(T):
                    pe.wait_ge(*drain(b, "spread", t, 1))
                    for c in range(8):
                        ins = pe.matmul(psum[:, k, t * P:(t + 1) * P], wide[:, c, t * P:(t + 1) * P],
                                        w["out"][:, c, :], start=(t == 0 and c == 0), stop=(c == 7),
                                        skip_group_check=True)
                ins.then_inc(*ends("hout"))

                attention(b, 1)
                k = product(b, "up1")
                pe.wait_ge(*drain(b, "aoT", 1))
                for t in range(T):
                    ins = pe.matmul(psum[:, k, t * P:(t + 1) * P], aoT[0:64, t * P:(t + 1) * P], w["up1"][:, :],
                                    start=True, stop=True)
                ins.then_inc(*ends("up1"))
                turn4(b, ("tT",), xn, h_done, T)
                k = product(b, "logit")
                pe.wait_ge(*drain(b, "tT"))
                for t in range(T):
                    ins = pe.matmul(psum[:, k, t * EXPERTS:(t + 1) * EXPERTS], hT[:, t * P:(t + 1) * P],
                                    w["router"][:, :], start=True, stop=True)
                ins.then_inc(*ends("logit"))
                for e in range(EXPERTS + 1):
                    if e < EXPERTS:
                        for fc in range(FC1):
                            k = product(b, "ehid", e, fc)
                            for i, name in enumerate(("w1", "w3")):
                                ins = pe.matmul(psum[:, k + i, :], w[name][:, e, fc * P:(fc + 1) * P], hT[:, :],
                                                start=True, stop=True)
                            ins.then_inc(*ends("ehid", e, fc))
                    if e:
                        k = product(b, "ey", e - 1)
                        pe.wait_ge(*drain(b, "ehid", e - 1, FC1 - 1))
                        for t in range(T):
                            for fc in range(FC1):
                                ins = pe.matmul(psum[:, k, t * P:(t + 1) * P],
                                                wide[:, 2 * ((e - 1) % 2) + fc, t * P:(t + 1) * P],
                                                w["w2"][:, (e - 1) * FC1 + fc, :],
                                                start=(t == 0 and fc == 0), stop=(fc == FC1 - 1),
                                                skip_group_check=True)
                        ins.then_inc(*ends("ey", e - 1))
            assert used == [k for k in PLAN], [(u, k) for u, k in zip(used, PLAN) if u != k][:3]


def ring_before():
    reader = {"smax": "dve", "mT": "dve", "o": "dve", "spread": "dve", "ey": "dve", "st": "act", "oT": "act",
              "hqk": "act", "hv": "act"}
    last, found = {}, {}
    for key, (pair, _, _) in PLAN.items():
        before = last.get(pair)
        found[key] = before is not None and reader.get(key[0], 0) == reader.get(before[0], 1)
        last[pair] = key
    return found


LAST_KIND = ring_before()
M_DMAS = 2 * R
STACK_DMAS = (2 * 6 * R + R, 2 * 6 * R + R + 2 * R)
COARSE_STEPS = LEVELS * 4
ROUTE_SUB = T + 1
ROUTE_STEPS = 2 * T + 12
SETUP_DVE = 2 + R + 4
SETUP_POOL = 7

RESIDENT = {
    "qk0": [P, 4, P], "v0": [P, P], "o0": [P, P], "rope0": [P, 2, N], "ident": [P, P],
    "bo": [P, P], "neg_half": [P, T], "eps": [P, 2, T], "halves": [P, LEVELS + 1],
    "qkv": [P, 3 * H * HDH], "out": [P, 8, P], "b_out": [P, P], "g1": [P, 1], "g2": [P, 1],
    "down1": [P, 64], "qk1": [64, 2, P], "v1": [64, 64], "up1": [64, P], "router": [P, EXPERTS],
    "w1": [P, EXPERTS, F], "w3": [P, EXPERTS, F], "w2": [P, EXPERTS * FC1, P],
    "rope1": [P, 2, N], "band": [P, 2, 32], "scatter": [P, 2, N], "numbers": [P, EXPERTS],
}
FIRST = ["qk0", "ident", "v0", "gate", "up", "rope0", "o0", "down", "bo", "neg_half", "eps"]
REST = [k for k in RESIDENT if k not in FIRST]


def head_order(hd):
    r, d, c = np.meshgrid(np.arange(R), np.arange(hd), np.arange(C), indexing="ij")
    return ((R * c + r) * hd + d).reshape(-1)


def rope_table(hd):
    inv = (1.0 / 10000.0 ** (np.arange(0, hd, 2, dtype=np.float32) / np.float32(hd))).astype(np.float32)
    ang = (np.arange(N, dtype=np.float32)[:, None] * inv[None, :]).astype(np.float32)
    d = head_order(hd) % hd
    sign = np.where(d % 2 == 0, -1.0, 1.0)[:, None]
    return np.stack([np.cos(ang).T[d // 2], np.sin(ang).T[d // 2] * sign], 1).astype(np.float32)


def constants():
    p = np.arange(P)
    c = {"ident": np.eye(P, dtype=np.float32), "rope0": rope_table(HD0)}
    c["rope1"] = np.concatenate([rope_table(HD1)] * 2, 0)
    c["neg_half"] = np.full((P, T), -0.5, np.float32)
    c["eps"] = np.stack([np.full((P, T), e, np.float32) for e in (LN_EPS, RMS_EPS)], 1)
    c["halves"] = np.tile((0.5 ** np.arange(LEVELS + 1)).astype(np.float32), (P, 1))
    row, col = (p % 32)[:, None], np.arange(32)[None, :]
    same = row // BLOCK == col // BLOCK
    c["band"] = np.stack([np.where(same & (col <= row), 0.0, NEG), np.where(same, 0.0, NEG)], 1).astype(np.float32)
    scatter = np.zeros((P, 2, N), np.float32)
    at = [0, 0]
    for level in range(1, LEVELS + 1):
        i = 0 if level == 1 else 1
        span = 2 * BLOCK << level
        for k in range(N // span):
            for j in range(BLOCK):
                scatter[at[i], i, k * span + span // 2 + ((j + 1) << level) - 1] = 1.0
                at[i] += 1
    c["scatter"] = scatter
    c["numbers"] = np.tile(np.arange(EXPERTS, dtype=np.float32), (P, 1))
    return c


def swapped(order):
    return order ^ 1


def kernel(**inputs):
    import concourse.bacc as bacc
    from concourse.bass_utils import run_bass_kernel_spmd

    a = {k: np.asarray(v) for k, v in inputs.items()}
    o0, o1 = head_order(HD0), head_order(HD1)

    def chunks(m):
        return m.reshape(-1, P, m.shape[1]).transpose(1, 0, 2)

    arrays = {
        "x": a["L0_attn_x"],
        "qk0": np.stack([a["L0_attn_Wq"][o0].T, a["L0_attn_Wq"][swapped(o0)].T,
                         a["L0_attn_Wk"][o0].T, a["L0_attn_Wk"][swapped(o0)].T], 1),
        "v0": a["L0_attn_Wv"].T, "o0": a["L0_attn_Wo"].T,
        "bo": np.broadcast_to(a["L0_attn_bo"], (P, D)),
        "gate": a["L0_ffn_w_gate"].T, "up": a["L0_ffn_w_up"].T,
        "down": chunks(a["L0_ffn_w_down"].T).reshape(P, -1),
        "qkv": a["L1_attn_w_qkv"].T, "out": chunks(a["L1_attn_w_out"].T),
        "b_out": np.broadcast_to(a["L1_attn_b_out"], (P, D)),
        "g1": a["L1_ffn_g1"][:, None], "g2": a["L1_ffn_g2"][:, None],
        "down1": a["L1_ffn_w_down"],
        "qk1": np.stack([np.concatenate([a["L1_ffn_wq"][:, o], a["L1_ffn_wk"][:, o]], 1)
                         for o in (o1, swapped(o1))], 1),
        "v1": a["L1_ffn_wv"], "up1": a["L1_ffn_w_up"], "router": a["L1_ffn_router_w"],
        "w1": a["L1_ffn_w1"].transpose(1, 0, 2), "w3": a["L1_ffn_w3"].transpose(1, 0, 2),
        "w2": chunks(a["L1_ffn_w2"].reshape(EXPERTS * F, D)),
        **constants(),
    }
    nc = bacc.Bacc("TRN2", target_bir_lowering=False, num_devices=1)
    sent, dram = {}, {}
    for name, v in arrays.items():
        v = np.ascontiguousarray(v)
        sent[f"in_{name}"] = v
        dram[name] = nc.dram_tensor(f"in_{name}", v.shape, mybir.dt.from_np(v.dtype), kind="ExternalInput").ap()
    out = nc.dram_tensor("out", (BATCH, N, D), F32, kind="ExternalOutput").ap()
    build(nc, dram, out)
    return run_bass_kernel_spmd(nc, [sent], core_ids=[0]).results[0]["out"]
```

```python
from contextlib import ExitStack

import concourse.bass as bass
from concourse import mybir
import numpy as np

F32 = mybir.dt.float32
BF16 = mybir.dt.bfloat16
I32 = mybir.dt.int32
U32 = mybir.dt.uint32
ALU = mybir.AluOpType
ACT = mybir.ActivationFunctionType
AX = mybir.AxisListType

P = 128
BATCH, N, D = 4, 512, 128
T = N // P
H = 16
HD0, HD1, HDH = 8, 4, 64
HIDDEN = 384
FC0 = HIDDEN // P
EXPERTS, F = 8, 256
FC1 = F // P
BLOCK = 16
LEVELS = 4
LN_EPS, RMS_EPS, H_EPS = 1e-5, 1e-5, 1e-8
W_SCALE = 1.0 / 127.0
NEG = -1e30

R, C = 2, H // 2
G, GH = 4, 4
SLOT = 64
MROW = 48
Q_PARTS = (0, 1, 2, 0, 1, 0)
K_PARTS = (0, 0, 0, 1, 1, 2)
XT = T + 2
UNITS = G * XT // 2
SOFT = GH * T
P_RING = 6
L0_AT = 5


OT_AT = 6
MT_AT = 3
LAG = 3
LEAD = (G * SOFT, 28)


MAX_FROM = 5
BANK, PLACES = 4, 12


def sharing(place):
    return [BANK + 2 * place, BANK + 2 * place + 1] if place < BANK else [(place - BANK) // 2]


ATTENTION_BANKS = (((0, 1, 2, 3), (4, 5), (6, 7), 3), ((3, 4, 5), (6,), (7,), 7))


def beside_places():
    def hidden(e, fc):
        return [("hidden", e, fc, k) for k in range(2)]

    def output(e, tiles=range(T)):
        return [("output", e, t) for t in tiles]

    def both(e):
        return hidden(e, 0) + output(e - 1, (0, 1)) + hidden(e, 1) + output(e - 1, (2, 3))
    places = {
        "start": hidden(0, 0) + hidden(0, 1),
        "xnT": hidden(1, 0) + hidden(1, 1),
        "rope": output(0) + hidden(2, 0) + hidden(2, 1),
        "ffn": output(1) + hidden(3, 0) + hidden(3, 1) + output(2) + hidden(4, 0) + hidden(4, 1)
        + output(3),
    }
    pieces = sum((both(e) for e in range(MAX_FROM, EXPERTS)), []) + output(EXPERTS - 1)
    assert 2 * len(pieces) <= G * SOFT
    for k, piece in enumerate(pieces):
        places["max", 2 * k + 1] = [piece]
    return places


BESIDE = beside_places()
EXPERT_ORDER = [item for items in BESIDE.values() for item in items]


def product_plan():
    plans = {}
    state = {}

    def begin(section):
        state.update(plan={}, uses=[0] * PLACES, signals=[0] * PLACES, order=[])
        plans[section] = (state["plan"], state["uses"], state["signals"])

    def use(place, *key, signalled=True):
        order = state["order"]
        since = order[len(order) - order[::-1].index(place):] if place in order else order
        shared = {o: state["uses"][o] for o in sharing(place) if o in since or place not in order}
        state["uses"][place] += 1
        state["signals"][place] += signalled
        order.append(place)
        state["plan"][key] = (place, state["uses"][place], state["signals"][place], shared)

    def expert(kind, e, *piece):
        if kind == "hidden" and piece[1] == 0:
            use(1 + piece[0] if e < MAX_FROM else 2, "ehid", e, piece[0])
        if kind == "output" and piece[0] == 0:
            use(BANK + 6 + e % 2, "ey", e)

    def beside(on, place):
        for item in BESIDE.get(place, []) if on else []:
            expert(*item)

    def attention(a, on):
        lead = LEAD[a]
        st, o_t, o, m_t = ATTENTION_BANKS[a]

        def maxima(n):
            g, i = divmod(n, SOFT)
            use(BANK + n % 3, "smax", a, g, i)
            if g and i == MT_AT:
                use(BANK + m_t, "mT", a, g - 1)
        for n in range(lead):
            maxima(n)
            if a == 0:
                beside(on, ("max", n))
        if lead == G * SOFT:
            use(BANK + m_t, "mT", a, G - 1)
        for n in range(G * SOFT + LAG):
            g, i = divmod(n, SOFT)
            if g < G:
                use(BANK + st[n % len(st)], "st", a, g, i)
            if i == LAG and g < G:
                use(BANK + o_t[g % len(o_t)], "oT", a, g, signalled=False)
            if n + lead < G * SOFT:
                maxima(n + lead)
            if lead < G * SOFT and n + lead == G * SOFT + MT_AT:
                use(BANK + m_t, "mT", a, G - 1)
            if g and i == OT_AT:
                use(BANK + o[(g - 1) % len(o)], "o", a, g - 1)
        use(BANK + o[(G - 1) % len(o)], "o", a, G - 1)
        use(BANK + o[0], "aoT", a)

    def head(on):
        beside(on, "start")
        use(BANK + 0, "xnT")
        beside(on, "xnT")
        use(3, "rope", 0)
        use(BANK + 1, "v0")
        use(0, "rope", 1)
        beside(on, "rope")
        for f in range(FC0):
            use((3, 0)[f % 2], "ffn", f)
        beside(on, "ffn")
        attention(0, on)
        use(2, "out0")

    def project(g):
        for cc in range(2):
            for side in range(2):
                use(3, "hqk", g, cc, side, 0)
                use(3, "hqk", g, cc, side, 1)
        for tp in range(XT // 2):
            use(3, "hv", g, tp)

    def rest():
        use(3, "xn1T")
        use(3, "hT")
        use(0, "c")
        use(1, "rope", 2)
        use(0, "v1")
        project(0)
        for u in range(UNITS + 2):
            if u < UNITS:
                use(u % 2, "hs", u)
                if u % 3 == 2 and u // 3 + 1 < G:
                    project(u // 3 + 1)
            if u >= 2 and (u - 2) % 3 == 0:
                use(2, "hy", (u - 2) // 3, signalled=False)
        use(3, "asum")
        for t in range(T):
            for half in range(2):
                use(3, "spread", t, half)
        use(2, "hout")
        attention(1, False)
        use(2, "up1")
        use(3, "tT")
        use(3, "logit")

    begin("first")
    head(False)
    begin("body")
    rest()
    head(True)
    begin("last")
    rest()
    for item in EXPERT_ORDER:
        expert(*item)
    return plans


PLANS = product_plan()


class Batch:

    def __init__(self, section, reg, ahead):
        self.section, self.reg, self.ahead = section, reg, ahead

    def count(self, per_batch, k):
        k += per_batch * self.ahead
        return k if self.section != "body" else self.reg * per_batch + k

    def plan_count(self, kind, place, k):
        first, body = PLANS["first"][kind][place], PLANS["body"][kind][place]
        if self.section == "first":
            return k
        if self.section == "last":
            return first + (BATCH - 1) * body + k
        return self.reg * body + (first + k)


RINGS = {"hqk", "hv", "spread"}


def ring_before(plan):
    reader = {"spread": "dve", "hqk": "act", "hv": "act"}
    last, found = {}, {}
    for key, (pair, *_) in plan.items():
        before = last.get(pair)
        found[key] = before is not None and reader.get(key[0], 0) == reader.get(before[0], 1)
        last[pair] = key
    return found


LAST_KIND = {section: ring_before(plan[0]) for section, plan in PLANS.items()}


def build(nc, dram, out):
    ctx = ExitStack()
    with ctx:
        def sb(name, shape, dt=F32):
            return ctx.enter_context(nc.sbuf_tensor(name, shape, dt))

        psum = ctx.enter_context(nc.psum_tensor("psum", [P, 8, N], F32))
        primed = []

        def sem(name, per_batch=0, prime=False):
            s = ctx.enter_context(nc.semaphore(name))
            if prime:
                primed.append(s)
            return s, per_batch, int(prime)

        w = {name: sb("w_" + name, shape) for name, shape in RESIDENT.items()}
        w_f = {name: sb("f_" + name, [P, HIDDEN]) for name in ("gate", "up", "down")}
        zeros = sb("zeros", [P, N], BF16)
        scratch = sb("scratch", [P, 40])
        ident_b = sb("ident_b", [P, P], BF16)
        hidden = sb("hidden", [P, 2, P], BF16)

        x_sb = sb("x_sb", [P, T, D])
        xn = sb("xn", [P, T, D])
        xnT = sb("xnT", [P, N])
        x1 = sb("x1", [P, T, D])
        xn1 = sb("xn1", [P, T, D])
        xn1T = sb("xn1T", [P, N])
        hT = sb("hT", [P, N])
        x2 = sb("x2", [P, T, D])
        stats = sb("stats", [P, T, 6])
        mv = sb("mv", [P, T, 2])
        rms = sb("rms", [P, T])
        var_eps = sb("var_eps", [P, T])
        rstd = sb("rstd", [P, T])

        rot = sb("rot", [P, 4, N])
        parts = sb("parts", [P, 2, 3, N], BF16)
        qs = sb("qs", [P, H, N], BF16)
        ks = sb("ks", [P, C, N], BF16)
        maxima = sb("maxima", [P, 2, SOFT])
        m_hi = sb("m_hi", [SOFT, 2, P], BF16)
        m_lo = sb("m_lo", [SOFT, 2, P], BF16)
        probs = sb("probs", [P, P_RING, N])
        v_aug = sb("v_aug", [P, T, H, 32])
        o_sb = sb("o_sb", [P, N])
        o_rc = sb("o_rc", [P, 2, T, GH])
        ao = sb("ao", [P, T, D])
        aoT = sb("aoT", [P, N])
        cT = sb("cT", [64, N])

        coarse = sb("coarse", [P, 3, 2 * P])
        qT = sb("qT", [P, 2, XT * P])
        kT = sb("kT", [P, 2, XT * P])
        v_h = sb("v_h", [P, 2, XT, GH * HDH])
        s32 = sb("s32", [P, 2, 2 * GH, 32])
        a32 = sb("a32", [P, 2, 2 * GH, 32])
        hmx = sb("hmx", [P, 2, 2 * GH])
        a_bd = sb("a_bd", [P, 2, 2 * GH, P])
        a_sum = sb("a_sum", [P, XT, H])
        a_rc = sb("a_rc", [P, 2, T, H])
        wide = sb("wide", [P, 8, N])
        w_int = {name: wide[:, i, 0:HIDDEN].bitcast(I32) for i, name in enumerate(("gate", "up", "down"))}
        esilu = (wide[:, 4, :], xn1T[:, :])
        silu = (aoT[:, :], o_sb[:, :])
        sums = probs[:, 0, 0:480]
        rc_wide = rot[:, :, :].rearrange("p (two h) (k d) -> p two (h k) d", two=2, d=HDH)

        logit = sb("logit", [P, T, EXPERTS])
        top = sb("top", [P, T, EXPERTS])
        top_at = sb("top_at", [P, T, EXPERTS], U32)
        top_f = sb("top_f", [P, T, 2])
        route = sb("route", [P, 6, T, EXPERTS])
        route_s = sb("route_s", [P, 4, T])

        filled = [sem(f"filled_{i}", prime=True) for i in range(PLACES)]
        drained = [sem(f"drained_{i}", prime=True) for i in range(PLACES)]
        setup_pool = sem("setup_pool")
        setup_dve = sem("setup_dve")
        in_first = sem("in_first")
        in_rest = sem("in_rest")
        x_in = sem("x_in", 16)
        out_done = sem("out_done", 16, prime=True)
        xb_done = sem("xb_done", 1)
        stats_done = sem("stats_done", 4 * T, prime=True)
        rstd_done = sem("rstd_done", 8)
        xn_done = sem("xn_done", T)
        xn1_done = sem("xn1_done", T)
        ss_done = sem("ss_done", 2 * T)
        h_done = sem("h_done", 2 * T)
        rot_a = sem("rot_a", 3)
        rot_done = sem("rot_done", 3)
        hi_done = sem("hi_done", 3)
        rem_done = sem("rem_done", 3)
        mid_done = sem("mid_done", 3)
        lo_done = sem("lo_done", 3)
        stack_in = [sem("stack_in0", 16 * STACK_DMAS[0]), sem("stack_in1", 16 * STACK_DMAS[1], prime=True)]
        m_hi_done = sem("m_hi_done", 2 * G)
        m_in = [sem(f"m_in{g}", 2 * M_DMAS * 16) for g in range(G)]
        pv_done = sem("pv_done", 2 * G * SOFT, prime=True)
        orc_done = sem("orc_done", 2 * G, prime=True)
        silu_done = sem("silu_done", FC0)
        esilu_done = sem("esilu_done", EXPERTS * FC1)
        base_done = sem("base_done", 1)
        coarse_done = sem("coarse_done", COARSE_STEPS)
        hmax_done = sem("hmax_done", UNITS)
        hsub_done = sem("hsub_done", UNITS)
        hexp_done = sem("hexp_done", UNITS)
        hsum_done = sem("hsum_done", UNITS)
        habd_done = sem("habd_done", UNITS)
        hpv_done = sem("hpv_done", UNITS, prime=True)
        arc_done = sem("arc_done", 1)
        wide_rc = sem("wide_rc", T)
        acc_done = sem("acc_done", 1)
        route_done = sem("route_done", ROUTE_STEPS)
        route_exp = sem("route_exp", 1)

        def nth(s, b, k):
            assert k + s[2] > 0
            return s[0], b.count(s[1], k + s[2])

        def fill(b, *key):
            place, _, signal, _ = PLANS[b.section][0][key]
            return filled[place][0], b.plan_count(2, place, signal + 1)

        def drain(b, *key):
            place, use, _, _ = PLANS[b.section][0][key]
            return drained[place][0], b.plan_count(1, place, use + 1)

        def room(b, *key):
            place, use, _, shared = PLANS[b.section][0][key]
            held = 2 if key[0] in RINGS and use > 1 and LAST_KIND[b.section][key] else 1
            return [(drained[place][0], b.plan_count(1, place, use - held + 1))] + \
                [(drained[o][0], b.plan_count(1, o, n + 1)) for o, n in shared.items()]

        def ends(b, *key):
            return filled[PLANS[b.section][0][key][0]][0], 1

        def frees(b, *key):
            return drained[PLANS[b.section][0][key][0]][0], 1

        def bank(b, *key):
            place, use, _, _ = PLANS[b.section][0][key]
            if place >= BANK:
                return place - BANK
            return 2 * place + (use % 2 if key[0] in RINGS else 0)

        def batches(engine, first, body, last):
            first(Batch("first", 0, 0), None)
            with engine.Fori(0, BATCH - 1) as reg:
                body(Batch("body", reg, 0))
                first(Batch("body", reg, 1), Batch("body", reg, 0))
            body(Batch("last", 0, BATCH - 1))
            last(Batch("last", 0, BATCH - 1))

        def beside(moe, place, do):
            for item in BESIDE.get(place, []) if moe else []:
                do(moe, *item)

        def apart(dve, at):
            dve.memset(scratch[:, at:at + 1], 0.0)

        block = ctx.enter_context(nc.Block())

        @block.sync
        def _(sp):
            x_v = dram["x"].rearrange("b (t p) d -> b p t d", p=P)
            out_v = out.rearrange("b (t p) d -> b p t d", p=P)

            def stack(b, a):
                hd = (HD0, HD1)[a]
                rows = hd * C
                for r in range(R):
                    to = qs[SLOT * r + MROW:SLOT * r + MROW + 2, C * r:C * (r + 1), :]
                    sp.dma_start(to, zeros[0:2 * C, :]).then_inc(stack_in[a][0], 16)
                    if a == 1:
                        used = 6 * HD1
                        for p0 in range(used, MROW, 16):
                            n = min(16, MROW - p0)
                            sp.dma_start(ks[SLOT * r + p0:SLOT * r + p0 + n, :, :], zeros[0:n * C, :])\
                                .then_inc(stack_in[a][0], 16)
                for side, (dst, order) in enumerate(((qs, Q_PARTS), (ks, K_PARTS))):
                    sp.wait_ge(*nth(lo_done, b, side + 1 if a == 0 else 3))
                    for s, part in enumerate(order):
                        for r in range(R):
                            p0 = SLOT * r + hd * s
                            if side == 0:
                                to = qs[p0:p0 + hd, C * r:C * (r + 1), :]
                            else:
                                to = ks[p0:p0 + hd, :, :]
                            src = parts[rows * r:rows * (r + 1), side, part, :] if a == 0 else \
                                parts[64 * side + rows * r:64 * side + rows * (r + 1), 0, part, :]
                            sp.dma_start(to, src).then_inc(stack_in[a][0], 16)

            def maxima_rows(b, a, g):
                sp.wait_ge(*drain(b, "mT", a, g))
                c0 = g * GH // R
                for src, row in ((m_hi, MROW), (m_lo, MROW + 1)):
                    for r in range(R):
                        k = SOFT // R
                        to = qs[SLOT * r + row:SLOT * r + row + 1, C * r + c0:C * r + c0 + GH // R, :]
                        sp.dma_start(to, src[k * r:k * (r + 1), g % 2, :]).then_inc(m_in[g][0], 16)

            def load_x(b):
                sp.dma_start(x_sb[:, :, :], x_v[bass.ds(b.count(1, 0), 1), :, :, :].rearrange("a p t d -> (a p) t d"))\
                    .then_inc(x_in[0], 16)

            def attention(b, a):
                sp.wait_ge(*nth(pv_done, b, a * G * SOFT))
                stack(b, a)
                for g in range(G):
                    maxima_rows(b, a, g)

            def store(b, last_expert):
                sp.wait_ge(*last_expert)
                sp.dma_start(out_v[bass.ds(b.count(1, 0), 1), :, :, :].rearrange("a p t d -> (a p) t d"),
                             x1[:, :, :]).then_inc(out_done[0], 16)

            def head(b, moe):
                attention(b, 0)
                if moe:
                    store(moe, drain(moe, "ey", EXPERTS - 1))

            def rest(b):
                if b.section == "body":
                    sp.wait_ge(*nth(stats_done, b, 4 * T))
                    load_x(Batch(b.section, b.reg, b.ahead + 1))
                attention(b, 1)

            load_x(Batch("first", 0, 0))
            sp.wait_ge(setup_dve[0], SETUP_DVE)
            sp.wait_ge(setup_pool[0], SETUP_POOL)
            batches(sp, head, rest, lambda b: store(b, drain(b, "ey", EXPERTS - 1)))
            sp.wait_ge(out_done[0], 16 * BATCH + out_done[2])

        @block.gpsimd
        def _(pool):
            pool.memset(qs[:, :, :].rearrange("p h n -> p (h n)").bitcast(F32), 0.0).then_inc(setup_pool[0], 1)
            pool.memset(v_aug[:, :, :, :], 1.0).then_inc(setup_pool[0], 1)
            pool.memset(a_bd[:, :, :, :], 0.0).then_inc(setup_pool[0], 1)
            pool.memset(coarse[:, :, 2 * P - BLOCK:2 * P], 0.0).then_inc(setup_pool[0], 1)
            pool.memset(hidden[:, :, :], 0.0).then_inc(setup_pool[0], 1)
            pool.wait_ge(setup_pool[0], 5)
            for k, sign in enumerate((-1, 1)):
                pool.affine_select(out=hidden[:, k, :], in_=hidden[:, k, :], compare_op=ALU.is_ge, fill=NEG,
                                   base=0, pattern=[[sign, P]], channel_multiplier=-sign)\
                    .then_inc(setup_pool[0], 1)
            pool.wait_ge(in_first[0], 16 * len(FIRST))
            pool.wait_ge(in_rest[0], 16 * len(REST))

            def inverse_root(b, k, src, eps):
                pool.tensor_tensor(var_eps[:, :], src, w["eps"][:, eps, :], ALU.add).then_inc(rstd_done[0], 1)
                pool.wait_ge(*nth(rstd_done, b, 2 * k + 1))
                pool.tensor_tensor(rstd[:, :], var_eps[:, :], w["neg_half"][:, :], ALU.pow)\
                    .then_inc(rstd_done[0], 1)

            def head(b, moe):
                pool.wait_ge(*nth(stats_done, b, 2 * T))
                inverse_root(b, 0, mv[:, :, 1], 0)
                pool.wait_ge(*nth(xn_done, b, T))
                pool.tensor_tensor(x_sb[:, :, :], x_sb[:, :, :],
                                   w["bo"][:, :].unsqueeze(1).to_broadcast([P, T, D]), ALU.add)\
                    .then_inc(xb_done[0], 1)

            def rest(b):
                pool.wait_ge(*nth(stats_done, b, 4 * T))
                inverse_root(b, 1, mv[:, :, 1], 0)
                pool.wait_ge(*nth(ss_done, b, T))
                inverse_root(b, 2, rms[:, :], 1)
                pool.wait_ge(*nth(xn1_done, b, T))
                pool.tensor_tensor(x1[:, :, :], x1[:, :, :],
                                   w["b_out"][:, :].unsqueeze(1).to_broadcast([P, T, D]), ALU.add)\
                    .then_inc(base_done[0], 1)
                pool.wait_ge(*drain(b, "xn1T"))
                pool.wait_ge(*nth(hpv_done, b, 0))
                src, at, width = xn1T[:, :], 0, N // 2
                for level in range(1, LEVELS + 1):
                    pair = src.rearrange("p (n two) -> p n two", two=2)
                    if level > 1:
                        pool.wait_ge(*nth(coarse_done, b, level - 1))
                    pool.tensor_tensor(sums[:, at:at + width], pair[:, :, 0], pair[:, :, 1], ALU.add)\
                        .then_inc(coarse_done[0], 1)
                    src, at, width = sums[:, at:at + width], at + width, width // 2
                pool.wait_ge(*nth(coarse_done, b, LEVELS))
                at, to = 0, 0
                for level in range(1, LEVELS + 1):
                    width = N >> level
                    halves = sums[:, at:at + width].rearrange("p (k two i) -> p k two i", two=2, i=BLOCK)
                    half = width // 2
                    for kind, (odd, power) in enumerate(((1, level), (0, level), (0, 0))):
                        scale = w["halves"][:, power:power + 1].unsqueeze(2)\
                            .to_broadcast([P, half // BLOCK, BLOCK])
                        pool.tensor_tensor(
                            coarse[:, kind, to:to + half].rearrange("p (k i) -> p k i", i=BLOCK),
                            halves[:, :, odd, :], scale, ALU.mult).then_inc(coarse_done[0], 1)
                    at, to = at + width, to + half
                for u in range(UNITS):
                    pool.wait_ge(*nth(hmax_done, b, u + 1))
                    pool.tensor_tensor(s32[:, u % 2, :, :], s32[:, u % 2, :, :],
                                       hmx[:, u % 2, :].unsqueeze(2).to_broadcast([P, 2 * GH, 32]),
                                       ALU.subtract).then_inc(hsub_done[0], 1)
                pool.wait_ge(*nth(ss_done, b, 2 * T))
                inverse_root(b, 3, rms[:, :], 1)
                pool.wait_ge(*drain(b, "up1"))
                pool.wait_ge(*drain(b, "hout"))
                pool.tensor_tensor(x1[:, :, :], x1[:, :, :], x2[:, :, :], ALU.add).then_inc(acc_done[0], 1)

            batches(pool, head, rest, lambda b: None)

        def take_y(act, b, g):
            act.wait_ge(*nth(hpv_done, b, 3 * (g + 1)))
            for cc in range(2):
                ins = act.activation(wide[:, 2 * g + cc, :], psum[:, bank(b, "hy", g) + cc, :], ACT.Copy)
            ins.then_inc(*frees(b, "hy", g))

        @block.scalar
        def _(act):
            for name in FIRST:
                target = w_int[name] if name in w_int else w[name][:]
                act.dma_start(target, dram[name]).then_inc(in_first[0], 16)
            for name in REST:
                act.dma_start(w[name][:], dram[name]).then_inc(in_rest[0], 16)
            act.wait_ge(in_first[0], 16 * len(FIRST))
            act.wait_ge(setup_pool[0], SETUP_POOL)

            def split(b, k, src, side):
                act.wait_ge(*nth(rot_done, b, k + 1))
                if k < 2:
                    act.wait_ge(*nth(stack_in[1], b, 0))
                else:
                    act.wait_ge(*nth(stack_in[0], b, 16 * STACK_DMAS[0]))
                act.activation(parts[:, side, 0, :], src, ACT.Copy).then_inc(hi_done[0], 1)
                act.wait_ge(*nth(rem_done, b, k + 1))
                act.activation(parts[:, side, 1, :], src, ACT.Copy).then_inc(mid_done[0], 1)

            def attention(b, a):
                for g in range(G):
                    for i in range(SOFT):
                        n = (a * G + g) * SOFT + i
                        width = N - (i % T) * P
                        act.wait_ge(*fill(b, "st", a, g, i))
                        act.wait_ge(*nth(pv_done, b, max(n - P_RING + 1, 0)))
                        act.activation(probs[:, n % P_RING, 0:width], psum[:, bank(b, "st", a, g, i), 0:width],
                                       ACT.Exp, scale=(1.0 / HD0, 1.0 / HD1 ** 0.5)[a])\
                            .then_inc(*frees(b, "st", a, g, i))
                        if i == LAG and g:
                            output(b, a, g - 1)
                output(b, a, G - 1)
                act.wait_ge(*fill(b, "aoT", a))
                act.activation(aoT[:, :], psum[:, bank(b, "aoT", a), :], ACT.Copy).then_inc(*frees(b, "aoT", a))

            def output(b, a, g):
                act.wait_ge(*nth(pv_done, b, (a * G + g + 1) * SOFT))
                if g:
                    act.wait_ge(*fill(b, "o", a, g - 1))
                act.activation(o_sb[:, :], psum[:, bank(b, "oT", a, g), :], ACT.Copy).then_inc(*frees(b, "oT", a, g))

            def expert(b, kind, e, *piece):
                if kind == "output" or piece[1] == 0:
                    return
                fc = piece[0]
                act.wait_ge(*fill(b, "ehid", e, fc))
                if e:
                    act.wait_ge(*drain(b, "ehid", e - 1, fc))
                act.activation(esilu[fc], psum[:, bank(b, "ehid", e, fc), :], ACT.Silu)\
                    .then_inc(esilu_done[0], 1)

            def head(b, moe):
                beside(moe, "start", expert)
                act.wait_ge(*fill(b, "xnT"))
                act.activation(xnT[:, :], psum[:, bank(b, "xnT"), :], ACT.Copy).then_inc(*frees(b, "xnT"))
                beside(moe, "xnT", expert)
                act.wait_ge(*fill(b, "v0"))
                act.activation(v_aug[:, :, :, 0:HD0],
                               psum[:, bank(b, "v0"), :].rearrange("p (t h d) -> p t h d", t=T, h=H), ACT.Copy)\
                    .then_inc(*frees(b, "v0"))
                split(b, 0, rot[:, 0, :], 0)
                split(b, 1, rot[:, 2, :], 1)
                beside(moe, "rope", expert)
                for f in range(FC0):
                    act.wait_ge(*fill(b, "ffn", f))
                    if f >= 2:
                        act.wait_ge(*drain(b, "ffn", f - 2))
                    act.activation(silu[f % 2], psum[:, bank(b, "ffn", f), :], ACT.Silu, scale=W_SCALE)\
                        .then_inc(silu_done[0], 1)
                beside(moe, "ffn", expert)
                for n in range(G * SOFT):
                    beside(moe, ("max", n), expert)
                attention(b, 0)

            def rest(b):
                act.wait_ge(*fill(b, "xn1T"))
                act.activation(xn1T[:, :], psum[:, bank(b, "xn1T"), :], ACT.Copy).then_inc(*frees(b, "xn1T"))
                act.wait_ge(in_rest[0], 16 * len(REST))
                act.wait_ge(*fill(b, "hT"))
                act.activation(hT[:, :], psum[:, bank(b, "hT"), :], ACT.Copy, scale=w["g1"][:, 0:1])\
                    .then_inc(*frees(b, "hT"))
                act.wait_ge(*fill(b, "c"))
                act.activation(cT[:, :], psum[0:64, bank(b, "c"), :], ACT.Copy).then_inc(*frees(b, "c"))
                split(b, 2, rot[:, 0, :], 0)
                act.wait_ge(*fill(b, "v1"))
                act.activation(v_aug[:, :, :, 0:HD1],
                               psum[:, bank(b, "v1"), 0:T * 64].rearrange("p (t h d) -> p t h d", t=T, h=H),
                               ACT.Copy).then_inc(*frees(b, "v1"))

                def take_projection(g):
                    for cc in range(2):
                        for side, dst in enumerate((qT, kT)):
                            for ext in range(2):
                                act.wait_ge(*fill(b, "hqk", g, cc, side, ext))
                                if g and cc == 0 and side == 0 and ext == 0:
                                    act.wait_ge(*fill(b, "hs", 3 * g - 1))
                                n0, n = (0, N) if ext == 0 else (N, 2 * P)
                                act.activation(dst[:, cc, n0:n0 + n],
                                               psum[:, bank(b, "hqk", g, cc, side, ext), 0:n], ACT.Copy)\
                                    .then_inc(*frees(b, "hqk", g, cc, side, ext))
                    for tp in range(XT // 2):
                        act.wait_ge(*fill(b, "hv", g, tp))
                        if tp == 0 and g >= 2:
                            act.wait_ge(*nth(hpv_done, b, 3 * (g - 1)))
                        act.activation(v_h[:, g % 2, 2 * tp:2 * tp + 2, :],
                                       psum[:, bank(b, "hv", g, tp), :].rearrange("p (t n) -> p t n", t=2),
                                       ACT.Copy).then_inc(*frees(b, "hv", g, tp))

                take_projection(0)
                for u in range(UNITS + 2):
                    if u < UNITS:
                        act.wait_ge(*nth(hsub_done, b, u + 1))
                        if u >= 2:
                            act.wait_ge(*nth(habd_done, b, u - 1))
                        act.activation(a32[:, u % 2, :, :], s32[:, u % 2, :, :], ACT.Exp, scale=HDH ** -0.5)\
                            .then_inc(hexp_done[0], 1)
                        if u % 3 == 2 and u // 3 + 1 < G:
                            take_projection(u // 3 + 1)
                    if u >= 4 and (u - 4) % 3 == 0:
                        take_y(act, b, (u - 4) // 3)
                attention(b, 1)
                act.wait_ge(*fill(b, "tT"))
                act.activation(hT[:, :], psum[:, bank(b, "tT"), :], ACT.Copy, scale=w["g2"][:, 0:1])\
                    .then_inc(*frees(b, "tT"))
                act.wait_ge(*nth(route_done, b, ROUTE_SUB))
                act.activation(route[:, 1, :, :], route[:, 0, :, :], ACT.Exp).then_inc(route_exp[0], 1)

            def last(b):
                for item in EXPERT_ORDER:
                    expert(b, *item)

            batches(act, head, rest, last)

        def spread(dve, b, t):
            if t == 0:
                dve.wait_ge(*drain(b, "hy", G - 1))
            for half in range(2):
                y = wide[:, 4 * half:4 * half + 4, t * P:(t + 1) * P]
                dve.wait_ge(*fill(b, "spread", t, half))
                dve.tensor_tensor(y, psum[:, bank(b, "spread", t, half), :].rearrange("p (c n) -> p c n", c=4),
                                  y, ALU.mult).then_inc(*frees(b, "spread", t, half))

        def wide_of(s):
            return s.unsqueeze(2).to_broadcast([P, T, EXPERTS])

        def chain(dve, b, done):
            steps = [done]

            def link(ins, wait=True):
                steps[0] += 1
                ins.then_inc(route_done[0], 1)
                if wait:
                    dve.wait_ge(*nth(route_done, b, steps[0]))
            return link, steps

        def router_start(dve, b):
            link, steps = chain(dve, b, 0)
            dve.wait_ge(*fill(b, "logit"))
            dve.tensor_copy(logit[:, :, :], psum[:, bank(b, "logit"), 0:T * EXPERTS].rearrange(
                "p (t e) -> p t e", t=T)).then_inc(*frees(b, "logit"))
            dve.wait_ge(*drain(b, "logit"))
            apart(dve, 4)
            for t in range(T):
                link(dve.max(top[:, t, :], logit[:, t, :]), wait=t == T - 1)
            link(dve.tensor_tensor(route[:, 0, :, :], logit[:, :, :], wide_of(top[:, :, 0]), ALU.subtract))
            assert steps[0] == ROUTE_SUB

        def router_end(dve, b):
            link, steps = chain(dve, b, ROUTE_SUB)
            apart(dve, 5)
            for t in range(T):
                link(dve.max_index(top_at[:, t, :], top[:, t, :], logit[:, t, :]), wait=t == T - 1)
            link(dve.tensor_copy(top_f[:, :, :], top_at[:, :, 0:2]))
            numbers = w["numbers"][:, :].unsqueeze(1).to_broadcast([P, T, EXPERTS])
            for k in range(2):
                link(dve.tensor_tensor(route[:, 2 + k, :, :], numbers, wide_of(top_f[:, :, k]), ALU.is_equal))
            link(dve.tensor_tensor(route[:, 2, :, :], route[:, 2, :, :], route[:, 3, :, :], ALU.add))
            dve.wait_ge(*nth(route_exp, b, 1))
            link(dve.tensor_reduce(route_s[:, 0, :], route[:, 1, :, :], AX.X, ALU.add))
            link(dve.reciprocal(route_s[:, 1, :], route_s[:, 0, :]))
            link(dve.tensor_tensor(route[:, 4, :, :], route[:, 1, :, :], wide_of(route_s[:, 1, :]), ALU.mult))
            link(dve.tensor_tensor(route[:, 4, :, :], route[:, 4, :, :], route[:, 2, :, :], ALU.mult))
            link(dve.tensor_reduce(route_s[:, 2, :], route[:, 4, :, :], AX.X, ALU.add))
            link(dve.reciprocal(route_s[:, 3, :], route_s[:, 2, :]))
            link(dve.tensor_tensor(route[:, 5, :, :], route[:, 4, :, :], wide_of(route_s[:, 3, :]), ALU.mult))
            assert steps[0] == ROUTE_STEPS, steps[0]

        def add_expert(dve, b, e):
            dve.wait_ge(*fill(b, "ey", e))
            if e == 0:
                dve.wait_ge(*nth(acc_done, b, 1))
            else:
                dve.wait_ge(*drain(b, "ey", e - 1))
            for t in range(T):
                ins = dve.scalar_tensor_tensor(out=x1[:, t, :], in0=psum[:, bank(b, "ey", e), t * P:(t + 1) * P],
                                               scalar=route[:, 5, t, e:e + 1], in1=x1[:, t, :],
                                               op0=ALU.mult, op1=ALU.add)
            ins.then_inc(*frees(b, "ey", e))

        @block.vector
        def _(dve):
            dve.memset(zeros[:, :], 0.0).then_inc(setup_dve[0], 1)
            dve.memset(ks[:, :, :], 0.0).then_inc(setup_dve[0], 1)
            for k, s in enumerate(primed):
                dve.memset(scratch[:, 8 + k:9 + k], 0.0).then_inc(s, 1)
            dve.wait_ge(setup_dve[0], 2)
            for r in range(R):
                dve.memset(ks[SLOT * r + 32:SLOT * (r + 1), :, :], 1.0).then_inc(setup_dve[0], 1)
            dve.wait_ge(in_first[0], 16 * len(FIRST))
            dve.tensor_copy(ident_b[:, :], w["ident"][:, :]).then_inc(setup_dve[0], 1)
            for name in ("gate", "up", "down"):
                dve.tensor_copy(w_f[name][:, :], w_int[name]).then_inc(setup_dve[0], 1)
            dve.wait_ge(setup_pool[0], SETUP_POOL)

            def norm_stats(b, k, src):
                for t in range(T):
                    dve.bn_stats(stats[:, t, :], src[:, t, :]).then_inc(stats_done[0], 1)
                dve.wait_ge(*nth(stats_done, b, 2 * T * k + T))
                apart(dve, k)
                for t in range(T):
                    dve.bn_aggr(mv[:, t, :], stats[:, t, :]).then_inc(stats_done[0], 1)

            def square_sums(b, k, src):
                apart(dve, 2 + k)
                for t in range(T):
                    dve.tensor_tensor_reduce(xn[:, t, :], src[:, t, :], src[:, t, :], 1.0 / D, 0.0,
                                             ALU.mult, ALU.add, rms[:, t:t + 1]).then_inc(ss_done[0], 1)

            def rotate(b, k, i, table, side):
                key = ("rope", k)
                dve.wait_ge(*fill(b, *key))
                dve.tensor_tensor(rot[:, i, :], psum[:, bank(b, *key), :], w[table][:, 0, :], ALU.mult)\
                    .then_inc(rot_a[0], 1)
                dve.tensor_tensor(rot[:, i + 1, :], psum[:, bank(b, *key) + 1, :], w[table][:, 1, :], ALU.mult)\
                    .then_inc(*frees(b, *key))
                dve.wait_ge(*drain(b, *key))
                dve.tensor_tensor(rot[:, i, :], rot[:, i, :], rot[:, i + 1, :], ALU.add).then_inc(rot_done[0], 1)

            def split(b, k, i, side):
                dve.wait_ge(*nth(hi_done, b, k + 1))
                dve.tensor_tensor(rot[:, i, :], rot[:, i, :], parts[:, side, 0, :], ALU.subtract)\
                    .then_inc(rem_done[0], 1)
                dve.wait_ge(*nth(mid_done, b, k + 1))
                dve.tensor_tensor(parts[:, side, 2, :], rot[:, i, :], parts[:, side, 1, :], ALU.subtract)\
                    .then_inc(lo_done[0], 1)

            def row_maxima(b, a, g, i):
                t = i % T
                width = (t + 1) * P
                s = psum[:, bank(b, "smax", a, g, i), 0:width]
                dve.wait_ge(*fill(b, "smax", a, g, i))
                dve.tensor_reduce(maxima[:, g % 2, i:i + 1], s, AX.X, ALU.max)\
                    .then_inc(*frees(b, "smax", a, g, i))

            def negate_maxima(b, a, g):
                src = psum[0:SOFT, bank(b, "mT", a, g), 0:P]
                dve.wait_ge(*fill(b, "mT", a, g))
                if g >= 2:
                    dve.wait_ge(*nth(m_in[g - 2], b, M_DMAS * 16 * (a + 1)))
                dve.tensor_scalar(m_hi[:, g % 2, :], src, -1.0, None, ALU.mult).then_inc(m_hi_done[0], 1)
                dve.wait_ge(*nth(m_hi_done, b, a * G + g + 1))
                dve.scalar_tensor_tensor(out=m_lo[:, g % 2, :], in0=src, scalar=-1.0, in1=m_hi[:, g % 2, :],
                                         op0=ALU.mult, op1=ALU.subtract).then_inc(*frees(b, "mT", a, g))

            def normalise(b, a, g):
                hd = (HD0, HD1)[a]
                o = psum[:, bank(b, "o", a, g), :].rearrange("p (t j d) -> p t j d", t=T, j=GH)
                dve.wait_ge(*fill(b, "o", a, g))
                dve.reciprocal(o_rc[:, g % 2, :, :], o[:, :, :, HD0]).then_inc(orc_done[0], 1)
                dve.wait_ge(*nth(orc_done, b, a * G + g + 1))
                dve.tensor_tensor(
                    ao[:, :, 0:H * hd].rearrange("p t (h d) -> p t h d", d=hd)[:, :, g * GH:(g + 1) * GH, :],
                    o[:, :, :, 0:hd], o_rc[:, g % 2, :, :].unsqueeze(3).to_broadcast([P, T, GH, hd]), ALU.mult)\
                    .then_inc(*frees(b, "o", a, g))

            def attention(b, a, moe):
                lead = LEAD[a]

                def maxima_step(n):
                    g, i = divmod(n, SOFT)
                    row_maxima(b, a, g, i)
                    if g and i == MT_AT:
                        negate_maxima(b, a, g - 1)

                for n in range(lead):
                    maxima_step(n)
                    beside(moe, ("max", n), expert)
                if lead == G * SOFT:
                    negate_maxima(b, a, G - 1)
                for n in range(G * SOFT):
                    g, i = divmod(n, SOFT)
                    if n + lead < G * SOFT:
                        maxima_step(n + lead)
                    if lead < G * SOFT and n + lead == G * SOFT + MT_AT:
                        negate_maxima(b, a, G - 1)
                    if g and i == OT_AT:
                        normalise(b, a, g - 1)
                normalise(b, a, G - 1)

            def expert(b, kind, e, *piece):
                if kind == "output":
                    if piece[0] == T - 1:
                        add_expert(dve, b, e)
                    return
                fc, k = piece
                if k == 0:
                    return
                dve.wait_ge(*nth(esilu_done, b, e * FC1 + fc + 1))
                dve.tensor_tensor(wide[:, 2 * (e % 2) + fc, :], psum[:, bank(b, "ehid", e, fc) + 1, :],
                                  esilu[fc], ALU.mult).then_inc(*frees(b, "ehid", e, fc))

            def head(b, moe):
                dve.wait_ge(*nth(x_in, b, 16))
                norm_stats(b, 0, x_sb)
                beside(moe, "start", expert)
                dve.wait_ge(*nth(rstd_done, b, 2))
                for t in range(T):
                    dve.tensor_scalar(xn[:, t, :], x_sb[:, t, :], mv[:, t, 0:1], rstd[:, t:t + 1],
                                      ALU.subtract, ALU.mult).then_inc(xn_done[0], 1)
                if moe:
                    router_end(dve, moe)
                beside(moe, "xnT", expert)
                rotate(b, 0, 0, "rope0", 0)
                rotate(b, 1, 2, "rope0", 1)
                split(b, 0, 0, 0)
                split(b, 1, 2, 1)
                beside(moe, "rope", expert)
                for f in range(FC0):
                    dve.wait_ge(*nth(silu_done, b, f + 1))
                    dve.scalar_tensor_tensor(out=wide[:, L0_AT + f, :], in0=psum[:, bank(b, "ffn", f) + 1, :],
                                             scalar=W_SCALE * W_SCALE, in1=silu[f % 2],
                                             op0=ALU.mult, op1=ALU.mult).then_inc(*frees(b, "ffn", f))
                beside(moe, "ffn", expert)
                attention(b, 0, moe)
                dve.wait_ge(*nth(xb_done, b, 1))
                dve.wait_ge(*nth(out_done, b, 0))
                dve.wait_ge(*fill(b, "out0"))
                dve.tensor_tensor(x1[:, :, :], psum[:, bank(b, "out0"), :].rearrange("p (t d) -> p t d", t=T),
                                  x_sb[:, :, :], ALU.add).then_inc(*frees(b, "out0"))
                dve.wait_ge(*drain(b, "out0"))

            def rest(b):
                norm_stats(b, 1, x1)
                dve.wait_ge(*nth(rstd_done, b, 4))
                for t in range(T):
                    dve.tensor_scalar(xn1[:, t, :], x1[:, t, :], mv[:, t, 0:1], rstd[:, t:t + 1],
                                      ALU.subtract, ALU.mult).then_inc(xn1_done[0], 1)
                dve.wait_ge(*nth(xn1_done, b, T))
                square_sums(b, 0, xn1)
                dve.wait_ge(*nth(rstd_done, b, 6))
                for t in range(T):
                    dve.tensor_scalar(xn[:, t, :], xn1[:, t, :], rstd[:, t:t + 1], None, ALU.mult)\
                        .then_inc(h_done[0], 1)
                rotate(b, 2, 0, "rope1", 0)
                split(b, 2, 0, 0)

                def extract(u):
                    kind = 0 if u % 3 < 2 else 1
                    pair = psum[:, bank(b, "hs", u):bank(b, "hs", u) + 2, :].rearrange("p k (h n) -> p (k h) n", n=P)
                    dve.wait_ge(*fill(b, "hs", u))
                    if u >= 2:
                        dve.wait_ge(*nth(hexp_done, b, u - 1))
                    for q in range(4):
                        rows = slice(32 * q, 32 * q + 32)
                        ins = dve.tensor_tensor(
                            s32[rows, u % 2, :, :], pair[rows, :, rows],
                            w["band"][rows, kind, :].unsqueeze(1).to_broadcast([32, 2 * GH, 32]), ALU.add)
                    ins.then_inc(*frees(b, "hs", u))
                    dve.wait_ge(*drain(b, "hs", u))
                    dve.tensor_reduce(hmx[:, u % 2, :], s32[:, u % 2, :, :], AX.X, ALU.max)\
                        .then_inc(hmax_done[0], 1)

                def turn(u):
                    g, tp = u // 3, u % 3
                    dve.wait_ge(*nth(hexp_done, b, u + 1))
                    dve.tensor_reduce(
                        a_sum[:, 2 * tp:2 * tp + 2, GH * g:GH * (g + 1)].rearrange("p t (c r) -> p r t c", r=R),
                        a32[:, u % 2, :, :].rearrange("p (r t c) n -> p r t c n", r=R, t=2), AX.X, ALU.add)\
                        .then_inc(hsum_done[0], 1)
                    if u >= 2:
                        dve.wait_ge(*nth(hpv_done, b, u - 1))
                    for q in range(4):
                        rows = slice(32 * q, 32 * q + 32)
                        ins = dve.transpose(a_bd[rows, u % 2, :, rows], a32[rows, u % 2, :, :])
                    ins.then_inc(habd_done[0], 1)

                for u in range(UNITS + 1):
                    if u < UNITS:
                        extract(u)
                    if u:
                        turn(u - 1)
                dve.wait_ge(*fill(b, "asum"))
                dve.tensor_scalar(a_rc[:, 0, :, :], psum[:, bank(b, "asum"), 0:T * H].rearrange(
                    "p (t h) -> p t h", t=T), H_EPS, None, ALU.add).then_inc(*frees(b, "asum"))
                dve.wait_ge(*drain(b, "asum"))
                dve.reciprocal(a_rc[:, 1, :, :], a_rc[:, 0, :, :]).then_inc(arc_done[0], 1)
                dve.wait_ge(*nth(arc_done, b, 1))
                for t in range(T):
                    if t >= 2:
                        dve.wait_ge(*fill(b, "spread", t - 2, 1))
                    dve.tensor_copy(rc_wide[:, t % 2, :, :],
                                    a_rc[:, 1, t, :].unsqueeze(2).to_broadcast([P, H, HDH]))\
                        .then_inc(wide_rc[0], 1)
                    if t:
                        spread(dve, b, t - 1)
                spread(dve, b, T - 1)
                dve.wait_ge(*nth(base_done, b, 1))
                dve.wait_ge(*fill(b, "hout"))
                dve.tensor_tensor(x1[:, :, :], psum[:, bank(b, "hout"), :].rearrange("p (t d) -> p t d", t=T),
                                  x1[:, :, :], ALU.add).then_inc(*frees(b, "hout"))
                attention(b, 1, None)
                dve.wait_ge(*fill(b, "up1"))
                dve.tensor_tensor(x2[:, :, :], psum[:, bank(b, "up1"), :].rearrange("p (t d) -> p t d", t=T),
                                  xn1[:, :, :], ALU.add).then_inc(*frees(b, "up1"))
                dve.wait_ge(*drain(b, "up1"))
                dve.wait_ge(*fill(b, "hT"))
                square_sums(b, 1, x2)
                dve.wait_ge(*nth(rstd_done, b, 8))
                for t in range(T):
                    dve.tensor_scalar(xn[:, t, :], x2[:, t, :], rstd[:, t:t + 1], None, ALU.mult)\
                        .then_inc(h_done[0], 1)
                router_start(dve, b)

            def last(b):
                for n, item in enumerate(EXPERT_ORDER):
                    if n == len(BESIDE["start"]):
                        router_end(dve, b)
                    expert(b, *item)

            batches(dve, head, rest, last)

        @block.tensor
        def _(pe):
            ident = w["ident"][:, :]
            used = {"first": [], "body": [], "last": []}

            def product(b, *key):
                used[b.section].append(key)
                for free in room(b, *key):
                    pe.wait_ge(*free)
                return bank(b, *key)

            def turn4(b, key, src, ready, n0, parts_of=P):
                k = product(b, *key)
                for t in range(T):
                    if ready is not None:
                        pe.wait_ge(*nth(ready, b, n0 + t + 1))
                    ins = pe.transpose(psum[0:parts_of, k, t * P:(t + 1) * P], src[:, t, 0:parts_of], ident)
                ins.then_inc(*ends(b, *key))

            def scores_q(b, a, g, i):
                r, cc, t = i // (SOFT // R), i // T % (GH // R), i % T
                c = g * GH // R + cc
                k = product(b, "smax", a, g, i)
                pe.matmul(psum[:, k, 0:(t + 1) * P], qs[:, C * r + c, t * P:(t + 1) * P],
                          ks[:, c, 0:(t + 1) * P], start=True, stop=True)
                pe.matmul(psum[:, k, t * P:(t + 1) * P], ident_b[:, :], hidden[:, 0, :], start=False, stop=True,
                          skip_group_check=True).then_inc(*ends(b, "smax", a, g, i))

            def turn_maxima(b, a, g):
                k = product(b, "mT", a, g)
                pe.wait_ge(*drain(b, "smax", a, g, SOFT - 1))
                pe.transpose(psum[0:SOFT, k, 0:P], maxima[:, g % 2, :], ident).then_inc(*ends(b, "mT", a, g))

            def scores_k(b, a, g, i):
                j, kb = i // T, i % T
                h = g * GH + j
                k = product(b, "st", a, g, i)
                if i == 0:
                    pe.wait_ge(*nth(m_in[g], b, 16 * M_DMAS * (a + 1)))
                pe.matmul(psum[:, k, 0:N - kb * P], ks[:, h // R, kb * P:(kb + 1) * P],
                          qs[:, C * (h % R) + h // R, kb * P:N], start=True, stop=True)
                pe.matmul(psum[:, k, 0:P], ident_b[:, :], hidden[:, 1, :], start=False, stop=True,
                          skip_group_check=True).then_inc(*ends(b, "st", a, g, i))

            def weigh(b, a, g, i):
                j, kb = i // T, i % T
                n = (a * G + g) * SOFT + i
                k = bank(b, "oT", a, g)
                pe.wait_ge(*drain(b, "st", a, g, i))
                pe.matmul(psum[32 * j:32 * j + 32, k, kb * P:N], v_aug[:, kb, g * GH + j, :],
                          probs[:, n % P_RING, 0:N - kb * P], start=(kb == 0), stop=(kb == T - 1),
                          skip_group_check=True).then_inc(pv_done[0], 1)

            def turn_output(b, a, g):
                k = product(b, "o", a, g)
                pe.wait_ge(*drain(b, "oT", a, g))
                for t in range(T):
                    ins = pe.transpose(psum[:, k, t * P:(t + 1) * P], o_sb[:, t * P:(t + 1) * P], ident)
                ins.then_inc(*ends(b, "o", a, g))

            def attention(b, a, moe):
                lead = LEAD[a]

                def maxima_step(n):
                    g, i = divmod(n, SOFT)
                    scores_q(b, a, g, i)
                    if g and i == MT_AT:
                        turn_maxima(b, a, g - 1)

                pe.wait_ge(*nth(stack_in[a], b, 16 * STACK_DMAS[a]))
                for n in range(lead):
                    maxima_step(n)
                    beside(moe, ("max", n), expert)
                if lead == G * SOFT:
                    turn_maxima(b, a, G - 1)
                for n in range(G * SOFT + LAG):
                    g, i = divmod(n, SOFT)
                    if g < G:
                        scores_k(b, a, g, i)
                    if i == LAG and g < G:
                        product(b, "oT", a, g)
                    if n >= LAG:
                        weigh(b, a, *divmod(n - LAG, SOFT))
                    if n + lead < G * SOFT:
                        maxima_step(n + lead)
                    if lead < G * SOFT and n + lead == G * SOFT + MT_AT:
                        turn_maxima(b, a, G - 1)
                    if g and i == OT_AT:
                        turn_output(b, a, g - 1)
                turn_output(b, a, G - 1)
                k = product(b, "aoT", a)
                pe.wait_ge(*drain(b, "o", a, G - 1))
                for t in range(T):
                    ins = pe.transpose(psum[:, k, t * P:(t + 1) * P], ao[:, t, :], ident)
                ins.then_inc(*ends(b, "aoT", a))

            def expert(b, kind, e, *piece):
                if kind == "hidden":
                    fc, i = piece
                    k = bank(b, "ehid", e, fc)
                    if i == 0:
                        product(b, "ehid", e, fc)
                    ins = pe.matmul(psum[:, k + i, :], w[("w1", "w3")[i]][:, e, fc * P:(fc + 1) * P], hT[:, :],
                                    start=True, stop=True)
                    if i == 1:
                        ins.then_inc(*ends(b, "ehid", e, fc))
                    return
                t = piece[0]
                k = bank(b, "ey", e)
                if t == 0:
                    product(b, "ey", e)
                    for fc in range(FC1 if e < MAX_FROM else 1):
                        pe.wait_ge(*drain(b, "ehid", e, FC1 - 1 - fc))
                for fc in range(FC1):
                    ins = pe.matmul(psum[:, k, t * P:(t + 1) * P],
                                    wide[:, 2 * (e % 2) + fc, t * P:(t + 1) * P],
                                    w["w2"][:, e * FC1 + fc, :], start=(t == 0 and fc == 0),
                                    stop=(fc == FC1 - 1), skip_group_check=True)
                if t == T - 1:
                    ins.then_inc(*ends(b, "ey", e))

            pe.wait_ge(in_first[0], 16 * len(FIRST))
            pe.wait_ge(setup_pool[0], SETUP_POOL)
            pe.wait_ge(setup_dve[0], SETUP_DVE)

            def head(b, moe):
                beside(moe, "start", expert)
                turn4(b, ("xnT",), xn, xn_done, 0)
                beside(moe, "xnT", expert)
                pe.wait_ge(*drain(b, "xnT"))

                def rope(k):
                    bk = product(b, "rope", k)
                    for swap in range(2):
                        ins = pe.matmul(psum[:, bk + swap, :], w["qk0"][:, 2 * k + swap, :], xnT[:, :],
                                        start=True, stop=True)
                    ins.then_inc(*ends(b, "rope", k))
                rope(0)
                bk = product(b, "v0")
                for t in range(T):
                    ins = pe.matmul(psum[:, bk, t * P:(t + 1) * P], xnT[:, t * P:(t + 1) * P], w["v0"][:, :],
                                    start=True, stop=True)
                ins.then_inc(*ends(b, "v0"))
                rope(1)
                beside(moe, "rope", expert)
                for f in range(FC0):
                    bk = product(b, "ffn", f)
                    for k, name in enumerate(("gate", "up")):
                        ins = pe.matmul(psum[:, bk + k, :], w_f[name][:, f * P:(f + 1) * P], xnT[:, :],
                                        start=True, stop=True)
                    ins.then_inc(*ends(b, "ffn", f))
                beside(moe, "ffn", expert)
                attention(b, 0, moe)
                bk = product(b, "out0")
                pe.wait_ge(*drain(b, "aoT", 0))
                pe.wait_ge(*drain(b, "ffn", FC0 - 1))
                for t in range(T):
                    pe.matmul(psum[:, bk, t * P:(t + 1) * P], aoT[:, t * P:(t + 1) * P], w["o0"][:, :],
                              start=(t == 0), stop=False, skip_group_check=True)
                    for f in range(FC0):
                        ins = pe.matmul(psum[:, bk, t * P:(t + 1) * P], wide[:, L0_AT + f, t * P:(t + 1) * P],
                                        w_f["down"][:, f * P:(f + 1) * P], start=False, stop=(f == FC0 - 1),
                                        skip_group_check=True)
                ins.then_inc(*ends(b, "out0"))

            def rest(b):
                pe.wait_ge(in_rest[0], 16 * len(REST))
                turn4(b, ("xn1T",), xn1, xn1_done, 0)
                turn4(b, ("hT",), xn, h_done, 0)
                bk = product(b, "c")
                pe.wait_ge(*drain(b, "hT"))
                pe.matmul(psum[0:64, bk, :], w["down1"][:, :], hT[:, :], start=True, stop=True)\
                    .then_inc(*ends(b, "c"))
                bk = product(b, "rope", 2)
                pe.wait_ge(*drain(b, "c"))
                for swap in range(2):
                    ins = pe.matmul(psum[:, bk + swap, :], w["qk1"][:, swap, :], cT[:, :], start=True, stop=True)
                ins.then_inc(*ends(b, "rope", 2))
                bk = product(b, "v1")
                for t in range(T):
                    ins = pe.matmul(psum[:, bk, t * 64:(t + 1) * 64], cT[:, t * P:(t + 1) * P], w["v1"][:, :],
                                    start=True, stop=True)
                ins.then_inc(*ends(b, "v1"))

                def project(g):
                    for cc in range(2):
                        for side in range(2):
                            lhs = w["qkv"][:, side * H * HDH + (2 * g + cc) * P:][:, 0:P]
                            for ext in range(2):
                                k = product(b, "hqk", g, cc, side, ext)
                                if g == 0 and ext == 1:
                                    pe.wait_ge(*nth(coarse_done, b, COARSE_STEPS))
                                rhs, n = (xn1T[:, :], N) if ext == 0 else (coarse[:, side, :], 2 * P)
                                pe.matmul(psum[:, k, 0:n], lhs, rhs, start=True, stop=True)\
                                    .then_inc(*ends(b, "hqk", g, cc, side, ext))
                    for tp in range(XT // 2):
                        k = product(b, "hv", g, tp)
                        for i in range(2):
                            t = 2 * tp + i
                            lhs = xn1T[:, t * P:(t + 1) * P] if t < T else \
                                coarse[:, 2, (t - T) * P:(t - T + 1) * P]
                            ins = pe.matmul(psum[:, k, i * GH * HDH:(i + 1) * GH * HDH], lhs,
                                            w["qkv"][:, 2 * H * HDH + g * GH * HDH:][:, 0:GH * HDH],
                                            start=True, stop=True)
                        ins.then_inc(*ends(b, "hv", g, tp))

                def hscores(u):
                    g, tp = u // 3, u % 3
                    k = product(b, "hs", u)
                    if tp == 0:
                        pe.wait_ge(*drain(b, "hqk", g, 1, 1, 1))
                    for i in range(2):
                        t = 2 * tp + i
                        for j in range(GH):
                            rows = slice(64 * (j % 2), 64 * (j % 2) + 64)
                            m = 2 * i + j // 2
                            ins = pe.matmul(psum[:, k + j % 2, m * P:(m + 1) * P],
                                            qT[rows, j // 2, t * P:(t + 1) * P],
                                            kT[rows, j // 2, t * P:(t + 1) * P], start=True, stop=True)
                    ins.then_inc(*ends(b, "hs", u))

                def hweigh(u):
                    g, tp = u // 3, u % 3
                    k = bank(b, "hy", g)
                    if tp == 0:
                        product(b, "hy", g)
                        pe.wait_ge(*drain(b, "hv", g, XT // 2 - 1))
                    pe.wait_ge(*nth(habd_done, b, u + 1))
                    for i in range(2):
                        t = 2 * tp + i
                        for j in range(GH):
                            rows = slice(64 * (j % 2), 64 * (j % 2) + 64)
                            y = psum[rows, k + j // 2, :]
                            v = v_h[:, g % 2, t, j * HDH:(j + 1) * HDH]
                            at = 0
                            for level in (range(0, 1) if t < T else range(1, 2) if t == T
                                          else range(2, LEVELS + 1)):
                                if level == 0:
                                    to, n = y[:, t * P:(t + 1) * P], P
                                    rhs = a_bd[:, u % 2, (j % 2) * GH + 2 * i + j // 2, :]
                                else:
                                    span = 2 * BLOCK << level
                                    n = N // span * BLOCK
                                    to = y.rearrange("p (k s) -> p k s", s=span)[
                                        :, :, span // 2 + (1 << level) - 1:span:1 << level]
                                    rhs = a_bd[:, u % 2, (j % 2) * GH + 2 * i + j // 2, at:at + n]\
                                        .rearrange("p (k i) -> p k i", i=BLOCK)
                                    at += n
                                ins = pe.matmul(to, v, rhs, start=(t == 0), stop=(level == LEVELS),
                                                skip_group_check=True)
                    ins.then_inc(hpv_done[0], 1)

                project(0)
                for u in range(UNITS + 2):
                    if u < UNITS:
                        hscores(u)
                        if u % 3 == 2 and u // 3 + 1 < G:
                            project(u // 3 + 1)
                    if u >= 2:
                        hweigh(u - 2)
                k = product(b, "asum")
                pe.wait_ge(*nth(hsum_done, b, UNITS))
                for t in range(T):
                    to = psum[:, k, t * H:(t + 1) * H]
                    pe.matmul(to, ident, a_sum[:, t, :], start=(t == 0), stop=False, skip_group_check=True)
                    for i in range(2):
                        ins = pe.matmul(to, w["scatter"][:, i, t * P:(t + 1) * P], a_sum[:, T + i, :],
                                        start=False, stop=(i == 1), skip_group_check=True)
                ins.then_inc(*ends(b, "asum"))
                for t in range(T):
                    for half in range(2):
                        k = product(b, "spread", t, half)
                        pe.wait_ge(*nth(wide_rc, b, t + 1))
                        for c in range(4):
                            h = 2 * (4 * half + c)
                            ins = pe.transpose(
                                psum[:, k, c * P:(c + 1) * P],
                                rc_wide[:, t % 2, h:h + 2, :].rearrange("p h d -> p (h d)"), ident)
                        ins.then_inc(*ends(b, "spread", t, half))
                k = product(b, "hout")
                for t in range(T):
                    pe.wait_ge(*drain(b, "spread", t, 1))
                    for c in range(8):
                        ins = pe.matmul(psum[:, k, t * P:(t + 1) * P], wide[:, c, t * P:(t + 1) * P],
                                        w["out"][:, c, :], start=(t == 0 and c == 0), stop=(c == 7),
                                        skip_group_check=True)
                ins.then_inc(*ends(b, "hout"))

                attention(b, 1, None)
                k = product(b, "up1")
                pe.wait_ge(*drain(b, "aoT", 1))
                for t in range(T):
                    ins = pe.matmul(psum[:, k, t * P:(t + 1) * P], aoT[0:64, t * P:(t + 1) * P], w["up1"][:, :],
                                    start=True, stop=True)
                ins.then_inc(*ends(b, "up1"))
                turn4(b, ("tT",), xn, h_done, T)
                k = product(b, "logit")
                pe.wait_ge(*drain(b, "tT"))
                for t in range(T):
                    ins = pe.matmul(psum[:, k, t * EXPERTS:(t + 1) * EXPERTS], hT[:, t * P:(t + 1) * P],
                                    w["router"][:, :], start=True, stop=True)
                ins.then_inc(*ends(b, "logit"))

            def last(b):
                for item in EXPERT_ORDER:
                    expert(b, *item)

            batches(pe, head, rest, last)
            for section, keys in used.items():
                plan = list(PLANS[section][0])
                assert keys == plan, [(section, u, k) for u, k in zip(keys, plan) if u != k][:3]


M_DMAS = 2 * R
STACK_DMAS = (2 * 6 * R + R, 2 * 6 * R + R + 2 * R)
COARSE_STEPS = LEVELS * 4
ROUTE_SUB = T + 1
ROUTE_STEPS = 2 * T + 12
SETUP_DVE = 2 + R + 4
SETUP_POOL = 7

RESIDENT = {
    "qk0": [P, 4, P], "v0": [P, P], "o0": [P, P], "rope0": [P, 2, N], "ident": [P, P],
    "bo": [P, P], "neg_half": [P, T], "eps": [P, 2, T], "halves": [P, LEVELS + 1],
    "qkv": [P, 3 * H * HDH], "out": [P, 8, P], "b_out": [P, P], "g1": [P, 1], "g2": [P, 1],
    "down1": [P, 64], "qk1": [64, 2, P], "v1": [64, 64], "up1": [64, P], "router": [P, EXPERTS],
    "w1": [P, EXPERTS, F], "w3": [P, EXPERTS, F], "w2": [P, EXPERTS * FC1, P],
    "rope1": [P, 2, N], "band": [P, 2, 32], "scatter": [P, 2, N], "numbers": [P, EXPERTS],
}
FIRST = ["qk0", "ident", "v0", "gate", "up", "rope0", "o0", "down", "bo", "neg_half", "eps"]
REST = [k for k in RESIDENT if k not in FIRST]


def head_order(hd):
    r, d, c = np.meshgrid(np.arange(R), np.arange(hd), np.arange(C), indexing="ij")
    return ((R * c + r) * hd + d).reshape(-1)


def rope_table(hd):
    inv = (1.0 / 10000.0 ** (np.arange(0, hd, 2, dtype=np.float32) / np.float32(hd))).astype(np.float32)
    ang = (np.arange(N, dtype=np.float32)[:, None] * inv[None, :]).astype(np.float32)
    d = head_order(hd) % hd
    sign = np.where(d % 2 == 0, -1.0, 1.0)[:, None]
    return np.stack([np.cos(ang).T[d // 2], np.sin(ang).T[d // 2] * sign], 1).astype(np.float32)


def constants():
    p = np.arange(P)
    c = {"ident": np.eye(P, dtype=np.float32), "rope0": rope_table(HD0)}
    c["rope1"] = np.concatenate([rope_table(HD1)] * 2, 0)
    c["neg_half"] = np.full((P, T), -0.5, np.float32)
    c["eps"] = np.stack([np.full((P, T), e, np.float32) for e in (LN_EPS, RMS_EPS)], 1)
    c["halves"] = np.tile((0.5 ** np.arange(LEVELS + 1)).astype(np.float32), (P, 1))
    row, col = (p % 32)[:, None], np.arange(32)[None, :]
    same = row // BLOCK == col // BLOCK
    c["band"] = np.stack([np.where(same & (col <= row), 0.0, NEG), np.where(same, 0.0, NEG)], 1).astype(np.float32)
    scatter = np.zeros((P, 2, N), np.float32)
    at = [0, 0]
    for level in range(1, LEVELS + 1):
        i = 0 if level == 1 else 1
        span = 2 * BLOCK << level
        for k in range(N // span):
            for j in range(BLOCK):
                scatter[at[i], i, k * span + span // 2 + ((j + 1) << level) - 1] = 1.0
                at[i] += 1
    c["scatter"] = scatter
    c["numbers"] = np.tile(np.arange(EXPERTS, dtype=np.float32), (P, 1))
    return c


def swapped(order):
    return order ^ 1


def kernel(**inputs):
    import concourse.bacc as bacc
    from concourse.bass_utils import run_bass_kernel_spmd

    a = {k: np.asarray(v) for k, v in inputs.items()}
    o0, o1 = head_order(HD0), head_order(HD1)

    def chunks(m):
        return m.reshape(-1, P, m.shape[1]).transpose(1, 0, 2)

    arrays = {
        "x": a["L0_attn_x"],
        "qk0": np.stack([a["L0_attn_Wq"][o0].T, a["L0_attn_Wq"][swapped(o0)].T,
                         a["L0_attn_Wk"][o0].T, a["L0_attn_Wk"][swapped(o0)].T], 1),
        "v0": a["L0_attn_Wv"].T, "o0": a["L0_attn_Wo"].T,
        "bo": np.broadcast_to(a["L0_attn_bo"], (P, D)),
        "gate": a["L0_ffn_w_gate"].T, "up": a["L0_ffn_w_up"].T,
        "down": chunks(a["L0_ffn_w_down"].T).reshape(P, -1),
        "qkv": a["L1_attn_w_qkv"].T, "out": chunks(a["L1_attn_w_out"].T),
        "b_out": np.broadcast_to(a["L1_attn_b_out"], (P, D)),
        "g1": a["L1_ffn_g1"][:, None], "g2": a["L1_ffn_g2"][:, None],
        "down1": a["L1_ffn_w_down"],
        "qk1": np.stack([np.concatenate([a["L1_ffn_wq"][:, o], a["L1_ffn_wk"][:, o]], 1)
                         for o in (o1, swapped(o1))], 1),
        "v1": a["L1_ffn_wv"], "up1": a["L1_ffn_w_up"], "router": a["L1_ffn_router_w"],
        "w1": a["L1_ffn_w1"].transpose(1, 0, 2), "w3": a["L1_ffn_w3"].transpose(1, 0, 2),
        "w2": chunks(a["L1_ffn_w2"].reshape(EXPERTS * F, D)),
        **constants(),
    }
    nc = bacc.Bacc("TRN2", target_bir_lowering=False, num_devices=1)
    sent, dram = {}, {}
    for name, v in arrays.items():
        v = np.ascontiguousarray(v)
        sent[f"in_{name}"] = v
        dram[name] = nc.dram_tensor(f"in_{name}", v.shape, mybir.dt.from_np(v.dtype), kind="ExternalInput").ap()
    out = nc.dram_tensor("out", (BATCH, N, D), F32, kind="ExternalOutput").ap()
    build(nc, dram, out)
    return run_bass_kernel_spmd(nc, [sent], core_ids=[0]).results[0]["out"]
```

```python
from contextlib import ExitStack

import concourse.bass as bass
from concourse import mybir
import numpy as np

F32 = mybir.dt.float32
BF16 = mybir.dt.bfloat16
I32 = mybir.dt.int32
U32 = mybir.dt.uint32
ALU = mybir.AluOpType
ACT = mybir.ActivationFunctionType
AX = mybir.AxisListType

P = 128
BATCH, N, D = 4, 512, 128
T = N // P
H = 16
HD0, HD1, HDH = 8, 4, 64
HIDDEN = 384
FC0 = HIDDEN // P
EXPERTS, F = 8, 256
FC1 = F // P
BLOCK = 16
LEVELS = 4
LN_EPS, RMS_EPS, H_EPS = 1e-5, 1e-5, 1e-8
W_SCALE = 1.0 / 127.0
NEG = -1e30

R, C = 2, H // 2
G, GH = 4, 4
SLOT = 64
MROW = 48
Q_PARTS = (0, 1, 2, 0, 1, 0)
K_PARTS = (0, 0, 0, 1, 1, 2)
XT = T + 2
UNITS = G * XT // 2
SOFT = GH * T
P_RING = 6
L0_AT = 5

OT_AT = 8
MT_AT = 3
LAG = 3
MAXIMA = G * SOFT
AHEAD, BESIDE_FROM = (2 * SOFT, MAXIMA), (0, 0)
MAX1_FROM, LAST_SHARE = 2, 0.5
MAX_FROM, MAX_TO = 4, 6
BANK, PLACES = 4, 12


def sharing(place):
    return [BANK + 2 * place, BANK + 2 * place + 1] if place < BANK else [(place - BANK) // 2]


ST_BANKS, O_T_BANKS, O_BANK = (0, 1, 2), ((3, 3), (3, 5)), 6


def smax_bank(a, n):
    early, late = (((0, 1, 2), (4, 5)), ((2, 3), ()))[a]
    banks = early if n < AHEAD[a] else late
    return banks[n % len(banks)]


def mt_bank(a, g):
    return (3 if g < 1 else 7, 3 if g < 2 else 7)[a]


SPREAD_BANK, HOUT_BANK = 7, 4
ENDINGS = {1: ("asum",)}
for tile in range(T):
    ENDINGS.update({4 + 6 * tile: ("spread", tile, 0), 6 + 6 * tile: ("spread", tile, 1),
                    9 + 6 * tile: ("hout", tile)})
NORM0_AT = 34


def pieces_at(u):
    g = u // 3 + 1
    if g >= G:
        return []
    return projections(g)[4 * (u % 3):4 * (u % 3 + 1)]


def projections(g):
    if g == 0:
        return [("hqk", 0, cc, side, 0) for cc in range(2) for side in range(2)] + \
            [("hv", 0, tp) for tp in range(T // 2)] + \
            [("hqk", 0, cc, side, 1) for cc in range(2) for side in range(2)] + [("hv", 0, XT // 2 - 1)]
    return [("hqk", g, cc, side, ext) for cc in range(2) for side in range(2) for ext in range(2)] + \
        [("hv", g, tp) for tp in range(XT // 2)]


def in_turn(pieces, steps):
    order = []
    for k in range(max(len(pieces), len(steps))):
        order += [("piece", p) for p in pieces[k:k + 1]] + [("step", n) for n in steps[k:k + 1]]
    return order


def maximum_beside(a, n):
    k = n - BESIDE_FROM[a] + AHEAD[a]
    return [k] if AHEAD[a] <= k < MAXIMA else []


def last_turn(a):
    return BESIDE_FROM[a] + MAXIMA - AHEAD[a] + MT_AT - 1


def maxima_at(u):
    if u < MAX1_FROM:
        return [], []
    share = [0] * MAX1_FROM + [2] * (UNITS - 3 - MAX1_FROM) + [LAST_SHARE] * 3
    lo, hi = [round(sum(share[:u + k]) * AHEAD[1] / sum(share)) for k in range(2)]
    return list(range(lo, (lo + hi) // 2)), list(range((lo + hi) // 2, hi))


def two_pairs(e):
    return e < MAX_FROM or e >= MAX_TO


def beside_places():
    def hidden(e, fc):
        return [("hidden", e, fc, k) for k in range(2)]

    def output(e, tiles=range(T)):
        return [("output", e, t) for t in tiles]

    def both(e):
        return hidden(e, 0) + output(e - 1, (0, 1)) + hidden(e, 1) + output(e - 1, (2, 3))
    places = {
        "start0": hidden(0, 0), "start1": hidden(0, 1),
        "gate": hidden(1, 0) + output(0) + hidden(1, 1),
        "ffn": output(1) + hidden(2, 0) + hidden(2, 1) + both(3),
    }
    pieces = both(4) + both(5)
    assert 2 * len(pieces) <= AHEAD[0]
    for k, piece in enumerate(pieces):
        places["max", 2 * k + 1] = [piece]
    places.update({
        "out0": hidden(6, 0) + output(5, (0, 1)), "norm1": hidden(6, 1) + output(5, (2, 3)),
        "xn1T": hidden(7, 0) + output(6, (0, 1)), "square": hidden(7, 1) + output(6, (2, 3)),
        "hT": output(7),
    })
    return places


BESIDE = beside_places()
EXPERT_ORDER = [item for place, items in BESIDE.items() if place not in ("start0", "start1") for item in items]


def product_plan():
    plans = {}
    state = {}

    def begin(section):
        state.update(plan={}, uses=[0] * PLACES, signals=[0] * PLACES, order=[])
        plans[section] = (state["plan"], state["uses"], state["signals"])

    def use(place, *key, signalled=True):
        order = state["order"]
        since = order[len(order) - order[::-1].index(place):] if place in order else order
        shared = {o: state["uses"][o] for o in sharing(place) if o in since or place not in order}
        state["uses"][place] += 1
        state["signals"][place] += signalled
        order.append(place)
        state["plan"][key] = (place, state["uses"][place], state["signals"][place], shared)

    def expert(kind, e, *piece):
        if kind == "hidden" and piece[1] == 0:
            use(1 + piece[0] if two_pairs(e) else 2, "ehid", e, piece[0])
        if kind == "output" and piece[0] == 0:
            use(BANK + 6 + e % 2, "ey", e)

    def beside(on, place):
        for item in BESIDE.get(place, []) if on else []:
            expert(*item)

    def maxima(a, n):
        g, i = divmod(n, SOFT)
        use(BANK + smax_bank(a, n), "smax", a, g, i)
        if g and i == MT_AT:
            use(BANK + mt_bank(a, g - 1), "mT", a, g - 1)

    def attention(a):
        for n in range(MAXIMA + LAG):
            g, i = divmod(n, SOFT)
            if g < G:
                use(BANK + ST_BANKS[n % len(ST_BANKS)], "st", a, g, i)
            if i == LAG and g < G:
                use(BANK + O_T_BANKS[a][g % 2], "oT", a, g, signalled=False)
            for k in maximum_beside(a, n):
                maxima(a, k)
            if n == last_turn(a):
                use(BANK + mt_bank(a, G - 1), "mT", a, G - 1)
            if g and i == OT_AT:
                use(BANK + O_BANK, "o", a, g - 1)
            if a == 1 and n in ENDINGS:
                ending(*ENDINGS[n])
        use(BANK + O_BANK, "o", a, G - 1)

    def ending(kind, *piece):
        if kind != "hout":
            use(BANK + SPREAD_BANK, kind, *piece)
        elif piece[0] == 0:
            use(BANK + HOUT_BANK, "hout")

    def junction(b, n):
        if n:
            use(BANK + 2, "xnT")
        if b:
            use(BANK + O_BANK, "aoT", 1)
        if n:
            use(0, "rope", 0)
        if b:
            use(BANK + 4, "up1")
        if n:
            use(BANK + 3, "v0")
            use(3, "rope", 1)
            use(0, "ffn", 0)
        if b:
            use(BANK + 5, "tT")
            use(BANK + 6, "logit")
            beside(True, "start0")
            beside(True, "start1")

    def head(on):
        beside(on, "gate")
        for f in range(1, FC0):
            use((0, 3)[f % 2], "ffn", f)
        beside(on, "ffn")
        for n in range(AHEAD[0]):
            maxima(0, n)
            beside(on, ("max", n))
        attention(0)
        use(BANK + 0, "out0")
        use(BANK + O_BANK, "aoT", 0)
        beside(on, "out0")
        beside(on, "norm1")
        use(BANK + 1, "xn1T")
        beside(on, "xn1T")
        beside(on, "square")
        use(BANK + 0, "hT")
        beside(on, "hT")
        use(BANK + 7, "c")
        use(1, "rope", 2)
        use(BANK + 1, "v1")

    def rest():
        for key in projections(0):
            use(3, *key)
        for u in range(UNITS + 2):
            if u < UNITS:
                use(0, "hs", u)
                early, late = maxima_at(u)
                for n in early:
                    maxima(1, n)
            if u >= 2 and (u - 2) % 3 == 0:
                use(2, "hy", (u - 2) // 3, signalled=False)
            if u < UNITS:
                for kind, key in in_turn(pieces_at(u), late):
                    if kind == "piece":
                        use(3, *key)
                    else:
                        maxima(1, key)
        attention(1)

    begin("first")
    junction(False, True)
    head(False)
    begin("body")
    rest()
    junction(True, True)
    head(True)
    begin("last")
    rest()
    junction(True, False)
    for item in EXPERT_ORDER:
        expert(*item)
    return plans


PLANS = product_plan()


class Batch:

    def __init__(self, section, reg, ahead):
        self.section, self.reg, self.ahead = section, reg, ahead

    def count(self, per_batch, k):
        k += per_batch * self.ahead
        return k if self.section != "body" else self.reg * per_batch + k

    def plan_count(self, kind, place, k):
        first, body = PLANS["first"][kind][place], PLANS["body"][kind][place]
        if self.section == "first":
            return k
        if self.section == "last":
            return first + (BATCH - 1) * body + k
        return self.reg * body + (first + k)


RING = ("hqk", "hv")


def follows_in_ring(plan):
    last, found = {}, {}
    for key, (place, *_) in plan.items():
        found[key] = key[0] in RING and last.get(place) in RING
        last[place] = key[0]
    return found


FOLLOWS_IN_RING = {section: follows_in_ring(plan[0]) for section, plan in PLANS.items()}


def build(nc, dram, out):
    ctx = ExitStack()
    with ctx:
        def sb(name, shape, dt=F32):
            return ctx.enter_context(nc.sbuf_tensor(name, shape, dt))

        psum = ctx.enter_context(nc.psum_tensor("psum", [P, 8, N], F32))
        primed = []

        def sem(name, per_batch=0, prime=False):
            s = ctx.enter_context(nc.semaphore(name))
            if prime:
                primed.append(s)
            return s, per_batch, int(prime)

        w = {name: sb("w_" + name, shape) for name, shape in RESIDENT.items()}
        w_f = {name: sb("f_" + name, [P, HIDDEN]) for name in ("gate", "up", "down")}
        zeros = sb("zeros", [P, N], BF16)
        scratch = sb("scratch", [P, 40])
        ident_b = sb("ident_b", [P, P], BF16)
        hidden = sb("hidden", [P, 2, P], BF16)

        x_sb = sb("x_sb", [P, T, D])
        xn = sb("xn", [P, T, D])
        xnT = sb("xnT", [P, N])
        x1 = sb("x1", [P, T, D])
        xn1 = sb("xn1", [P, T, D])
        xn1T = sb("xn1T", [P, N])
        hT = sb("hT", [P, N])
        x2 = sb("x2", [P, T, D])
        stats = [sb(f"stats{i}", [P, T, 6]) for i in range(2)]
        mv = [sb(f"mv{i}", [P, T, 2]) for i in range(2)]
        rms = sb("rms", [P, T])
        var_eps = [sb(f"var_eps{i}", [P, T]) for i in range(2)]
        rstd = [sb(f"rstd{i}", [P, T]) for i in range(2)]

        rot = sb("rot", [P, 4, N])
        parts = sb("parts", [P, 2, 3, N], BF16)
        qs = sb("qs", [P, H, N], BF16)
        ks = sb("ks", [P, C, N], BF16)
        maxima = sb("maxima", [P, 2, SOFT])
        m_hi = sb("m_hi", [SOFT, 2, P], BF16)
        m_lo = sb("m_lo", [SOFT, 2, P], BF16)
        probs = sb("probs", [P, P_RING, N])
        v_aug = sb("v_aug", [P, T, H, 32])
        o_sb = sb("o_sb", [P, N])
        o_rc = sb("o_rc", [P, 2, T, GH])
        ao = sb("ao", [P, T, D])
        aoT = sb("aoT", [P, N])
        cT = sb("cT", [64, N])

        coarse = sb("coarse", [P, 3, 2 * P])
        qT = [sb("qT", [P, 2, XT * P])]
        kT = [sb("kT", [P, 2, XT * P])]
        v_h = sb("v_h", [P, 2, XT, GH * HDH])
        s32 = sb("s32", [P, 2, 2 * GH, 32])
        a32 = sb("a32", [P, 2, 2 * GH, 32])
        hmx = sb("hmx", [P, 2, 2 * GH])
        a_bd = sb("a_bd", [P, 2, 2 * GH, P])
        a_sum = sb("a_sum", [P, XT, H])
        a_rc = sb("a_rc", [P, 2, T, H])
        wide = sb("wide", [P, 8, N])
        w_int = {name: wide[:, i, 0:HIDDEN].bitcast(I32) for i, name in enumerate(("gate", "up", "down"))}
        esilu = (wide[:, 4, :], x2[:, :, :].rearrange("p t d -> p (t d)"))
        silu = (aoT[:, :], o_sb[:, :])
        h1T = o_sb
        qT.append(probs[:, 0:3, :].rearrange("p a (h n) -> p (a h) n", h=2).rearrange(
            "p (two k) n -> p two (k n)", two=2))
        kT.append(rot[:, 0:3, :].rearrange("p a (h n) -> p (a h) n", h=2).rearrange(
            "p (two k) n -> p two (k n)", two=2))
        sums = probs[:, 0, 0:480]
        rc_wide = rot[:, :, :].rearrange("p (two h) (k d) -> p two (h k) d", two=2, d=HDH)

        logit = sb("logit", [P, T, EXPERTS])
        top = sb("top", [P, T, EXPERTS])
        top_at = sb("top_at", [P, T, EXPERTS], U32)
        top_f = sb("top_f", [P, T, 2])
        route = sb("route", [P, 6, T, EXPERTS])
        route_s = sb("route_s", [P, 4, T])

        filled = [sem(f"filled_{i}", prime=True) for i in range(PLACES)]
        drained = [sem(f"drained_{i}", prime=True) for i in range(PLACES)]
        setup_pool = sem("setup_pool")
        setup_dve = sem("setup_dve")
        in_first = sem("in_first")
        in_rest = sem("in_rest")
        x_in = sem("x_in", 16)
        out_done = sem("out_done", 16, prime=True)
        xb_done = sem("xb_done", 1)
        stats0_done = sem("stats0_done", 2 * T)
        stats1_done = sem("stats1_done", 2 * T)
        rstd0_done = sem("rstd0_done", 2)
        rstd_done = sem("rstd_done", 6)
        xn_done = sem("xn_done", T)
        xn1_done = sem("xn1_done", T)
        ss_done = sem("ss_done", 2 * T)
        h_done = sem("h_done", 2 * T)
        rot_a = sem("rot_a", 3)
        rot_done = sem("rot_done", 3)
        hi_done = sem("hi_done", 3)
        rem_done = sem("rem_done", 3)
        mid_done = sem("mid_done", 3)
        lo_done = sem("lo_done", 3)
        stack_in = [sem("stack_in0", 16 * STACK_DMAS[0]), sem("stack_in1", 16 * STACK_DMAS[1], prime=True)]
        m_hi_done = sem("m_hi_done", 2 * G)
        m_in = [sem(f"m_in{g}", 2 * M_DMAS * 16) for g in range(G)]
        pv_done = sem("pv_done", 2 * G * SOFT, prime=True)
        orc_done = sem("orc_done", 2 * G, prime=True)
        silu_done = sem("silu_done", FC0)
        esilu_done = sem("esilu_done", EXPERTS * FC1)
        base_done = sem("base_done", 1)
        coarse_done = sem("coarse_done", COARSE_STEPS)
        hmax_done = sem("hmax_done", UNITS)
        hsub_done = sem("hsub_done", UNITS)
        hexp_done = sem("hexp_done", UNITS)
        hsum_done = sem("hsum_done", UNITS)
        habd_done = sem("habd_done", UNITS)
        hpv_done = sem("hpv_done", UNITS, prime=True)
        arc_done = sem("arc_done", 1)
        wide_rc = sem("wide_rc", T)
        acc_done = sem("acc_done", 1)
        route_done = sem("route_done", ROUTE_STEPS)
        route_exp = sem("route_exp", 1)

        def nth(s, b, k):
            assert k + s[2] > 0
            return s[0], b.count(s[1], k + s[2])

        def fill(b, *key):
            place, _, signal, _ = PLANS[b.section][0][key]
            return filled[place][0], b.plan_count(2, place, signal + 1)

        def drain(b, *key):
            place, use, _, _ = PLANS[b.section][0][key]
            return drained[place][0], b.plan_count(1, place, use + 1)

        def room(b, *key):
            place, use, _, shared = PLANS[b.section][0][key]
            held = 2 if FOLLOWS_IN_RING[b.section][key] else 1
            return [(place, use - held)] + list(shared.items())

        def ends(b, *key):
            return filled[PLANS[b.section][0][key][0]][0], 1

        def frees(b, *key):
            return drained[PLANS[b.section][0][key][0]][0], 1

        def bank(b, *key):
            place, use, _, _ = PLANS[b.section][0][key]
            if place >= BANK:
                return place - BANK
            return 2 * place + (use % 2 if key[0] in RING else 0)

        def batches(engine, rest, junction, head, last):
            junction(None, Batch("first", 0, 0))
            head(Batch("first", 0, 0), None)
            copy = engine.alloc_register("turn")
            with engine.Fori(0, BATCH - 1) as reg:
                b, after = Batch("body", reg, 0), Batch("body", reg, 1)
                rest(b, after)
                engine.reg_mov(copy, reg)
                again = engine.snap(copy)
                b, after = Batch("body", again, 0), Batch("body", again, 1)
                junction(b, after)
                head(after, b)
            b = Batch("last", 0, BATCH - 1)
            rest(b, None)
            junction(b, None)
            last(b)

        def beside(moe, place, do):
            for item in BESIDE.get(place, []) if moe else []:
                do(moe, *item)

        def apart(dve, at):
            dve.memset(scratch[:, at:at + 1], 0.0)

        block = ctx.enter_context(nc.Block())

        @block.sync
        def _(sp):
            x_v = dram["x"].rearrange("b (t p) d -> b p t d", p=P)
            out_v = out.rearrange("b (t p) d -> b p t d", p=P)

            def stack(b, a):
                hd = (HD0, HD1)[a]
                rows = hd * C
                for r in range(R):
                    to = qs[SLOT * r + MROW:SLOT * r + MROW + 2, C * r:C * (r + 1), :]
                    sp.dma_start(to, zeros[0:2 * C, :]).then_inc(stack_in[a][0], 16)
                    if a == 1:
                        used = 6 * HD1
                        for p0 in range(used, MROW, 16):
                            n = min(16, MROW - p0)
                            sp.dma_start(ks[SLOT * r + p0:SLOT * r + p0 + n, :, :], zeros[0:n * C, :])\
                                .then_inc(stack_in[a][0], 16)
                for sides in ((0,), (1,)) if a == 0 else ((0, 1),):
                    for part, done in enumerate((hi_done, mid_done, lo_done)):
                        sp.wait_ge(*nth(done, b, sides[0] + 1 if a == 0 else 3))
                        for side in sides:
                            dst, order = ((qs, Q_PARTS), (ks, K_PARTS))[side]
                            for s, r in [(s, r) for s in range(6) for r in range(R) if order[s] == part]:
                                p0 = SLOT * r + hd * s
                                to = dst[p0:p0 + hd, C * r:C * (r + 1), :] if side == 0 else \
                                    dst[p0:p0 + hd, :, :]
                                src = parts[rows * r:rows * (r + 1), side, part, :] if a == 0 else \
                                    parts[64 * side + rows * r:64 * side + rows * (r + 1), 0, part, :]
                                sp.dma_start(to, src).then_inc(stack_in[a][0], 16)

            def maxima_rows(b, a, g):
                sp.wait_ge(*drain(b, "mT", a, g))
                c0 = g * GH // R
                for src, row in ((m_hi, MROW), (m_lo, MROW + 1)):
                    for r in range(R):
                        k = SOFT // R
                        to = qs[SLOT * r + row:SLOT * r + row + 1, C * r + c0:C * r + c0 + GH // R, :]
                        sp.dma_start(to, src[k * r:k * (r + 1), g % 2, :]).then_inc(m_in[g][0], 16)

            def load_x(b):
                sp.dma_start(x_sb[:, :, :], x_v[bass.ds(b.count(1, 0), 1), :, :, :].rearrange("a p t d -> (a p) t d"))\
                    .then_inc(x_in[0], 16)

            def stacks(b, a):
                sp.wait_ge(*nth(pv_done, b, a * MAXIMA))
                stack(b, a)

            def rows(b, a):
                for g in range(G):
                    maxima_rows(b, a, g)

            def store(b, last_expert):
                sp.wait_ge(*last_expert)
                sp.dma_start(out_v[bass.ds(b.count(1, 0), 1), :, :, :].rearrange("a p t d -> (a p) t d"),
                             x1[:, :, :]).then_inc(out_done[0], 16)

            def head(b, moe):
                stacks(b, 0)
                rows(b, 0)
                if moe:
                    store(moe, drain(moe, "ey", EXPERTS - 1))
                stacks(b, 1)

            def rest(b, after):
                if after:
                    sp.wait_ge(*nth(base_done, b, 1))
                    load_x(after)
                rows(b, 1)

            load_x(Batch("first", 0, 0))
            sp.wait_ge(in_first[0], 16 * len(FIRST))
            for name in REST:
                sp.dma_start(w[name][:], dram[name]).then_inc(in_rest[0], 16)
            sp.wait_ge(setup_dve[0], SETUP_DVE)
            sp.wait_ge(setup_pool[0], SETUP_POOL)
            batches(sp, rest, lambda b, after: None, head, lambda b: store(b, drain(b, "ey", EXPERTS - 1)))
            sp.wait_ge(out_done[0], 16 * BATCH + out_done[2])

        @block.gpsimd
        def _(pool):
            pool.memset(qs[:, :, :].rearrange("p h n -> p (h n)").bitcast(F32), 0.0).then_inc(setup_pool[0], 1)
            pool.memset(v_aug[:, :, :, :], 1.0).then_inc(setup_pool[0], 1)
            pool.memset(a_bd[:, :, :, :], 0.0).then_inc(setup_pool[0], 1)
            pool.memset(coarse[:, :, 2 * P - BLOCK:2 * P], 0.0).then_inc(setup_pool[0], 1)
            pool.memset(hidden[:, :, :], 0.0).then_inc(setup_pool[0], 1)
            pool.wait_ge(setup_pool[0], 5)
            for k, sign in enumerate((-1, 1)):
                pool.affine_select(out=hidden[:, k, :], in_=hidden[:, k, :], compare_op=ALU.is_ge, fill=NEG,
                                   base=0, pattern=[[sign, P]], channel_multiplier=-sign)\
                    .then_inc(setup_pool[0], 1)
            pool.wait_ge(in_first[0], 16 * len(FIRST))

            def inverse_root(b, i, done, k, src, eps):
                pool.tensor_tensor(var_eps[i][:, :], src, w["eps"][:, eps, :], ALU.add).then_inc(done[0], 1)
                pool.wait_ge(*nth(done, b, 2 * k + 1))
                pool.tensor_tensor(rstd[i][:, :], var_eps[i][:, :], w["neg_half"][:, :], ALU.pow)\
                    .then_inc(done[0], 1)

            def norm0(b):
                pool.wait_ge(*nth(stats0_done, b, 2 * T))
                inverse_root(b, 0, rstd0_done, 0, mv[0][:, :, 1], 0)
                pool.wait_ge(*nth(xn_done, b, T))
                pool.tensor_tensor(x_sb[:, :, :], x_sb[:, :, :],
                                   w["bo"][:, :].unsqueeze(1).to_broadcast([P, T, D]), ALU.add)\
                    .then_inc(xb_done[0], 1)

            def head(b, moe):
                pool.wait_ge(*nth(stats1_done, b, 2 * T))
                inverse_root(b, 1, rstd_done, 0, mv[1][:, :, 1], 0)
                pool.wait_ge(*nth(ss_done, b, T))
                inverse_root(b, 1, rstd_done, 1, rms[:, :], 1)
                pool.wait_ge(in_rest[0], 16 * len(REST))
                pool.wait_ge(*drain(b, "xn1T"))
                pool.wait_ge(*nth(hpv_done, b, 0))
                src, at, width = xn1T[:, :], 0, N // 2
                for level in range(1, LEVELS + 1):
                    pair = src.rearrange("p (n two) -> p n two", two=2)
                    if level > 1:
                        pool.wait_ge(*nth(coarse_done, b, level - 1))
                    pool.tensor_tensor(sums[:, at:at + width], pair[:, :, 0], pair[:, :, 1], ALU.add)\
                        .then_inc(coarse_done[0], 1)
                    src, at, width = sums[:, at:at + width], at + width, width // 2
                pool.wait_ge(*nth(coarse_done, b, LEVELS))
                at, to = 0, 0
                for level in range(1, LEVELS + 1):
                    width = N >> level
                    halves = sums[:, at:at + width].rearrange("p (k two i) -> p k two i", two=2, i=BLOCK)
                    half = width // 2
                    for kind, (odd, power) in enumerate(((1, level), (0, level), (0, 0))):
                        scale = w["halves"][:, power:power + 1].unsqueeze(2)\
                            .to_broadcast([P, half // BLOCK, BLOCK])
                        pool.tensor_tensor(
                            coarse[:, kind, to:to + half].rearrange("p (k i) -> p k i", i=BLOCK),
                            halves[:, :, odd, :], scale, ALU.mult).then_inc(coarse_done[0], 1)
                    at, to = at + width, to + half

            def rest(b, after):
                pool.wait_ge(*nth(xn1_done, b, T))
                pool.wait_ge(*nth(out_done, b, 0))
                pool.tensor_tensor(x1[:, :, :], x_sb[:, :, :],
                                   w["b_out"][:, :].unsqueeze(1).to_broadcast([P, T, D]), ALU.add)\
                    .then_inc(base_done[0], 1)
                for u in range(UNITS):
                    pool.wait_ge(*nth(hmax_done, b, u + 1))
                    pool.tensor_tensor(s32[:, u % 2, :, :], s32[:, u % 2, :, :],
                                       hmx[:, u % 2, :].unsqueeze(2).to_broadcast([P, 2 * GH, 32]),
                                       ALU.subtract).then_inc(hsub_done[0], 1)
                if after:
                    norm0(after)

            def junction(b, after):
                if not b:
                    norm0(after)
                    return
                pool.wait_ge(*nth(ss_done, b, 2 * T))
                inverse_root(b, 1, rstd_done, 2, rms[:, :], 1)
                pool.wait_ge(*drain(b, "up1"))
                pool.wait_ge(*drain(b, "hout"))
                pool.tensor_tensor(x1[:, :, :], x1[:, :, :], x2[:, :, :], ALU.add).then_inc(acc_done[0], 1)

            batches(pool, rest, junction, head, lambda b: None)

        def take_y(act, b, g):
            act.wait_ge(*nth(hpv_done, b, 3 * (g + 1)))
            for cc in range(2):
                ins = act.activation(wide[:, 2 * g + cc, :], psum[:, bank(b, "hy", g) + cc, :], ACT.Copy)
            ins.then_inc(*frees(b, "hy", g))

        @block.scalar
        def _(act):
            for name in FIRST:
                target = w_int[name] if name in w_int else w[name][:]
                act.dma_start(target, dram[name]).then_inc(in_first[0], 16)
            act.wait_ge(in_first[0], 16 * len(FIRST))
            act.wait_ge(setup_pool[0], SETUP_POOL)

            def split(b, k, src, side):
                act.wait_ge(*nth(rot_done, b, k + 1))
                if k < 2:
                    act.wait_ge(*nth(stack_in[1], b, 0))
                else:
                    act.wait_ge(*nth(stack_in[0], b, 16 * STACK_DMAS[0]))
                act.activation(parts[:, side, 0, :], src, ACT.Copy).then_inc(hi_done[0], 1)

            def split_rest(b, k, src, side):
                act.wait_ge(*nth(rem_done, b, k + 1))
                act.activation(parts[:, side, 1, :], src, ACT.Copy).then_inc(mid_done[0], 1)

            def attention(b, a):
                for g in range(G):
                    for i in range(SOFT):
                        n = (a * G + g) * SOFT + i
                        width = N - (i % T) * P
                        act.wait_ge(*fill(b, "st", a, g, i))
                        act.wait_ge(*nth(pv_done, b, max(n - P_RING + 1, 0)))
                        act.activation(probs[:, n % P_RING, 0:width], psum[:, bank(b, "st", a, g, i), 0:width],
                                       ACT.Exp, scale=(1.0 / HD0, 1.0 / HD1 ** 0.5)[a])\
                            .then_inc(*frees(b, "st", a, g, i))
                        if i == LAG and g:
                            output(b, a, g - 1)
                output(b, a, G - 1)

            def take_ao(b, a):
                act.wait_ge(*fill(b, "aoT", a))
                act.activation(aoT[:, :], psum[:, bank(b, "aoT", a), :], ACT.Copy).then_inc(*frees(b, "aoT", a))

            def output(b, a, g):
                act.wait_ge(*nth(pv_done, b, (a * G + g + 1) * SOFT))
                if g:
                    act.wait_ge(*fill(b, "o", a, g - 1))
                act.activation(o_sb[:, :], psum[:, bank(b, "oT", a, g), :], ACT.Copy).then_inc(*frees(b, "oT", a, g))

            def expert(b, kind, e, *piece):
                if kind == "output" or piece[1] == 0:
                    return
                fc = piece[0]
                act.wait_ge(*fill(b, "ehid", e, fc))
                if e:
                    act.wait_ge(*drain(b, "ehid", e - 1, fc))
                elif fc:
                    act.wait_ge(*nth(acc_done, b, 1))
                act.activation(esilu[fc], psum[:, bank(b, "ehid", e, fc), :], ACT.Silu)\
                    .then_inc(esilu_done[0], 1)

            def junction(b, after):
                if after:
                    act.wait_ge(*fill(after, "xnT"))
                    act.activation(xnT[:, :], psum[:, bank(after, "xnT"), :], ACT.Copy)\
                        .then_inc(*frees(after, "xnT"))
                if b:
                    take_ao(b, 1)
                if after:
                    act.wait_ge(*fill(after, "v0"))
                    act.activation(v_aug[:, :, :, 0:HD0],
                                   psum[:, bank(after, "v0"), :].rearrange("p (t h d) -> p t h d", t=T, h=H),
                                   ACT.Copy).then_inc(*frees(after, "v0"))
                    split(after, 0, rot[:, 0, :], 0)
                if b:
                    act.wait_ge(*fill(b, "tT"))
                    act.activation(hT[:, :], psum[:, bank(b, "tT"), :], ACT.Copy, scale=w["g2"][:, 0:1])\
                        .then_inc(*frees(b, "tT"))
                if after:
                    split_rest(after, 0, rot[:, 0, :], 0)
                beside(b, "start0", expert)
                if after:
                    split(after, 1, rot[:, 2, :], 1)
                    split_rest(after, 1, rot[:, 2, :], 1)
                beside(b, "start1", expert)
                if b:
                    act.wait_ge(*nth(route_done, b, ROUTE_SUB))
                    act.activation(route[:, 1, :, :], route[:, 0, :, :], ACT.Exp).then_inc(route_exp[0], 1)

            def head(b, moe):
                beside(moe, "gate", expert)
                for f in range(FC0):
                    act.wait_ge(*fill(b, "ffn", f))
                    if f >= 2:
                        act.wait_ge(*drain(b, "ffn", f - 2))
                    act.activation(silu[f % 2], psum[:, bank(b, "ffn", f), :], ACT.Silu, scale=W_SCALE)\
                        .then_inc(silu_done[0], 1)
                beside(moe, "ffn", expert)
                for n in range(AHEAD[0]):
                    beside(moe, ("max", n), expert)
                attention(b, 0)
                take_ao(b, 0)
                beside(moe, "out0", expert)
                beside(moe, "norm1", expert)
                act.wait_ge(*fill(b, "xn1T"))
                act.activation(xn1T[:, :], psum[:, bank(b, "xn1T"), :], ACT.Copy).then_inc(*frees(b, "xn1T"))
                beside(moe, "xn1T", expert)
                beside(moe, "square", expert)
                act.wait_ge(in_rest[0], 16 * len(REST))
                act.wait_ge(*fill(b, "hT"))
                act.activation(h1T[:, :], psum[:, bank(b, "hT"), :], ACT.Copy, scale=w["g1"][:, 0:1])\
                    .then_inc(*frees(b, "hT"))
                beside(moe, "hT", expert)
                act.wait_ge(*fill(b, "c"))
                act.activation(cT[:, :], psum[0:64, bank(b, "c"), :], ACT.Copy).then_inc(*frees(b, "c"))
                act.wait_ge(*fill(b, "v1"))
                act.activation(v_aug[:, :, :, 0:HD1],
                               psum[:, bank(b, "v1"), 0:T * 64].rearrange("p (t h d) -> p t h d", t=T, h=H),
                               ACT.Copy).then_inc(*frees(b, "v1"))

            def rest(b, after):
                def take(key):
                    g = key[1]
                    act.wait_ge(*fill(b, *key))
                    if key == projections(g)[0] and g == 1:
                        act.wait_ge(*nth(lo_done, b, 3))
                    if key == projections(g)[0] and g >= 2:
                        act.wait_ge(*fill(b, "hs", 3 * (g - 1) - 1))
                    if key[0] == "hqk":
                        _, _, cc, side, ext = key
                        n0, n = (0, N) if ext == 0 else (N, 2 * P)
                        act.activation((qT, kT)[side][g % 2][:, cc, n0:n0 + n], psum[:, bank(b, *key), 0:n],
                                       ACT.Copy).then_inc(*frees(b, *key))
                        return
                    tp = key[2]
                    if tp == 0 and g >= 2:
                        act.wait_ge(*nth(hpv_done, b, 3 * (g - 1)))
                    act.activation(v_h[:, g % 2, 2 * tp:2 * tp + 2, :],
                                   psum[:, bank(b, *key), :].rearrange("p (t n) -> p t n", t=2),
                                   ACT.Copy).then_inc(*frees(b, *key))

                for k, key in enumerate(projections(0)):
                    take(key)
                    if k == 0:
                        split(b, 2, rot[:, 0, :], 0)
                    if k == 2:
                        split_rest(b, 2, rot[:, 0, :], 0)
                for u in range(UNITS + 2):
                    if u < UNITS:
                        for key in pieces_at(u):
                            take(key)
                        act.wait_ge(*nth(hsub_done, b, u + 1))
                        if u >= 2:
                            act.wait_ge(*nth(habd_done, b, u - 1))
                        act.activation(a32[:, u % 2, :, :], s32[:, u % 2, :, :], ACT.Exp, scale=HDH ** -0.5)\
                            .then_inc(hexp_done[0], 1)
                    if u >= 4 and (u - 4) % 3 == 0:
                        take_y(act, b, (u - 4) // 3)
                attention(b, 1)

            def last(b):
                for item in EXPERT_ORDER:
                    expert(b, *item)

            batches(act, rest, junction, head, last)

        def wide_of(s):
            return s.unsqueeze(2).to_broadcast([P, T, EXPERTS])

        def chain(dve, b, done):
            steps = [done]

            def link(ins, wait=True):
                steps[0] += 1
                ins.then_inc(route_done[0], 1)
                if wait:
                    dve.wait_ge(*nth(route_done, b, steps[0]))
            return link, steps

        def router_start(dve, b):
            link, steps = chain(dve, b, 0)
            dve.wait_ge(*fill(b, "logit"))
            dve.tensor_copy(logit[:, :, :], psum[:, bank(b, "logit"), 0:T * EXPERTS].rearrange(
                "p (t e) -> p t e", t=T)).then_inc(*frees(b, "logit"))
            dve.wait_ge(*drain(b, "logit"))
            apart(dve, 4)
            for t in range(T):
                link(dve.max(top[:, t, :], logit[:, t, :]), wait=t == T - 1)
            link(dve.tensor_tensor(route[:, 0, :, :], logit[:, :, :], wide_of(top[:, :, 0]), ALU.subtract))
            assert steps[0] == ROUTE_SUB

        def router_end(dve, b):
            link, steps = chain(dve, b, ROUTE_SUB)
            apart(dve, 5)
            for t in range(T):
                link(dve.max_index(top_at[:, t, :], top[:, t, :], logit[:, t, :]), wait=t == T - 1)
            link(dve.tensor_copy(top_f[:, :, :], top_at[:, :, 0:2]))
            numbers = w["numbers"][:, :].unsqueeze(1).to_broadcast([P, T, EXPERTS])
            for k in range(2):
                link(dve.tensor_tensor(route[:, 2 + k, :, :], numbers, wide_of(top_f[:, :, k]), ALU.is_equal))
            link(dve.tensor_tensor(route[:, 2, :, :], route[:, 2, :, :], route[:, 3, :, :], ALU.add))
            dve.wait_ge(*nth(route_exp, b, 1))
            link(dve.tensor_reduce(route_s[:, 0, :], route[:, 1, :, :], AX.X, ALU.add))
            link(dve.reciprocal(route_s[:, 1, :], route_s[:, 0, :]))
            link(dve.tensor_tensor(route[:, 4, :, :], route[:, 1, :, :], wide_of(route_s[:, 1, :]), ALU.mult))
            link(dve.tensor_tensor(route[:, 4, :, :], route[:, 4, :, :], route[:, 2, :, :], ALU.mult))
            link(dve.tensor_reduce(route_s[:, 2, :], route[:, 4, :, :], AX.X, ALU.add))
            link(dve.reciprocal(route_s[:, 3, :], route_s[:, 2, :]))
            link(dve.tensor_tensor(route[:, 5, :, :], route[:, 4, :, :], wide_of(route_s[:, 3, :]), ALU.mult))
            assert steps[0] == ROUTE_STEPS, steps[0]

        def add_expert(dve, b, e):
            dve.wait_ge(*fill(b, "ey", e))
            if e == 0:
                dve.wait_ge(*nth(acc_done, b, 1))
            else:
                dve.wait_ge(*drain(b, "ey", e - 1))
            for t in range(T):
                ins = dve.scalar_tensor_tensor(out=x1[:, t, :], in0=psum[:, bank(b, "ey", e), t * P:(t + 1) * P],
                                               scalar=route[:, 5, t, e:e + 1], in1=x1[:, t, :],
                                               op0=ALU.mult, op1=ALU.add)
            ins.then_inc(*frees(b, "ey", e))

        @block.vector
        def _(dve):
            dve.memset(zeros[:, :], 0.0).then_inc(setup_dve[0], 1)
            dve.memset(ks[:, :, :], 1.0).then_inc(setup_dve[0], 1)
            for k, s in enumerate(primed):
                dve.memset(scratch[:, 8 + k:9 + k], 0.0).then_inc(s, 1)
            dve.wait_ge(in_first[0], 16 * len(FIRST))
            dve.tensor_copy(ident_b[:, :], w["ident"][:, :]).then_inc(setup_dve[0], 1)
            for name in ("gate", "up", "down"):
                dve.tensor_copy(w_f[name][:, :], w_int[name]).then_inc(setup_dve[0], 1)
            dve.wait_ge(setup_pool[0], SETUP_POOL)

            def norm_stats(b, k, src):
                done = (stats0_done, stats1_done)[k]
                for t in range(T):
                    dve.bn_stats(stats[k][:, t, :], src[:, t, :]).then_inc(done[0], 1)
                dve.wait_ge(*nth(done, b, T))
                apart(dve, k)
                for t in range(T):
                    dve.bn_aggr(mv[k][:, t, :], stats[k][:, t, :]).then_inc(done[0], 1)

            def norm(b, k, src, dst, done):
                for t in range(T):
                    dve.tensor_scalar(dst[:, t, :], src[:, t, :], mv[k][:, t, 0:1], rstd[k][:, t:t + 1],
                                      ALU.subtract, ALU.mult).then_inc(done[0], 1)

            def norm0(b):
                dve.wait_ge(*nth(rstd0_done, b, 2))
                norm(b, 0, x_sb, xn, xn_done)

            def stats0(b):
                dve.wait_ge(*nth(x_in, b, 16))
                norm_stats(b, 0, x_sb)

            def square_sums(b, k, src):
                apart(dve, 2 + k)
                for t in range(T):
                    dve.tensor_tensor_reduce(ao[:, t, :], src[:, t, :], src[:, t, :], 1.0 / D, 0.0,
                                             ALU.mult, ALU.add, rms[:, t:t + 1]).then_inc(ss_done[0], 1)

            def rms_norm(b, k, src):
                dve.wait_ge(*nth(rstd_done, b, 2 * k))
                for t in range(T):
                    dve.tensor_scalar(ao[:, t, :], src[:, t, :], rstd[1][:, t:t + 1], None, ALU.mult)\
                        .then_inc(h_done[0], 1)

            def rotate(b, k, i, table):
                key = ("rope", k)
                dve.wait_ge(*fill(b, *key))
                dve.tensor_tensor(rot[:, i, :], psum[:, bank(b, *key), :], w[table][:, 0, :], ALU.mult)\
                    .then_inc(rot_a[0], 1)
                dve.tensor_tensor(rot[:, i + 1, :], psum[:, bank(b, *key) + 1, :], w[table][:, 1, :], ALU.mult)\
                    .then_inc(*frees(b, *key))
                dve.wait_ge(*drain(b, *key))
                dve.tensor_tensor(rot[:, i, :], rot[:, i, :], rot[:, i + 1, :], ALU.add).then_inc(rot_done[0], 1)

            def split(b, k, i, side):
                dve.wait_ge(*nth(hi_done, b, k + 1))
                dve.tensor_tensor(rot[:, i, :], rot[:, i, :], parts[:, side, 0, :], ALU.subtract)\
                    .then_inc(rem_done[0], 1)
                dve.wait_ge(*nth(mid_done, b, k + 1))
                dve.tensor_tensor(parts[:, side, 2, :], rot[:, i, :], parts[:, side, 1, :], ALU.subtract)\
                    .then_inc(lo_done[0], 1)

            def row_maxima(b, a, g, i):
                t = i % T
                width = (t + 1) * P
                s = psum[:, bank(b, "smax", a, g, i), 0:width]
                dve.wait_ge(*fill(b, "smax", a, g, i))
                dve.tensor_reduce(maxima[:, g % 2, i:i + 1], s, AX.X, ALU.max)\
                    .then_inc(*frees(b, "smax", a, g, i))

            def negate_maxima(b, a, g):
                src = psum[0:SOFT, bank(b, "mT", a, g), 0:P]
                dve.wait_ge(*fill(b, "mT", a, g))
                if g >= 2:
                    dve.wait_ge(*nth(m_in[g - 2], b, M_DMAS * 16 * (a + 1)))
                dve.tensor_scalar(m_hi[:, g % 2, :], src, -1.0, None, ALU.mult).then_inc(m_hi_done[0], 1)
                dve.wait_ge(*nth(m_hi_done, b, a * G + g + 1))
                dve.scalar_tensor_tensor(out=m_lo[:, g % 2, :], in0=src, scalar=-1.0, in1=m_hi[:, g % 2, :],
                                         op0=ALU.mult, op1=ALU.subtract).then_inc(*frees(b, "mT", a, g))

            def normalise(b, a, g):
                hd = (HD0, HD1)[a]
                o = psum[:, bank(b, "o", a, g), :].rearrange("p (t j d) -> p t j d", t=T, j=GH)
                dve.wait_ge(*fill(b, "o", a, g))
                dve.reciprocal(o_rc[:, g % 2, :, :], o[:, :, :, HD0]).then_inc(orc_done[0], 1)
                dve.wait_ge(*nth(orc_done, b, a * G + g + 1))
                dve.tensor_tensor(
                    ao[:, :, 0:H * hd].rearrange("p t (h d) -> p t h d", d=hd)[:, :, g * GH:(g + 1) * GH, :],
                    o[:, :, :, 0:hd], o_rc[:, g % 2, :, :].unsqueeze(3).to_broadcast([P, T, GH, hd]), ALU.mult)\
                    .then_inc(*frees(b, "o", a, g))

            def maxima_step(b, a, n):
                g, i = divmod(n, SOFT)
                row_maxima(b, a, g, i)
                if g and i == MT_AT:
                    negate_maxima(b, a, g - 1)

            def attention(b, a, after):
                for n in range(MAXIMA):
                    g, i = divmod(n, SOFT)
                    for k in maximum_beside(a, n):
                        maxima_step(b, a, k)
                    if n == last_turn(a):
                        negate_maxima(b, a, G - 1)
                    if g and i == OT_AT:
                        normalise(b, a, g - 1)
                    if after and n == NORM0_AT:
                        stats0(after)
                    if after and n == NORM0_AT + 8:
                        norm0(after)
                    if a == 1 and n in ENDINGS:
                        ending(b, *ENDINGS[n])
                normalise(b, a, G - 1)

            def widen(b, t):
                dve.tensor_copy(rc_wide[:, t % 2, :, :],
                                a_rc[:, 1, t, :].unsqueeze(2).to_broadcast([P, H, HDH]))\
                    .then_inc(wide_rc[0], 1)

            def ending(b, kind, *piece):
                if kind == "asum":
                    dve.wait_ge(*fill(b, "asum"))
                    dve.scalar_tensor_tensor(
                        out=a_rc[:, 0, :, :], in0=psum[:, bank(b, "asum"), 0:T * H].rearrange(
                            "p (t h) -> p t h", t=T), scalar=H_EPS, in1=a_sum[:, 0:T, :],
                        op0=ALU.add, op1=ALU.add).then_inc(*frees(b, "asum"))
                    dve.wait_ge(*drain(b, "asum"))
                    dve.reciprocal(a_rc[:, 1, :, :], a_rc[:, 0, :, :]).then_inc(arc_done[0], 1)
                    dve.wait_ge(*nth(arc_done, b, 1))
                    widen(b, 0)
                    widen(b, 1)
                elif kind == "spread":
                    t, half = piece
                    y = wide[:, 4 * half:4 * half + 4, t * P:(t + 1) * P]
                    if t == 0 and half == 0:
                        dve.wait_ge(*drain(b, "hy", G - 1))
                    dve.wait_ge(*fill(b, "spread", t, half))
                    dve.tensor_tensor(y, psum[:, bank(b, "spread", t, half), :].rearrange("p (c n) -> p c n", c=4),
                                      y, ALU.mult).then_inc(*frees(b, "spread", t, half))
                    if half == 1 and t + 2 < T:
                        widen(b, t + 2)
                elif piece[0] == T - 1:
                    dve.wait_ge(*nth(base_done, b, 1))
                    dve.wait_ge(*fill(b, "hout"))
                    dve.tensor_tensor(x1[:, :, :], psum[:, bank(b, "hout"), :].rearrange("p (t d) -> p t d", t=T),
                                      x1[:, :, :], ALU.add).then_inc(*frees(b, "hout"))

            def expert(b, kind, e, *piece):
                if kind == "output":
                    if piece[0] == T - 1:
                        add_expert(dve, b, e)
                    return
                fc, k = piece
                if k == 0:
                    return
                dve.wait_ge(*nth(esilu_done, b, e * FC1 + fc + 1))
                dve.tensor_tensor(wide[:, 2 * (e % 2) + fc, :], psum[:, bank(b, "ehid", e, fc) + 1, :],
                                  esilu[fc], ALU.mult).then_inc(*frees(b, "ehid", e, fc))

            def junction(b, after):
                if not b:
                    stats0(after)
                    norm0(after)
                if b:
                    dve.wait_ge(*fill(b, "up1"))
                    dve.tensor_tensor(x2[:, :, :], psum[:, bank(b, "up1"), :].rearrange("p (t d) -> p t d", t=T),
                                      xn1[:, :, :], ALU.add).then_inc(*frees(b, "up1"))
                    dve.wait_ge(*drain(b, "up1"))
                    square_sums(b, 1, x2)
                if after:
                    rotate(after, 0, 0, "rope0")
                if b:
                    rms_norm(b, 3, x2)
                if after:
                    rotate(after, 1, 2, "rope0")
                    split(after, 0, 0, 0)
                beside(b, "start0", expert)
                if after:
                    split(after, 1, 2, 1)
                if b:
                    router_start(dve, b)
                beside(b, "start1", expert)
                if b:
                    router_end(dve, b)

            def head(b, moe):
                beside(moe, "gate", expert)
                for f in range(FC0):
                    dve.wait_ge(*nth(silu_done, b, f + 1))
                    dve.scalar_tensor_tensor(out=wide[:, L0_AT + f, :], in0=psum[:, bank(b, "ffn", f) + 1, :],
                                             scalar=W_SCALE * W_SCALE, in1=silu[f % 2],
                                             op0=ALU.mult, op1=ALU.mult).then_inc(*frees(b, "ffn", f))
                beside(moe, "ffn", expert)
                for n in range(AHEAD[0]):
                    maxima_step(b, 0, n)
                    beside(moe, ("max", n), expert)
                attention(b, 0, None)
                dve.wait_ge(*nth(xb_done, b, 1))
                dve.wait_ge(*fill(b, "out0"))
                dve.tensor_tensor(x_sb[:, :, :], psum[:, bank(b, "out0"), :].rearrange("p (t d) -> p t d", t=T),
                                  x_sb[:, :, :], ALU.add).then_inc(*frees(b, "out0"))
                dve.wait_ge(*drain(b, "out0"))
                norm_stats(b, 1, x_sb)
                beside(moe, "out0", expert)
                dve.wait_ge(*nth(rstd_done, b, 2))
                norm(b, 1, x_sb, xn1, xn1_done)
                beside(moe, "norm1", expert)
                dve.wait_ge(*nth(xn1_done, b, T))
                square_sums(b, 0, xn1)
                beside(moe, "xn1T", expert)
                rms_norm(b, 2, xn1)
                beside(moe, "square", expert)
                beside(moe, "hT", expert)
                rotate(b, 2, 0, "rope1")
                split(b, 2, 0, 0)

            def rest(b, after):
                def extract(u):
                    kind = 0 if u % 3 < 2 else 1
                    pair = psum[:, bank(b, "hs", u):bank(b, "hs", u) + 2, :].rearrange("p k (h n) -> p (k h) n", n=P)
                    dve.wait_ge(*fill(b, "hs", u))
                    if u >= 2:
                        dve.wait_ge(*nth(hexp_done, b, u - 1))
                    for q in range(4):
                        rows = slice(32 * q, 32 * q + 32)
                        ins = dve.tensor_tensor(
                            s32[rows, u % 2, :, :], pair[rows, :, rows],
                            w["band"][rows, kind, :].unsqueeze(1).to_broadcast([32, 2 * GH, 32]), ALU.add)
                    ins.then_inc(*frees(b, "hs", u))
                    dve.wait_ge(*drain(b, "hs", u))
                    dve.tensor_reduce(hmx[:, u % 2, :], s32[:, u % 2, :, :], AX.X, ALU.max)\
                        .then_inc(hmax_done[0], 1)

                def turn(u):
                    g, tp = u // 3, u % 3
                    dve.wait_ge(*nth(hexp_done, b, u + 1))
                    dve.tensor_reduce(
                        a_sum[:, 2 * tp:2 * tp + 2, GH * g:GH * (g + 1)].rearrange("p t (c r) -> p r t c", r=R),
                        a32[:, u % 2, :, :].rearrange("p (r t c) n -> p r t c n", r=R, t=2), AX.X, ALU.add)\
                        .then_inc(hsum_done[0], 1)
                    if u >= 2:
                        dve.wait_ge(*nth(hpv_done, b, u - 1))
                    for q in range(4):
                        rows = slice(32 * q, 32 * q + 32)
                        ins = dve.transpose(a_bd[rows, u % 2, :, rows], a32[rows, u % 2, :, :])
                    ins.then_inc(habd_done[0], 1)

                for u in range(UNITS + 1):
                    early, late = maxima_at(u) if u < UNITS else ([], [])
                    for n in early:
                        maxima_step(b, 1, n)
                    if u < UNITS:
                        extract(u)
                    if u:
                        turn(u - 1)
                    for n in late:
                        maxima_step(b, 1, n)
                attention(b, 1, after)

            def last(b):
                for item in EXPERT_ORDER:
                    expert(b, *item)

            batches(dve, rest, junction, head, last)

        @block.tensor
        def _(pe):
            ident = w["ident"][:, :]
            used = {"first": [], "body": [], "last": []}
            seen = {}

            def product(b, *key):
                used[b.section].append(key)
                for place, n in room(b, *key):
                    if n > seen.get((b.section, place), -1):
                        pe.wait_ge(drained[place][0], b.plan_count(1, place, n + 1))
                        seen[b.section, place] = n
                return bank(b, *key)

            def turn4(b, name, src, ready, n0):
                k = product(b, name)
                for t in range(T):
                    pe.wait_ge(*nth(ready, b, n0 + t + 1))
                    ins = pe.transpose(psum[:, k, t * P:(t + 1) * P], src[:, t, :], ident)
                ins.then_inc(*ends(b, name))

            def scores_q(b, a, g, i):
                r, cc, t = i // (SOFT // R), i // T % (GH // R), i % T
                c = g * GH // R + cc
                k = product(b, "smax", a, g, i)
                pe.matmul(psum[:, k, 0:(t + 1) * P], qs[:, C * r + c, t * P:(t + 1) * P],
                          ks[:, c, 0:(t + 1) * P], start=True, stop=True)
                pe.matmul(psum[:, k, t * P:(t + 1) * P], ident_b[:, :], hidden[:, 0, :], start=False, stop=True,
                          skip_group_check=True).then_inc(*ends(b, "smax", a, g, i))

            def turn_maxima(b, a, g):
                k = product(b, "mT", a, g)
                pe.wait_ge(*drain(b, "smax", a, g, SOFT - 1))
                pe.transpose(psum[0:SOFT, k, 0:P], maxima[:, g % 2, :], ident).then_inc(*ends(b, "mT", a, g))

            def scores_k(b, a, g, i):
                j, kb = i // T, i % T
                h = g * GH + j
                k = product(b, "st", a, g, i)
                if i == 0:
                    pe.wait_ge(*nth(m_in[g], b, 16 * M_DMAS * (a + 1)))
                pe.matmul(psum[:, k, 0:N - kb * P], ks[:, h // R, kb * P:(kb + 1) * P],
                          qs[:, C * (h % R) + h // R, kb * P:N], start=True, stop=True)
                pe.matmul(psum[:, k, 0:P], ident_b[:, :], hidden[:, 1, :], start=False, stop=True,
                          skip_group_check=True).then_inc(*ends(b, "st", a, g, i))

            def weigh(b, a, g, i):
                j, kb = i // T, i % T
                n = (a * G + g) * SOFT + i
                k = bank(b, "oT", a, g)
                pe.wait_ge(*drain(b, "st", a, g, i))
                pe.matmul(psum[32 * j:32 * j + 32, k, kb * P:N], v_aug[:, kb, g * GH + j, :],
                          probs[:, n % P_RING, 0:N - kb * P], start=(kb == 0), stop=(kb == T - 1),
                          skip_group_check=True).then_inc(pv_done[0], 1)

            def turn_output(b, a, g):
                k = product(b, "o", a, g)
                pe.wait_ge(*drain(b, "oT", a, g))
                for t in range(T):
                    ins = pe.transpose(psum[:, k, t * P:(t + 1) * P], o_sb[:, t * P:(t + 1) * P], ident)
                ins.then_inc(*ends(b, "o", a, g))

            def ending(b, kind, *piece):
                if kind == "asum":
                    k = product(b, "asum")
                    pe.wait_ge(*nth(hsum_done, b, UNITS))
                    for t in range(T):
                        to = psum[:, k, t * H:(t + 1) * H]
                        for i in range(2):
                            ins = pe.matmul(to, w["scatter"][:, i, t * P:(t + 1) * P], a_sum[:, T + i, :],
                                            start=(t == 0 and i == 0), stop=(i == 1), skip_group_check=True)
                    ins.then_inc(*ends(b, "asum"))
                elif kind == "spread":
                    t, half = piece
                    k = product(b, "spread", t, half)
                    pe.wait_ge(*nth(wide_rc, b, t + 1))
                    for c in range(4):
                        h = 2 * (4 * half + c)
                        ins = pe.transpose(psum[:, k, c * P:(c + 1) * P],
                                           rc_wide[:, t % 2, h:h + 2, :].rearrange("p h d -> p (h d)"), ident)
                    ins.then_inc(*ends(b, "spread", t, half))
                else:
                    t = piece[0]
                    k = product(b, "hout") if t == 0 else bank(b, "hout")
                    pe.wait_ge(*drain(b, "spread", t, 1))
                    for c in range(8):
                        ins = pe.matmul(psum[:, k, t * P:(t + 1) * P], wide[:, c, t * P:(t + 1) * P],
                                        w["out"][:, c, :], start=(t == 0 and c == 0), stop=(c == 7),
                                        skip_group_check=True)
                    if t == T - 1:
                        ins.then_inc(*ends(b, "hout"))

            def maxima_step(b, a, n):
                g, i = divmod(n, SOFT)
                if n == 0:
                    pe.wait_ge(*nth(stack_in[a], b, 16 * STACK_DMAS[a]))
                scores_q(b, a, g, i)
                if g and i == MT_AT:
                    turn_maxima(b, a, g - 1)

            def attention(b, a):
                for n in range(MAXIMA + LAG):
                    g, i = divmod(n, SOFT)
                    if g < G:
                        scores_k(b, a, g, i)
                    if i == LAG and g < G:
                        product(b, "oT", a, g)
                    if n >= LAG:
                        weigh(b, a, *divmod(n - LAG, SOFT))
                    for k in maximum_beside(a, n):
                        maxima_step(b, a, k)
                    if n == last_turn(a):
                        turn_maxima(b, a, G - 1)
                    if g and i == OT_AT:
                        turn_output(b, a, g - 1)
                    if a == 1 and n in ENDINGS:
                        ending(b, *ENDINGS[n])
                turn_output(b, a, G - 1)

            def turn_ao(b, a):
                k = product(b, "aoT", a)
                pe.wait_ge(*drain(b, "o", a, G - 1))
                for t in range(T):
                    ins = pe.transpose(psum[:, k, t * P:(t + 1) * P], ao[:, t, :], ident)
                ins.then_inc(*ends(b, "aoT", a))

            def expert(b, kind, e, *piece):
                if kind == "hidden":
                    fc, i = piece
                    k = product(b, "ehid", e, fc) if i == 0 else bank(b, "ehid", e, fc)
                    ins = pe.matmul(psum[:, k + i, :], w[("w1", "w3")[i]][:, e, fc * P:(fc + 1) * P], hT[:, :],
                                    start=True, stop=True)
                    if i == 1:
                        ins.then_inc(*ends(b, "ehid", e, fc))
                    return
                t = piece[0]
                k = bank(b, "ey", e)
                if t == 0:
                    product(b, "ey", e)
                    for fc in range(FC1 if two_pairs(e) else 1):
                        pe.wait_ge(*drain(b, "ehid", e, FC1 - 1 - fc))
                for fc in range(FC1):
                    ins = pe.matmul(psum[:, k, t * P:(t + 1) * P],
                                    wide[:, 2 * (e % 2) + fc, t * P:(t + 1) * P],
                                    w["w2"][:, e * FC1 + fc, :], start=(t == 0 and fc == 0),
                                    stop=(fc == FC1 - 1), skip_group_check=True)
                if t == T - 1:
                    ins.then_inc(*ends(b, "ey", e))

            pe.wait_ge(in_first[0], 16 * len(FIRST))
            pe.wait_ge(setup_pool[0], SETUP_POOL)
            pe.wait_ge(setup_dve[0], SETUP_DVE)

            def rope(b, k):
                bk = product(b, "rope", k)
                for swap in range(2):
                    ins = pe.matmul(psum[:, bk + swap, :], w["qk0"][:, 2 * k + swap, :], xnT[:, :],
                                    start=True, stop=True)
                ins.then_inc(*ends(b, "rope", k))

            def feed(b, f):
                bk = product(b, "ffn", f)
                for k, name in enumerate(("gate", "up")):
                    ins = pe.matmul(psum[:, bk + k, :], w_f[name][:, f * P:(f + 1) * P], xnT[:, :],
                                    start=True, stop=True)
                ins.then_inc(*ends(b, "ffn", f))

            def junction(b, after):
                if after:
                    turn4(after, "xnT", xn, xn_done, 0)
                if b:
                    turn_ao(b, 1)
                if after:
                    pe.wait_ge(*drain(after, "xnT"))
                    rope(after, 0)
                if b:
                    k = product(b, "up1")
                    pe.wait_ge(*drain(b, "aoT", 1))
                    for t in range(T):
                        ins = pe.matmul(psum[:, k, t * P:(t + 1) * P], aoT[0:64, t * P:(t + 1) * P],
                                        w["up1"][:, :], start=True, stop=True)
                    ins.then_inc(*ends(b, "up1"))
                if after:
                    k = product(after, "v0")
                    for t in range(T):
                        ins = pe.matmul(psum[:, k, t * P:(t + 1) * P], xnT[:, t * P:(t + 1) * P], w["v0"][:, :],
                                        start=True, stop=True)
                    ins.then_inc(*ends(after, "v0"))
                    rope(after, 1)
                    feed(after, 0)
                if b:
                    turn4(b, "tT", ao, h_done, T)
                    k = product(b, "logit")
                    pe.wait_ge(*drain(b, "tT"))
                    for t in range(T):
                        ins = pe.matmul(psum[:, k, t * EXPERTS:(t + 1) * EXPERTS], hT[:, t * P:(t + 1) * P],
                                        w["router"][:, :], start=True, stop=True)
                    ins.then_inc(*ends(b, "logit"))
                    beside(b, "start0", expert)
                    beside(b, "start1", expert)

            def head(b, moe):
                beside(moe, "gate", expert)
                for f in range(1, FC0):
                    feed(b, f)
                beside(moe, "ffn", expert)
                for n in range(AHEAD[0]):
                    maxima_step(b, 0, n)
                    beside(moe, ("max", n), expert)
                attention(b, 0)
                bk = product(b, "out0")
                pe.wait_ge(*drain(b, "ffn", FC0 - 1))
                for t in range(T):
                    for f in range(FC0):
                        pe.matmul(psum[:, bk, t * P:(t + 1) * P], wide[:, L0_AT + f, t * P:(t + 1) * P],
                                  w_f["down"][:, f * P:(f + 1) * P], start=(t == 0 and f == 0), stop=False,
                                  skip_group_check=True)
                turn_ao(b, 0)
                pe.wait_ge(*drain(b, "aoT", 0))
                for t in range(T):
                    ins = pe.matmul(psum[:, bk, t * P:(t + 1) * P], aoT[:, t * P:(t + 1) * P], w["o0"][:, :],
                                    start=False, stop=True, skip_group_check=True)
                ins.then_inc(*ends(b, "out0"))
                beside(moe, "out0", expert)
                beside(moe, "norm1", expert)
                pe.wait_ge(in_rest[0], 16 * len(REST))
                turn4(b, "xn1T", xn1, xn1_done, 0)
                beside(moe, "xn1T", expert)
                beside(moe, "square", expert)
                turn4(b, "hT", ao, h_done, 0)
                beside(moe, "hT", expert)
                bk = product(b, "c")
                pe.wait_ge(*drain(b, "hT"))
                pe.matmul(psum[0:64, bk, :], w["down1"][:, :], h1T[:, :], start=True, stop=True)\
                    .then_inc(*ends(b, "c"))
                bk = product(b, "rope", 2)
                pe.wait_ge(*drain(b, "c"))
                for swap in range(2):
                    ins = pe.matmul(psum[:, bk + swap, :], w["qk1"][:, swap, :], cT[:, :], start=True, stop=True)
                ins.then_inc(*ends(b, "rope", 2))
                bk = product(b, "v1")
                for t in range(T):
                    ins = pe.matmul(psum[:, bk, t * 64:(t + 1) * 64], cT[:, t * P:(t + 1) * P], w["v1"][:, :],
                                    start=True, stop=True)
                ins.then_inc(*ends(b, "v1"))

            def rest(b, after):
                def project(key):
                    k = product(b, *key)
                    g = key[1]
                    if key[0] == "hqk":
                        _, _, cc, side, ext = key
                        lhs = w["qkv"][:, side * H * HDH + (2 * g + cc) * P:][:, 0:P]
                        if g == 0 and ext == 1:
                            pe.wait_ge(*nth(coarse_done, b, COARSE_STEPS))
                        rhs, n = (xn1T[:, :], N) if ext == 0 else (coarse[:, side, :], 2 * P)
                        pe.matmul(psum[:, k, 0:n], lhs, rhs, start=True, stop=True).then_inc(*ends(b, *key))
                        return
                    for i in range(2):
                        t = 2 * key[2] + i
                        lhs = xn1T[:, t * P:(t + 1) * P] if t < T else \
                            coarse[:, 2, (t - T) * P:(t - T + 1) * P]
                        ins = pe.matmul(psum[:, k, i * GH * HDH:(i + 1) * GH * HDH], lhs,
                                        w["qkv"][:, 2 * H * HDH + g * GH * HDH:][:, 0:GH * HDH],
                                        start=True, stop=True)
                    ins.then_inc(*ends(b, *key))

                def hscores(u, steps):
                    g, tp = u // 3, u % 3
                    k = product(b, "hs", u)
                    if tp == 0:
                        pe.wait_ge(*drain(b, "hqk", g, 1, 1, 1))
                    for i in range(2):
                        t = 2 * tp + i
                        for j in range(GH):
                            rows = slice(64 * (j % 2), 64 * (j % 2) + 64)
                            m = 2 * i + j // 2
                            for n in steps[:1] if GH * i + j else []:
                                maxima_step(b, 1, n)
                            del steps[:1 if GH * i + j else 0]
                            ins = pe.matmul(psum[:, k + j % 2, m * P:(m + 1) * P],
                                            qT[g % 2][rows, j // 2, t * P:(t + 1) * P],
                                            kT[g % 2][rows, j // 2, t * P:(t + 1) * P], start=True, stop=True)
                    ins.then_inc(*ends(b, "hs", u))
                    assert not steps

                def hweigh(u):
                    g, tp = u // 3, u % 3
                    k = bank(b, "hy", g)
                    if tp == 0:
                        product(b, "hy", g)
                        pe.wait_ge(*drain(b, "hv", g, XT // 2 - 1))
                    pe.wait_ge(*nth(habd_done, b, u + 1))
                    for i in range(2):
                        t = 2 * tp + i
                        for j in range(GH):
                            rows = slice(64 * (j % 2), 64 * (j % 2) + 64)
                            y = psum[rows, k + j // 2, :]
                            v = v_h[:, g % 2, t, j * HDH:(j + 1) * HDH]
                            at = 0
                            for level in (range(0, 1) if t < T else range(1, 2) if t == T
                                          else range(2, LEVELS + 1)):
                                if level == 0:
                                    to, n = y[:, t * P:(t + 1) * P], P
                                    rhs = a_bd[:, u % 2, (j % 2) * GH + 2 * i + j // 2, :]
                                else:
                                    span = 2 * BLOCK << level
                                    n = N // span * BLOCK
                                    to = y.rearrange("p (k s) -> p k s", s=span)[
                                        :, :, span // 2 + (1 << level) - 1:span:1 << level]
                                    rhs = a_bd[:, u % 2, (j % 2) * GH + 2 * i + j // 2, at:at + n]\
                                        .rearrange("p (k i) -> p k i", i=BLOCK)
                                    at += n
                                ins = pe.matmul(to, v, rhs, start=(t == 0), stop=(level == LEVELS),
                                                skip_group_check=True)
                    ins.then_inc(hpv_done[0], 1)

                for key in projections(0):
                    project(key)
                for u in range(UNITS + 2):
                    if u < UNITS:
                        early, late = maxima_at(u)
                        hscores(u, early)
                    if u >= 2:
                        hweigh(u - 2)
                    if u < UNITS:
                        for kind, key in in_turn(pieces_at(u), late):
                            if kind == "piece":
                                project(key)
                            else:
                                maxima_step(b, 1, key)
                attention(b, 1)

            def last(b):
                for item in EXPERT_ORDER:
                    expert(b, *item)

            batches(pe, rest, junction, head, last)
            for section, keys in used.items():
                plan = list(PLANS[section][0])
                assert keys == plan, [(section, u, k) for u, k in zip(keys, plan) if u != k][:3]


M_DMAS = 2 * R
STACK_DMAS = (2 * 6 * R + R, 2 * 6 * R + R + 2 * R)
COARSE_STEPS = LEVELS * 4
ROUTE_SUB = T + 1
ROUTE_STEPS = 2 * T + 12
SETUP_DVE = 2 + 4
SETUP_POOL = 7

RESIDENT = {
    "qk0": [P, 4, P], "v0": [P, P], "o0": [P, P], "rope0": [P, 2, N], "ident": [P, P],
    "bo": [P, P], "neg_half": [P, T], "eps": [P, 2, T], "halves": [P, LEVELS + 1],
    "qkv": [P, 3 * H * HDH], "out": [P, 8, P], "b_out": [P, P], "g1": [P, 1], "g2": [P, 1],
    "down1": [P, 64], "qk1": [64, 2, P], "v1": [64, 64], "up1": [64, P], "router": [P, EXPERTS],
    "w1": [P, EXPERTS, F], "w3": [P, EXPERTS, F], "w2": [P, EXPERTS * FC1, P],
    "rope1": [P, 2, N], "band": [P, 2, 32], "scatter": [P, 2, N], "numbers": [P, EXPERTS],
}
FIRST = ["qk0", "ident", "v0", "gate", "up", "rope0", "o0", "down", "bo", "neg_half", "eps"]
REST = [k for k in RESIDENT if k not in FIRST]


def head_order(hd):
    r, d, c = np.meshgrid(np.arange(R), np.arange(hd), np.arange(C), indexing="ij")
    return ((R * c + r) * hd + d).reshape(-1)


def rope_table(hd):
    inv = (1.0 / 10000.0 ** (np.arange(0, hd, 2, dtype=np.float32) / np.float32(hd))).astype(np.float32)
    ang = (np.arange(N, dtype=np.float32)[:, None] * inv[None, :]).astype(np.float32)
    d = head_order(hd) % hd
    sign = np.where(d % 2 == 0, -1.0, 1.0)[:, None]
    return np.stack([np.cos(ang).T[d // 2], np.sin(ang).T[d // 2] * sign], 1).astype(np.float32)


def constants():
    p = np.arange(P)
    c = {"ident": np.eye(P, dtype=np.float32), "rope0": rope_table(HD0)}
    c["rope1"] = np.concatenate([rope_table(HD1)] * 2, 0)
    c["neg_half"] = np.full((P, T), -0.5, np.float32)
    c["eps"] = np.stack([np.full((P, T), e, np.float32) for e in (LN_EPS, RMS_EPS)], 1)
    c["halves"] = np.tile((0.5 ** np.arange(LEVELS + 1)).astype(np.float32), (P, 1))
    row, col = (p % 32)[:, None], np.arange(32)[None, :]
    same = row // BLOCK == col // BLOCK
    c["band"] = np.stack([np.where(same & (col <= row), 0.0, NEG), np.where(same, 0.0, NEG)], 1).astype(np.float32)
    scatter = np.zeros((P, 2, N), np.float32)
    at = [0, 0]
    for level in range(1, LEVELS + 1):
        i = 0 if level == 1 else 1
        span = 2 * BLOCK << level
        for k in range(N // span):
            for j in range(BLOCK):
                scatter[at[i], i, k * span + span // 2 + ((j + 1) << level) - 1] = 1.0
                at[i] += 1
    c["scatter"] = scatter
    c["numbers"] = np.tile(np.arange(EXPERTS, dtype=np.float32), (P, 1))
    return c


def swapped(order):
    return order ^ 1


def kernel(**inputs):
    import concourse.bacc as bacc
    from concourse.bass_utils import run_bass_kernel_spmd

    a = {k: np.asarray(v) for k, v in inputs.items()}
    o0, o1 = head_order(HD0), head_order(HD1)

    def chunks(m):
        return m.reshape(-1, P, m.shape[1]).transpose(1, 0, 2)

    arrays = {
        "x": a["L0_attn_x"],
        "qk0": np.stack([a["L0_attn_Wq"][o0].T, a["L0_attn_Wq"][swapped(o0)].T,
                         a["L0_attn_Wk"][o0].T, a["L0_attn_Wk"][swapped(o0)].T], 1),
        "v0": a["L0_attn_Wv"].T, "o0": a["L0_attn_Wo"].T,
        "bo": np.broadcast_to(a["L0_attn_bo"], (P, D)),
        "gate": a["L0_ffn_w_gate"].T, "up": a["L0_ffn_w_up"].T,
        "down": chunks(a["L0_ffn_w_down"].T).reshape(P, -1),
        "qkv": a["L1_attn_w_qkv"].T, "out": chunks(a["L1_attn_w_out"].T),
        "b_out": np.broadcast_to(a["L1_attn_b_out"], (P, D)),
        "g1": a["L1_ffn_g1"][:, None], "g2": a["L1_ffn_g2"][:, None],
        "down1": a["L1_ffn_w_down"],
        "qk1": np.stack([np.concatenate([a["L1_ffn_wq"][:, o], a["L1_ffn_wk"][:, o]], 1)
                         for o in (o1, swapped(o1))], 1),
        "v1": a["L1_ffn_wv"], "up1": a["L1_ffn_w_up"], "router": a["L1_ffn_router_w"],
        "w1": a["L1_ffn_w1"].transpose(1, 0, 2), "w3": a["L1_ffn_w3"].transpose(1, 0, 2),
        "w2": chunks(a["L1_ffn_w2"].reshape(EXPERTS * F, D)),
        **constants(),
    }
    nc = bacc.Bacc("TRN2", target_bir_lowering=False, num_devices=1)
    sent, dram = {}, {}
    for name, v in arrays.items():
        v = np.ascontiguousarray(v)
        sent[f"in_{name}"] = v
        dram[name] = nc.dram_tensor(f"in_{name}", v.shape, mybir.dt.from_np(v.dtype), kind="ExternalInput").ap()
    out = nc.dram_tensor("out", (BATCH, N, D), F32, kind="ExternalOutput").ap()
    build(nc, dram, out)
    return run_bass_kernel_spmd(nc, [sent], core_ids=[0]).results[0]["out"]
```
